# Optimizing a Trainium2 kernel written in Bass

```python
import numpy as np
import jax
import jax.numpy as jnp

def _softmax(x, axis=-1):
    return jax.nn.softmax(x, axis=axis)

def _gelu(x):
    return jax.nn.gelu(x, approximate=True)

def _silu(x):
    return jax.nn.silu(x)

def _sigmoid(x):
    return jax.nn.sigmoid(x)

def _layernorm(x, axis=-1, eps=1e-05):
    m = jnp.mean(x, axis=axis, keepdims=True)
    v = jnp.var(x, axis=axis, keepdims=True)
    return (x - m) / jnp.sqrt(v + eps)

def _scatter_add(tgt, idx, src, axis=0):
    return tgt.at[idx].add(src)

def _segment_sum(src, seg, n):
    return jax.ops.segment_sum(src, seg, n)
kernel_name = 'mk_decoder_postln_d1_seqx_r4_3601ca'

def setup_inputs(seed: int=0):
    np.random.seed(seed)
    _w = jnp.asarray

    def _rec_inputs():
        import jax
        import jax.numpy as jnp
        _rk = jax.random.key(seed)
        x = -0.0003929 + 0.9999 * jax.random.normal(jax.random.fold_in(_rk, 1), (16, 256, 256), jnp.float32)
        _lenS = 256 - jax.random.randint(jax.random.fold_in(_rk, 7), (16,), 0, max(1, 256 // 4) + 1, jnp.int32)
        _lenS2 = 120 - jax.random.randint(jax.random.fold_in(_rk, 8), (16,), 0, max(1, 120 // 4) + 1, jnp.int32)
        _ctx_768P = jax.random.normal(jax.random.fold_in(_rk, 11), (16, 16, 192), jnp.float32)
        _ctx_768c = jax.random.dirichlet(jax.random.fold_in(_rk, 511), 0.3 * jnp.ones((16,), jnp.float32), (16, 120))
        _ctx_768t = jnp.einsum('bsk,bkd->bsd', _ctx_768c, _ctx_768P)
        _ctx_768t = _ctx_768t * jax.lax.rsqrt(jnp.mean(jnp.square(_ctx_768t)) + 1e-12) * 0.953939
        ctx_768 = -0.00055796 + 0.999787 * (_ctx_768t + 0.3 * jax.random.normal(jax.random.fold_in(_rk, 611), (16, 120, 192), jnp.float32))
        return (x, ctx_768)
    x, ctx_768 = _rec_inputs()

    def _L0_attn_setup():
        import math
        import jax, jax.numpy as jnp
        import numpy as np
        L, D, H, F = (4, 256, 16, 1024)
        HD = D // H
        EPS = 1e-05

        def get_alibi_slopes(num_heads):
            closest = 2 ** math.floor(math.log2(num_heads))
            base = 2 ** (-2 ** (-(math.log2(closest) - 3)))
            slopes = base ** np.arange(1, closest + 1)
            if closest != num_heads:
                extra_base = 2 ** (-2 ** (-(math.log2(2 * closest) - 3)))
                extra = extra_base ** np.arange(1, 2 * (num_heads - closest) + 1, 2)
                slopes = np.concatenate([slopes, extra])
            return jnp.asarray(slopes, dtype=jnp.float32)

        def build_mask(num_heads, T):
            pos = jnp.arange(T)
            dist = pos[None, :] - pos[:, None]
            alibi = get_alibi_slopes(num_heads)[:, None, None] * dist[None]
            causal = jnp.where(dist > 0, -jnp.inf, 0.0).astype(jnp.float32)
            return causal[None] + alibi

        def layer_norm(x, w, b):
            mu = jnp.mean(x, axis=-1, keepdims=True)
            var = jnp.mean(jnp.square(x - mu), axis=-1, keepdims=True)
            return (x - mu) * jax.lax.rsqrt(var + EPS) * w + b

        def mha(x, mask, Wi, bi, Wo, bo):
            B, T, _ = x.shape
            qkv = x @ Wi.T + bi
            q, k, v = jnp.split(qkv, 3, axis=-1)
            q = q.reshape(B, T, H, HD).transpose(0, 2, 1, 3)
            k = k.reshape(B, T, H, HD).transpose(0, 2, 1, 3)
            v = v.reshape(B, T, H, HD).transpose(0, 2, 1, 3)
            scores = jnp.einsum('bhqd,bhkd->bhqk', q, k) / math.sqrt(HD)
            scores = scores + mask[None]
            attn = jax.nn.softmax(scores, axis=-1)
            out = jnp.einsum('bhqk,bhkd->bhqd', attn, v)
            out = out.transpose(0, 2, 1, 3).reshape(B, T, D)
            return out @ Wo.T + bo
        key = jax.random.key(seed)
        ks = jax.random.split(key, 13)
        s = 0.02
        inp = {'x': jax.random.normal(ks[0], (2, 512, D), dtype=jnp.float32), 'in_proj_w': jax.random.normal(ks[1], (L, 3 * D, D), dtype=jnp.float32) * s, 'in_proj_b': jnp.zeros((L, 3 * D), dtype=jnp.float32), 'out_proj_w': jax.random.normal(ks[2], (L, D, D), dtype=jnp.float32) * s, 'out_proj_b': jnp.zeros((L, D), dtype=jnp.float32), 'ffn1_w': jax.random.normal(ks[3], (L, F, D), dtype=jnp.float32) * s, 'ffn1_b': jnp.zeros((L, F), dtype=jnp.float32), 'ffn2_w': jax.random.normal(ks[4], (L, D, F), dtype=jnp.float32) * s, 'ffn2_b': jnp.zeros((L, D), dtype=jnp.float32), 'ln1_w': jnp.ones((L, D), dtype=jnp.float32), 'ln1_b': jnp.zeros((L, D), dtype=jnp.float32), 'ln2_w': jnp.ones((L, D), dtype=jnp.float32), 'ln2_b': jnp.zeros((L, D), dtype=jnp.float32), 'final_w': jnp.ones((D,), dtype=jnp.float32), 'final_b': jnp.zeros((D,), dtype=jnp.float32)}
        return inp
    _L0_attn_all = _L0_attn_setup()
    _L0_attn_in = {k: v for k, v in _L0_attn_all.items() if k in ('in_proj_w', 'in_proj_b', 'out_proj_w', 'out_proj_b', 'ffn1_w', 'ffn1_b', 'ffn2_w', 'ffn2_b', 'ln1_w', 'ln1_b', 'ln2_w', 'ln2_b', 'final_w', 'final_b')}
    del _L0_attn_all

    def _L0_xattn_setup():
        import jax, jax.numpy as jnp
        import numpy as np
        IMAGE_DIM = 256
        TEXT_DIM = 192
        NUM_HEADS = 16
        HEAD_DIM = IMAGE_DIM // NUM_HEADS
        key = jax.random.key(seed)
        ks = jax.random.split(key, 14)
        B, N, M = (4, 1024, 128)
        s_img = 1.0 / np.sqrt(IMAGE_DIM)
        s_txt = 1.0 / np.sqrt(TEXT_DIM)
        s_ff = 1.0 / np.sqrt(2 * IMAGE_DIM)
        return {'x': jax.random.normal(ks[0], (B, N, IMAGE_DIM), jnp.float32), 'y': jax.random.normal(ks[1], (B, M, TEXT_DIM), jnp.float32), 'Wq': jax.random.normal(ks[2], (IMAGE_DIM, IMAGE_DIM), jnp.float32) * s_img, 'bq': jax.random.normal(ks[3], (IMAGE_DIM,), jnp.float32) * s_img, 'Wk': jax.random.normal(ks[4], (TEXT_DIM, IMAGE_DIM), jnp.float32) * s_txt, 'bk': jax.random.normal(ks[5], (IMAGE_DIM,), jnp.float32) * s_txt, 'Wv': jax.random.normal(ks[6], (TEXT_DIM, IMAGE_DIM), jnp.float32) * s_txt, 'bv': jax.random.normal(ks[7], (IMAGE_DIM,), jnp.float32) * s_txt, 'W1': jax.random.normal(ks[8], (IMAGE_DIM, 2 * IMAGE_DIM), jnp.float32) * s_img, 'b1': jax.random.normal(ks[9], (2 * IMAGE_DIM,), jnp.float32) * s_img, 'W2': jax.random.normal(ks[10], (2 * IMAGE_DIM, IMAGE_DIM), jnp.float32) * s_ff, 'b2': jax.random.normal(ks[11], (IMAGE_DIM,), jnp.float32) * s_ff}
    _L0_xattn_all = _L0_xattn_setup()
    _L0_xattn_in = {k: v for k, v in _L0_xattn_all.items() if k in ('Wq', 'bq', 'Wk', 'bk', 'Wv', 'bv', 'W1', 'b1', 'W2', 'b2')}
    del _L0_xattn_all

    def _L0_ffn_setup():
        import jax, jax.numpy as jnp
        import numpy as np
        from jax import lax
        D = 256
        H = 1024
        E = 8
        TOPK = 2
        key = jax.random.key(seed)
        ks = jax.random.split(key, 7)
        s = 0.02
        return {'x': jax.random.normal(ks[0], (2, 512, D), dtype=jnp.float32), 'W1': jax.random.normal(ks[1], (E, D, H), dtype=jnp.float32) * s, 'b1': jnp.zeros((E, H), dtype=jnp.float32), 'W2': jax.random.normal(ks[2], (E, H, D), dtype=jnp.float32) * s, 'b2': jnp.zeros((E, D), dtype=jnp.float32), 'Wr': jax.random.normal(ks[3], (D, E), dtype=jnp.float32) * s, 'br': jnp.zeros((E,), dtype=jnp.float32)}
    _L0_ffn_all = _L0_ffn_setup()
    _L0_ffn_in = {k: v for k, v in _L0_ffn_all.items() if k in ('W1', 'b1', 'W2', 'b2', 'Wr', 'br')}
    del _L0_ffn_all
    return {'x': x, 'ctx_768': ctx_768, 'L0_attn_in_proj_w': _L0_attn_in['in_proj_w'], 'L0_attn_in_proj_b': _L0_attn_in['in_proj_b'], 'L0_attn_out_proj_w': _L0_attn_in['out_proj_w'], 'L0_attn_out_proj_b': _L0_attn_in['out_proj_b'], 'L0_attn_ffn1_w': _L0_attn_in['ffn1_w'], 'L0_attn_ffn1_b': _L0_attn_in['ffn1_b'], 'L0_attn_ffn2_w': _L0_attn_in['ffn2_w'], 'L0_attn_ffn2_b': _L0_attn_in['ffn2_b'], 'L0_attn_ln1_w': _L0_attn_in['ln1_w'], 'L0_attn_ln1_b': _L0_attn_in['ln1_b'], 'L0_attn_ln2_w': _L0_attn_in['ln2_w'], 'L0_attn_ln2_b': _L0_attn_in['ln2_b'], 'L0_attn_final_w': _L0_attn_in['final_w'], 'L0_attn_final_b': _L0_attn_in['final_b'], 'L0_xattn_Wq': _L0_xattn_in['Wq'], 'L0_xattn_bq': _L0_xattn_in['bq'], 'L0_xattn_Wk': _L0_xattn_in['Wk'], 'L0_xattn_bk': _L0_xattn_in['bk'], 'L0_xattn_Wv': _L0_xattn_in['Wv'], 'L0_xattn_bv': _L0_xattn_in['bv'], 'L0_xattn_W1': _L0_xattn_in['W1'], 'L0_xattn_b1': _L0_xattn_in['b1'], 'L0_xattn_W2': _L0_xattn_in['W2'], 'L0_xattn_b2': _L0_xattn_in['b2'], 'L0_ffn_W1': _L0_ffn_in['W1'], 'L0_ffn_b1': _L0_ffn_in['b1'], 'L0_ffn_W2': _L0_ffn_in['W2'], 'L0_ffn_b2': _L0_ffn_in['b2'], 'L0_ffn_Wr': _L0_ffn_in['Wr'], 'L0_ffn_br': _L0_ffn_in['br']}

def reference(x, ctx_768, L0_attn_in_proj_w, L0_attn_in_proj_b, L0_attn_out_proj_w, L0_attn_out_proj_b, L0_attn_ffn1_w, L0_attn_ffn1_b, L0_attn_ffn2_w, L0_attn_ffn2_b, L0_attn_ln1_w, L0_attn_ln1_b, L0_attn_ln2_w, L0_attn_ln2_b, L0_attn_final_w, L0_attn_final_b, L0_xattn_Wq, L0_xattn_bq, L0_xattn_Wk, L0_xattn_bk, L0_xattn_Wv, L0_xattn_bv, L0_xattn_W1, L0_xattn_b1, L0_xattn_W2, L0_xattn_b2, L0_ffn_W1, L0_ffn_b1, L0_ffn_W2, L0_ffn_b2, L0_ffn_Wr, L0_ffn_br):
    import jax
    import jax.numpy as jnp

    def _L0_attn_ref(x, in_proj_w, in_proj_b, out_proj_w, out_proj_b, ffn1_w, ffn1_b, ffn2_w, ffn2_b, ln1_w, ln1_b, ln2_w, ln2_b, final_w, final_b):
        import math
        import jax, jax.numpy as jnp
        import numpy as np
        L, D, H, F = (4, 256, 16, 1024)
        HD = D // H
        EPS = 1e-05

        def get_alibi_slopes(num_heads):
            closest = 2 ** math.floor(math.log2(num_heads))
            base = 2 ** (-2 ** (-(math.log2(closest) - 3)))
            slopes = base ** np.arange(1, closest + 1)
            if closest != num_heads:
                extra_base = 2 ** (-2 ** (-(math.log2(2 * closest) - 3)))
                extra = extra_base ** np.arange(1, 2 * (num_heads - closest) + 1, 2)
                slopes = np.concatenate([slopes, extra])
            return jnp.asarray(slopes, dtype=jnp.float32)

        def build_mask(num_heads, T):
            pos = jnp.arange(T)
            dist = pos[None, :] - pos[:, None]
            alibi = get_alibi_slopes(num_heads)[:, None, None] * dist[None]
            causal = jnp.where(dist > 0, -jnp.inf, 0.0).astype(jnp.float32)
            return causal[None] + alibi

        def layer_norm(x, w, b):
            mu = jnp.mean(x, axis=-1, keepdims=True)
            var = jnp.mean(jnp.square(x - mu), axis=-1, keepdims=True)
            return (x - mu) * jax.lax.rsqrt(var + EPS) * w + b

        def mha(x, mask, Wi, bi, Wo, bo):
            B, T, _ = x.shape
            qkv = x @ Wi.T + bi
            q, k, v = jnp.split(qkv, 3, axis=-1)
            q = q.reshape(B, T, H, HD).transpose(0, 2, 1, 3)
            k = k.reshape(B, T, H, HD).transpose(0, 2, 1, 3)
            v = v.reshape(B, T, H, HD).transpose(0, 2, 1, 3)
            scores = jnp.einsum('bhqd,bhkd->bhqk', q, k) / math.sqrt(HD)
            scores = scores + mask[None]
            attn = jax.nn.softmax(scores, axis=-1)
            out = jnp.einsum('bhqk,bhkd->bhqd', attn, v)
            out = out.transpose(0, 2, 1, 3).reshape(B, T, D)
            return out @ Wo.T + bo
        T = x.shape[1]
        mask = build_mask(H, T)
        for i in range(L):
            xn = layer_norm(x, ln1_w[i], ln1_b[i])
            x = x + mha(xn, mask, in_proj_w[i], in_proj_b[i], out_proj_w[i], out_proj_b[i])
            xn = layer_norm(x, ln2_w[i], ln2_b[i])
            h = jax.nn.gelu(xn @ ffn1_w[i].T + ffn1_b[i], approximate=False)
            x = x + (h @ ffn2_w[i].T + ffn2_b[i])
        return layer_norm(x, final_w, final_b)

    def _L0_xattn_ref(x, y, Wq, bq, Wk, bk, Wv, bv, W1, b1, W2, b2):
        import jax, jax.numpy as jnp
        import numpy as np
        IMAGE_DIM = 256
        TEXT_DIM = 192
        NUM_HEADS = 16
        HEAD_DIM = IMAGE_DIM // NUM_HEADS
        B, N, _ = x.shape
        M = y.shape[1]
        q = (x @ Wq + bq).reshape(B, N, NUM_HEADS, HEAD_DIM)
        k = (y @ Wk + bk).reshape(B, M, NUM_HEADS, HEAD_DIM)
        v = (y @ Wv + bv).reshape(B, M, NUM_HEADS, HEAD_DIM)
        scale = 1.0 / np.sqrt(HEAD_DIM)
        scores = jnp.einsum('bnhd,bmhd->bhnm', q, k) * scale
        attn = jax.nn.softmax(scores, axis=-1)
        out = jnp.einsum('bhnm,bmhd->bnhd', attn, v).reshape(B, N, IMAGE_DIM)
        h = jax.nn.relu(out @ W1 + b1)
        return h @ W2 + b2

    def _L0_ffn_ref(x, W1, b1, W2, b2, Wr, br):
        import jax, jax.numpy as jnp
        import numpy as np
        from jax import lax
        D = 256
        H = 1024
        E = 8
        TOPK = 2
        B, S, _ = x.shape
        xf = x.reshape(-1, D)
        logits = xf @ Wr + br
        topv, _ = lax.top_k(logits, TOPK)
        thresh = topv[:, TOPK - 1:TOPK]
        masked = jnp.where(logits >= thresh, logits, -jnp.inf)
        weights = jax.nn.softmax(masked, axis=-1)
        h = jax.nn.gelu(jnp.einsum('td,edh->eth', xf, W1) + b1[:, None, :], approximate=False)
        expert_out = jnp.einsum('eth,ehd->etd', h, W2) + b2[:, None, :]
        out = jnp.einsum('etd,te->td', expert_out, weights)
        return out.reshape(B, S, D)
    x = _layernorm(x + _L0_attn_ref(x, L0_attn_in_proj_w, L0_attn_in_proj_b, L0_attn_out_proj_w, L0_attn_out_proj_b, L0_attn_ffn1_w, L0_attn_ffn1_b, L0_attn_ffn2_w, L0_attn_ffn2_b, L0_attn_ln1_w, L0_attn_ln1_b, L0_attn_ln2_w, L0_attn_ln2_b, L0_attn_final_w, L0_attn_final_b), axis=-1)
    x = _layernorm(x + _L0_xattn_ref(x, ctx_768, L0_xattn_Wq, L0_xattn_bq, L0_xattn_Wk, L0_xattn_bk, L0_xattn_Wv, L0_xattn_bv, L0_xattn_W1, L0_xattn_b1, L0_xattn_W2, L0_xattn_b2), axis=-1)
    x = _layernorm(x + _L0_ffn_ref(x, L0_ffn_W1, L0_ffn_b1, L0_ffn_W2, L0_ffn_b2, L0_ffn_Wr, L0_ffn_br), axis=-1)
    return x

_drawn_inputs = setup_inputs


def setup_inputs(seed=0):
    import zlib

    import numpy as np

    out = dict(_drawn_inputs(seed))
    spreads = {'L0_attn_in_proj_b': (0.0, 0.1),
     'L0_attn_out_proj_b': (0.0, 0.1),
     'L0_attn_ffn1_b': (0.0, 0.1),
     'L0_attn_ffn2_b': (0.0, 0.1),
     'L0_attn_ln1_w': (1.0, 0.6),
     'L0_attn_ln1_b': (0.0, 0.603),
     'L0_attn_ln2_w': (1.0, 0.6),
     'L0_attn_ln2_b': (0.0, 0.519),
     'L0_attn_final_w': (1.0, 0.2),
     'L0_attn_final_b': (0.0, 0.1),
     'L0_ffn_b1': (0.0, 0.318),
     'L0_ffn_b2': (0.0, 0.1),
     'L0_ffn_br': (0.0, 0.1)}
    factors = {'L0_xattn_bq': 4.662, 'L0_xattn_bk': 8.0}
    for name, (base, spread) in spreads.items():
        noise = np.random.default_rng([zlib.crc32(name.encode()), seed]).standard_normal(out[name].shape)
        drawn = base * np.exp(spread * noise) if base else spread * noise
        out[name] = jnp.asarray(drawn.astype(out[name].dtype))
    for name, factor in factors.items():
        out[name] = (out[name] * factor).astype(out[name].dtype)
    return out
```

```python
from contextlib import ExitStack

import concourse.bass as bass
from concourse import mybir

ALU = mybir.AluOpType
ACT = mybir.ActivationFunctionType
AX = mybir.AxisListType
F32 = mybir.dt.float32
F16 = mybir.dt.float16
BF16 = mybir.dt.bfloat16

P = 128
D = 256
KD = D // P
B, T = 16, 256
N_TOK = B * T
GT = 512
NG = N_TOK // GT
TT = GT // P
GB = GT // T
L = 4
H, HD = 16, 16
F = 1024
KF = F // P
C = 4
S, E_CTX = 120, 192
F2 = 512
KF2 = F2 // P
E = 8
EPS = 1e-5
WS = 64.0

R_LO, R_HI2, R_POS, R_MAX = 16, 32, 48, 96


class Signal:

    def __init__(self, sem, per, unit=1):
        self.sem, self.per, self.unit = sem, per, unit

    def credit(self):
        return self.per * self.unit

    def after(self, n, k=None):
        k = self.per if k is None else k
        return n * (self.per * self.unit) + (self.per + k) * self.unit


def part_from_wait(engine, gate):
    engine.sem_inc(gate, 1)


def split_matmuls(pe, out, stat, mov, tiles, hold_open=False):
    last = None
    for k in range(tiles):
        for n, (a, b) in enumerate(((0, 0), (0, 1), (1, 0))):
            last = pe.matmul(out, stat(a, k), mov(b, k), start=(k == 0 and n == 0),
                             stop=(k == tiles - 1 and n == 2))
    return last


NEWTON = 3
NORM_STEPS = 2 * TT + 3 + 3 * NEWTON


class NormBuffers:

    def __init__(self, sb, name, gate):
        self.gate = gate
        self.stats = sb(f"{name}_stats", [P, TT, 6], F32)
        self.mean_var = sb(f"{name}_mean_var", [P, TT, 2], F32)
        self.var = sb(f"{name}_var", [P, TT], F32)
        self.half = sb(f"{name}_half", [P, TT], mybir.dt.int32)
        self.root = [sb(f"{name}_root{i}", [P, TT], F32) for i in range(2)]
        self.square = sb(f"{name}_square", [P, TT], F32)
        self.slope = sb(f"{name}_slope", [P, TT], F32)


def layer_norm(dve, x_tiles, z_tiles, buf, steps, value, done):
    part_from_wait(dve, buf.gate)
    for t in range(TT):
        dve.bn_stats(buf.stats[:, t, :], x_tiles(t)).then_inc(steps, 1)
    dve.wait_ge(steps, value(TT))
    part_from_wait(dve, buf.gate)
    for t in range(TT):
        dve.bn_aggr(buf.mean_var[:, t, :], buf.stats[:, t, :]).then_inc(steps, 1)
    k = 2 * TT
    dve.wait_ge(steps, value(k))
    dve.tensor_scalar(buf.var[:, :], buf.mean_var[:, :, 1], EPS, None, ALU.add).then_inc(steps, 1)
    dve.wait_ge(steps, value(k + 1))
    dve.tensor_scalar(buf.half[:, :], buf.var[:, :].bitcast(mybir.dt.int32), 1, None,
                      ALU.logical_shift_right).then_inc(steps, 1)
    dve.wait_ge(steps, value(k + 2))
    dve.tensor_scalar(buf.root[0][:, :].bitcast(mybir.dt.int32), buf.half[:, :], -1.0, float(0x5F3759DF),
                      ALU.mult, ALU.add).then_inc(steps, 1)
    k += 3
    for i in range(NEWTON):
        y, new = buf.root[i % 2], buf.root[(i + 1) % 2]
        dve.wait_ge(steps, value(k))
        dve.tensor_tensor(buf.square[:, :], y[:, :], y[:, :], ALU.mult).then_inc(steps, 1)
        dve.wait_ge(steps, value(k + 1))
        dve.scalar_tensor_tensor(buf.slope[:, :], buf.square[:, :], -0.5, buf.var[:, :], ALU.mult, ALU.mult)\
           .then_inc(steps, 1)
        dve.wait_ge(steps, value(k + 2))
        dve.scalar_tensor_tensor(new[:, :], buf.slope[:, :], 1.5, y[:, :], ALU.add, ALU.mult).then_inc(steps, 1)
        k += 3
    rstd = buf.root[NEWTON % 2]
    dve.wait_ge(steps, value(k))
    for t in range(TT):
        dve.tensor_scalar(z_tiles(t), x_tiles(t), buf.mean_var[:, t, 0:1], rstd[:, t:t + 1],
                          ALU.subtract, ALU.mult).then_inc(done, 1)


def decoder(nc, sb, sem, psum, shared, dram):
    x, ident, QS, KS, VS = shared["x"], shared["ident"], shared["QS"], shared["KS"], shared["VS"]
    W, M, SC, O = psum["W"], psum["M"], psum["S"], psum["O"]

    CH = 768
    NCH = 8
    assert KD * (3 * D + D + F) + KF * D == CH * NCH
    w_raw = [sb(f"w_raw{i}", [P, CH], F32) for i in range(2)]
    w_half = [sb(f"w_half{i}", [P, CH * NCH], F16) for i in range(2)]
    at = 0
    views = {}
    for name, k, cols in (("qkv", KD, 3 * D), ("o", KD, D), ("f1", KD, F), ("f2", KF, D)):
        views[name] = [w[:, at:at + k * cols].rearrange("p (k n) -> p k n", k=k) for w in w_half]
        at += k * cols
    rows = sb("rows", [P, 3, D], F32)
    cols = sb("cols", [P, 20], F32)
    qbias = sb("qbias", [P, 2], F32)
    COL = {"qkb": 0, "f1b": 4, "ln1w": 12, "ln1b": 14, "ln2w": 16, "ln2b": 18}

    ident_b = sb("ident_b", [P, P], BF16)
    mask_q = sb("mask_q", [P, P], BF16)
    mask_k = sb("mask_k", [P, P], BF16)

    z = [sb(f"z{i}", [P, TT, D], F32) for i in range(2)]
    xT32 = [sb(f"xT32_{i}", [P, KD, GT], F32) for i in range(2)]
    xT = [[sb(f"xT{i}_{h}", [P, KD, GT], F16) for h in range(2)] for i in range(2)]
    norm_buf = [NormBuffers(sb, f"norm{i + 1}", shared["dve_gate"]) for i in range(2)]
    QK = shared["QK"]
    qk32 = shared["qk32"]
    mx, mrow, PR, OTs, On, oT = (shared[k] for k in ("mx", "mrow", "PR", "OTs", "On", "oT"))
    rden = shared["rden"]
    h32 = sb("h32", [P, 2, GT], F32)
    hT = [sb(f"hT_{h}", [P, KF, GT], F16) for h in range(2)]

    def sig(name, per, unit=1):
        return Signal(sem("d_" + name), per, unit)

    s_const = sem("d_const")
    s_init = sem("d_init")
    raw_in, w_hi, w_lo = [sig(f"raw_in{i}", NCH // 2, 16) for i in range(2)], sig("w_hi", NCH), sig("w_lo", NCH)
    bias_in, qb_ready = sig("bias_in", 2, 16), sig("qb_ready", 1)
    ln1_steps, z1 = sig("ln1_steps", NORM_STEPS), sig("z1", TT)
    T1_ps, xh1, xf1, xl1 = sig("T1_ps", KD), sig("xh1", KD), sig("xf1", KD), sig("xl1", KD)
    V_ps, v_in = sig("V_ps", 2), sig("v_in", TT)
    QK_ps, qk_h, qk_f, qk_l = sig("QK_ps", 4), sig("qk_h", 4), sig("qk_f", 4), sig("qk_l", 4)
    heads_in = [sig(f"heads_in{m}", 6, 16) for m in range(2)]
    M_ps, mx_in = sig("M_ps", 6 * C), sig("mx_in", 6 * C)
    MT_ps, mrow_in, m_in = sig("MT_ps", C), sig("mrow_in", C), [sig(f"m_in{i}", C // 2, 16) for i in range(2)]
    S_ps, p_in, O_ps, o_in = sig("S_ps", 6 * C), sig("p_in", 6 * C), sig("O_ps", C), sig("o_in", C)
    OS_ps, rd_in, on_in = sig("OS_ps", TT), sig("rd_in", TT), sig("on_in", TT)
    OT_ps, oh, ol = sig("OT_ps", KD), sig("oh", KD), sig("ol", KD)
    OP_ps, xo = sig("OP_ps", 2), sig("xo", 2)
    xb1, xb2 = sig("xb1", 1), sig("xb2", 1)
    ln2_steps, z2 = sig("ln2_steps", NORM_STEPS), sig("z2", TT)
    T2_ps, xh2, xf2, xl2 = sig("T2_ps", KD), sig("xh2", KD), sig("xf2", KD), sig("xl2", KD)
    H_ps, h_f, h_h, h_l = sig("H_ps", KF), sig("h_f", KF), sig("h_h", KF), sig("h_l", KF)
    Y_ps, y_x = sig("Y_ps", 2), sig("y_x", 2)

    R = len(W)
    READERS = {
        "T1": [(xf1, 1)], "V": [(v_in, 2)], "QK": [(qk_f, 1)], "MT": [(mrow_in, 1)],
        "OS": [(on_in, 1)], "OT": [(oh, 1), (ol, 1)], "OP": [(xo, 1)], "T2": [(xf2, 1)],
        "H": [(h_f, 1)], "Y": [(y_x, 1)],
    }
    ROUND = {"T1": 1, "QK": 1, "V": 0, "MT": 0} | {stage: -1 for stage in ("OS", "OT", "OP", "T2", "H", "Y")}

    def tiles_of(ahead, front, back):
        a, f, b = (lambda *x: list(x) if ahead else []), (lambda *x: list(x) if front else []), \
                  (lambda *x: list(x) if back else [])
        two, four = range(2), range(4)
        out = f(*(("V", k) for k in two)) + b(*(("OS", k) for k in four)) + b(*(("OT", k) for k in two))
        out += f(("MT", 0)) + b(*(("OP", k) for k in two)) + f(("MT", 1))
        out += a(*(("T1", k) for k in two), *(("QK", k) for k in four)) + f(("MT", 2))
        out += b(*(("T2", k) for k in two)) + f(("MT", 3)) + b(*(("H", m) for m in range(KF)))
        out += b(*(("Y", k) for k in two))
        return out + [None] * (-len(out) % R)

    PRE, HEAD, STEADY = tiles_of(True, False, False), tiles_of(True, True, False), tiles_of(True, True, True)
    LAST, TAIL = tiles_of(False, True, True), tiles_of(False, False, True)
    BEFORE = {id(PRE): [(TAIL, 1)], id(HEAD): [(PRE, -1)], id(STEADY): [(HEAD, -1), (STEADY, -1)],
              id(LAST): [(STEADY, -1)], id(TAIL): [(LAST, -1)]}

    def free_tile(pe, kind, n, tile, inputs=()):
        pos = kind.index(tile)
        need = {signal: (-1, signal.per) for signal in inputs}
        for other, m in [(kind, 0)] if pos >= R else BEFORE[id(kind)]:
            q = pos - R if pos >= R else len(other) - R + pos
            while other[q] is None:
                q -= R
            stage, k = other[q]
            for signal, each in READERS[stage]:
                at = (m + ROUND[stage], (k + 1) * each)
                need[signal] = max(need.get(signal, at), at)
        for signal, (m, raises) in need.items():
            pe.wait_ge(signal.sem, signal.after(n + m, raises))
        return W[pos % R]

    block_ctx = ExitStack()
    block = block_ctx.enter_context(nc.Block())

    @block.sync
    def _(sp):
        for s in (*raw_in, bias_in, *heads_in, *m_in):
            sp.sem_inc(s.sem, s.credit())
        sp.dma_start(ident[:, :], dram["ident"]).then_inc(s_const, 16)
        sp.dma_start(z[0][:, 0, :], dram["masks"]).then_inc(s_const, 16)
        sp.dma_start(x[:, :, :], dram["x"].rearrange("(n p) d -> p n d", p=P)).then_inc(s_const, 16)
        sp.wait_ge(s_init, 3)
        sp.dma_start(QS[R_POS:R_POS + 2, :, :], dram["ones2"]).then_inc(s_const, 16)
        sp.dma_start(KS[R_POS:R_POS + 2, :, :], dram["alibi"]).then_inc(s_const, 16)
        sp.dma_start(KS[R_MAX:R_MAX + 1, :, :], dram["ones2"][0:1]).then_inc(s_const, 16)

        def heads(n, m):
            sp.wait_ge(S_ps.sem, S_ps.after(n - 1, 12 * (m + 1)))
            part_from_wait(sp, shared["sp_gate"])
            sp.wait_ge(qk_h.sem, qk_h.after(n, 2 * m + 2))
            sp.wait_ge(qk_l.sem, qk_l.after(n, 2 * m + 2))
            for tile, dst, half_rows in ((2 * m, QS, ((0, 0), (R_HI2, 0), (R_LO, 1))),
                                         (2 * m + 1, KS, ((0, 0), (R_LO, 0), (R_HI2, 1)))):
                for row, half in half_rows:
                    sp.dma_start(dst[row:row + HD, 8 * m:8 * m + 8, :], QK[half][:, tile, :])\
                      .then_inc(heads_in[m].sem, 16)

        def maximum(n, c):
            sp.wait_ge(mrow_in.sem, mrow_in.after(n, c + 1))
            sp.dma_start(QS[R_MAX:R_MAX + 1, C * c:C * c + C, :], mrow[c % 2][0:C, :])\
              .then_inc(m_in[c % 2].sem, 16)

        def body(n, ahead):
            for c in range(3):
                maximum(n, c)
            if ahead:
                heads(n + 1, 0)
            maximum(n, 3)
            if ahead:
                heads(n + 1, 1)

        with sp.Fori(0, L) as l:
            sp.wait_ge(y_x.sem, y_x.after(l * NG - 1))
            sp.wait_ge(h_f.sem, h_f.after(l * NG - 1))
            sp.dma_start(rows[:, :, :], dram["rows"][bass.ds(l, 1)].rearrange("a r d -> a (r d)")
                         .rearrange("a n -> (a n)").partition_broadcast(P).rearrange("p (r d) -> p r d", r=3))\
              .then_inc(bias_in.sem, 16)
            sp.dma_start(cols[:, :], dram["cols"][bass.ds(l, 1)].rearrange("a p c -> (a p) c")).then_inc(bias_in.sem, 16)
            for i in range(NCH):
                if i < 2:
                    sp.wait_ge(w_lo.sem, w_lo.after(l - 1, NCH - 1 + i))
                    sp.wait_ge(w_hi.sem, w_hi.after(l - 1, NCH - 1 + i))
                else:
                    sp.wait_ge(w_lo.sem, w_lo.after(l, i - 1))
                    sp.wait_ge(w_hi.sem, w_hi.after(l, i - 1))
                sp.dma_start(w_raw[i % 2][:, :], dram["weights"][bass.ds(l, 1), :, i * CH:(i + 1) * CH]
                             .rearrange("a p n -> (a p) n")).then_inc(raw_in[i % 2].sem, 16)
            heads(l * NG, 0)
            heads(l * NG, 1)
            body(l * NG, True)
            with sp.Fori(1, NG - 1) as g:
                body(l * NG + g, True)
            body(l * NG + NG - 1, False)

    @block.tensor
    def _(pe):
        for s in (T1_ps, V_ps, QK_ps, M_ps, MT_ps, S_ps, O_ps, OS_ps, OT_ps, OP_ps, T2_ps, H_ps, Y_ps):
            pe.sem_inc(s.sem, s.credit())
        pe.wait_ge(s_const, 16 * 6)
        pe.wait_ge(s_init, 4)

        def transpose_group(kind, n, name, ps, src, ready, ready_n):
            for k in range(KD):
                bank = free_tile(pe, kind, n, (name, k))
                pe.wait_ge(ready.sem, ready.after(ready_n))
                for t in range(TT):
                    last = pe.transpose(bank[:, t * P:(t + 1) * P], src[:, t, k * P:(k + 1) * P], ident[:, :])
                last.then_inc(ps.sem, 1)

        def values(kind, n):
            for k in range(2):
                bank = free_tile(pe, kind, n, ("V", k))
                for u in range(2):
                    t = 2 * k + u
                    last = split_matmuls(pe, bank[:, u * D:(u + 1) * D],
                                         lambda h, kk: xT[0][h][:, kk, t * P:(t + 1) * P],
                                         lambda h, kk: views["qkv"][h][:, kk, 2 * D:3 * D], KD)
                last.then_inc(V_ps.sem, 1)

        def queries_keys(kind, n):
            for m in range(4):
                bank = free_tile(pe, kind, n, ("QK", m))
                if m == 0:
                    pe.wait_ge(xh1.sem, xh1.after(n + 1))
                    pe.wait_ge(xl1.sem, xl1.after(n + 1))
                split_matmuls(pe, bank[:, :], lambda h, kk: views["qkv"][h][:, kk, m * P:(m + 1) * P],
                              lambda h, kk: xT[0][h][:, kk, :], KD).then_inc(QK_ps.sem, 1)

        def chunk_bank(banks, made, read, n, c, i):
            q = 6 * c + i
            if q >= 2:
                pe.wait_ge(read.sem, read.after(n, q - 1))
            else:
                pe.wait_ge(read.sem, read.after(n - 1, 6 * C - 1 + q))
            return banks[q % 2]

        def row_scores(n, c, chunks):
            if c % 2 == 0 and 0 in chunks:
                pe.wait_ge(heads_in[c // 2].sem, heads_in[c // 2].after(n))
            for q in chunks:
                b, i = divmod(q, 3)
                bank = chunk_bank(M, M_ps, mx_in, n, c, q)
                if i < 2:
                    for u in range(2):
                        h = C * c + 2 * i + u
                        pe.matmul(bank[:, u * T:(u + 1) * T], QS[0:R_MAX, h, b * T + P:(b + 1) * T],
                                  KS[0:R_MAX, h, b * T:(b + 1) * T], start=True, stop=False)
                        last = pe.matmul(bank[:, u * T + P:(u + 1) * T], ident_b[:, :], mask_q[:, :],
                                         start=False, stop=True)
                else:
                    for u in range(C):
                        h = C * c + u
                        pe.matmul(bank[:, u * P:(u + 1) * P], QS[0:R_MAX, h, b * T:b * T + P],
                                  KS[0:R_MAX, h, b * T:b * T + P], start=True, stop=False)
                        last = pe.matmul(bank[:, u * P:(u + 1) * P], ident_b[:, :], mask_q[:, :],
                                         start=False, stop=True)
                last.then_inc(M_ps.sem, 1)

        def turn_maxima(kind, n, c):
            bank = free_tile(pe, kind, n, ("MT", c))
            pe.wait_ge(mx_in.sem, mx_in.after(n, 6 * c + 6))
            for t in range(TT):
                last = pe.transpose(bank[0:C, t * P:(t + 1) * P], mx[c % 2][:, t, :], ident[:, :])
            last.then_inc(MT_ps.sem, 1)

        def key_scores(n, c, chunks):
            if 0 in chunks:
                pe.wait_ge(m_in[c % 2].sem, m_in[c % 2].after(n, c // 2 + 1))
            for q in chunks:
                b, i = divmod(q, 3)
                bank = chunk_bank(SC, S_ps, p_in, n, c, q)
                if i < 2:
                    for u in range(2):
                        h = C * c + 2 * i + u
                        pe.matmul(bank[:, u * T:(u + 1) * T], KS[:, h, b * T:b * T + P],
                                  QS[:, h, b * T:(b + 1) * T], start=True, stop=False)
                        last = pe.matmul(bank[:, u * T:u * T + P], ident_b[:, :], mask_k[:, :],
                                         start=False, stop=True)
                else:
                    for u in range(C):
                        h = C * c + u
                        pe.matmul(bank[:, u * P:(u + 1) * P], KS[:, h, b * T + P:(b + 1) * T],
                                  QS[:, h, b * T + P:(b + 1) * T], start=True, stop=False)
                        last = pe.matmul(bank[:, u * P:(u + 1) * P], ident_b[:, :], mask_k[:, :],
                                         start=False, stop=True)
                last.then_inc(S_ps.sem, 1)

        def attend(n, c):
            if c == 0:
                pe.wait_ge(v_in.sem, v_in.after(n))
            pe.wait_ge(p_in.sem, p_in.after(n, 6 * c + 6))
            if c == 0:
                pe.wait_ge(o_in.sem, o_in.after(n - 1))
            else:
                pe.wait_ge(o_in.sem, o_in.after(n, c))
            probs = PR[c % 2]
            for b in range(GB):
                for u in range(C):
                    pe.matmul(O[32 * u:32 * u + 32, b * T:(b + 1) * T], VS[:, 2 * b, C * c + u, :],
                              probs[:, 3 * b + u // 2, (u % 2) * T:(u % 2 + 1) * T], start=True, stop=False)
                for u in range(C):
                    last = pe.matmul(O[32 * u:32 * u + 32, b * T + P:(b + 1) * T],
                                     VS[:, 2 * b + 1, C * c + u, :],
                                     probs[:, 3 * b + 2, u * P:(u + 1) * P], start=False, stop=True)
            last.then_inc(O_ps.sem, 1)

        def turn_outputs(kind, n):
            for t in range(TT):
                bank = free_tile(pe, kind, n, ("OS", t))
                pe.wait_ge(o_in.sem, o_in.after(n - 1))
                for c in range(C):
                    last = pe.transpose(bank[:, c * P:(c + 1) * P], OTs[:, c, t * P:(t + 1) * P], ident[:, :])
                last.then_inc(OS_ps.sem, 1)

        def token_major(kind, n, name, ps, src, weight, tiles, ready):
            for k in range(2):
                bank = free_tile(pe, kind, n, (name, k), ready)
                for u in range(2):
                    t = 2 * k + u
                    last = split_matmuls(pe, bank[:, u * D:(u + 1) * D],
                                         lambda h, kk: src[h][:, kk, t * P:(t + 1) * P],
                                         lambda h, kk: weight[h][:, kk, :], tiles)
                last.then_inc(ps.sem, 1)

        def hidden(kind, n, m):
            bank = free_tile(pe, kind, n, ("H", m))
            if m == 0:
                pe.wait_ge(xh2.sem, xh2.after(n - 1))
                pe.wait_ge(xl2.sem, xl2.after(n - 1))
            split_matmuls(pe, bank[:, :], lambda h, kk: views["f1"][h][:, kk, m * P:(m + 1) * P],
                          lambda h, kk: xT[1][h][:, kk, :], KD).then_inc(H_ps.sem, 1)

        def body(kind, n, ahead, front, back):
            def interleaved(c):
                for q in range(6):
                    row_scores(n, c + 1, [q])
                    key_scores(n, c, [q])

            if front:
                values(kind, n)
            if back:
                turn_outputs(kind, n)
            if front:
                row_scores(n, 0, range(3))
            if back:
                transpose_group(kind, n, "OT", OT_ps, On, on_in, n - 1)
            if front:
                row_scores(n, 0, range(3, 6))
                turn_maxima(kind, n, 0)
            if back:
                token_major(kind, n, "OP", OP_ps, oT, views["o"], KD, (oh, ol))
            if front:
                interleaved(0)
                turn_maxima(kind, n, 1)
                attend(n, 0)
            if ahead:
                transpose_group(kind, n, "T1", T1_ps, z[0], z1, n + 1)
                queries_keys(kind, n)
            if front:
                interleaved(1)
                turn_maxima(kind, n, 2)
                attend(n, 1)
            if back:
                transpose_group(kind, n, "T2", T2_ps, z[1], z2, n - 1)
            if front:
                interleaved(2)
                turn_maxima(kind, n, 3)
                attend(n, 2)
            if back:
                for m in range(0, 4):
                    hidden(kind, n, m)
            if front:
                key_scores(n, 3, range(6))
            if back:
                for m in range(4, KF):
                    hidden(kind, n, m)
            if front:
                attend(n, 3)
            if back:
                token_major(kind, n, "Y", Y_ps, hT, views["f2"], KF, (h_h, h_l))

        with pe.Fori(0, L) as l:
            pe.wait_ge(w_hi.sem, w_hi.after(l))
            pe.wait_ge(w_lo.sem, w_lo.after(l))
            body(PRE, l * NG - 1, True, False, False)
            body(HEAD, l * NG, True, True, False)
            with pe.Fori(1, NG - 1) as g:
                body(STEADY, l * NG + g, True, True, True)
            body(LAST, l * NG + NG - 1, False, True, True)
            body(TAIL, l * NG + NG, False, False, True)

    @block.scalar
    def _(act):
        for s in (w_hi, xf1, qk_f, mrow_in, p_in, o_in, oh, xf2, h_f):
            act.sem_inc(s.sem, s.credit())

        def weights(l):
            act.wait_ge(Y_ps.sem, Y_ps.after(l * NG - 1))
            for i in range(NCH):
                act.wait_ge(raw_in[i % 2].sem, raw_in[i % 2].after(l, i // 2 + 1))
                act.activation(w_half[0][:, i * CH:(i + 1) * CH], w_raw[i % 2][:, :], ACT.Copy, scale=WS)\
                   .then_inc(w_hi.sem, 1)

        def project(kind, n):
            for k in range(KD):
                act.wait_ge(T1_ps.sem, T1_ps.after(n, k + 1))
                if k == 0:
                    act.wait_ge(xh1.sem, xh1.after(n - 1))
                    act.wait_ge(xl1.sem, xl1.after(n - 1))
                act.activation(xT32[0][:, k, :], W[kind.index(("T1", k)) % R][:, :], ACT.Identity,
                               bias=cols[:, COL["ln1b"] + k:COL["ln1b"] + k + 1],
                               scale=cols[:, COL["ln1w"] + k:COL["ln1w"] + k + 1]).then_inc(xf1.sem, 1)
            for m in range(4):
                act.wait_ge(QK_ps.sem, QK_ps.after(n, m + 1))
                for s in (qk_h, qk_l):
                    act.wait_ge(s.sem, s.after(n, m - 1) if m >= 2 else s.after(n - 1, m + 3))
                query = m % 2 == 0
                bias = qbias[:, m // 2:m // 2 + 1] if query else cols[:, COL["qkb"] + m:COL["qkb"] + m + 1]
                act.activation(qk32[:, m % 2, :], W[kind.index(("QK", m)) % R][:, :], ACT.Identity, bias=bias,
                               scale=(HD ** -0.5 if query else 1.0) / WS).then_inc(qk_f.sem, 1)

        def outputs_high(kind, n):
            for k in range(KD):
                act.wait_ge(OT_ps.sem, OT_ps.after(n - 1, k + 1))
                if k == 0:
                    act.wait_ge(OP_ps.sem, OP_ps.after(n - 2))
                act.activation(oT[0][:, k, :], W[kind.index(("OT", k)) % R][:, :], ACT.Copy).then_inc(oh.sem, 1)

        def norm2(kind, n):
            for k in range(KD):
                act.wait_ge(T2_ps.sem, T2_ps.after(n - 1, k + 1))
                if k == 0:
                    act.wait_ge(xh2.sem, xh2.after(n - 2))
                    act.wait_ge(xl2.sem, xl2.after(n - 2))
                act.activation(xT32[1][:, k, :], W[kind.index(("T2", k)) % R][:, :], ACT.Identity,
                               bias=cols[:, COL["ln2b"] + k:COL["ln2b"] + k + 1],
                               scale=cols[:, COL["ln2w"] + k:COL["ln2w"] + k + 1]).then_inc(xf2.sem, 1)

        def max_row(kind, n, c):
            act.wait_ge(MT_ps.sem, MT_ps.after(n, c + 1))
            act.wait_ge(m_in[c % 2].sem, m_in[c % 2].after(n, c // 2))
            act.activation(mrow[c % 2][0:C, :], W[kind.index(("MT", c)) % R][0:C, :], ACT.Copy)\
               .then_inc(mrow_in.sem, 1)

        def gelu(kind, n, m):
            act.wait_ge(H_ps.sem, H_ps.after(n - 1, m + 1))
            for s in (h_h, h_l):
                if m >= 2:
                    act.wait_ge(s.sem, s.after(n - 1, m - 1))
                else:
                    act.wait_ge(s.sem, s.after(n - 2, KF - 1 + m))
            act.activation(h32[:, m % 2, :], W[kind.index(("H", m)) % R][:, :], ACT.Gelu,
                           bias=cols[:, COL["f1b"] + m:COL["f1b"] + m + 1], scale=1.0 / WS).then_inc(h_f.sem, 1)

        def exps(n, c):
            if c < 2:
                act.wait_ge(O_ps.sem, O_ps.after(n - 1, c + 3))
            else:
                act.wait_ge(O_ps.sem, O_ps.after(n, c - 1))
            for q in range(6):
                act.wait_ge(S_ps.sem, S_ps.after(n, 6 * c + q + 1))
                act.activation(PR[c % 2][:, q, :], SC[(6 * c + q) % 2][:, :], ACT.Exp).then_inc(p_in.sem, 1)

        def out_rows(n, c):
            act.wait_ge(O_ps.sem, O_ps.after(n, c + 1))
            if c == 0:
                act.wait_ge(OS_ps.sem, OS_ps.after(n - 1))
            act.activation(OTs[:, c, :], O[:, :], ACT.Copy).then_inc(o_in.sem, 1)

        def body(kind, n, ahead, front, back):
            if back:
                outputs_high(kind, n)
            if front:
                max_row(kind, n, 0)
                exps(n, 0)
                max_row(kind, n, 1)
                out_rows(n, 0)
            if ahead:
                project(kind, n + 1)
            if front:
                exps(n, 1)
                max_row(kind, n, 2)
                out_rows(n, 1)
            if back:
                norm2(kind, n)
            if front:
                exps(n, 2)
                max_row(kind, n, 3)
                out_rows(n, 2)
            if back:
                for m in range(0, 4):
                    gelu(kind, n, m)
            if front:
                exps(n, 3)
            if back:
                for m in range(4, KF):
                    gelu(kind, n, m)
            if front:
                out_rows(n, 3)

        with act.Fori(0, L) as l:
            weights(l)
            act.wait_ge(bias_in.sem, bias_in.after(l))
            act.wait_ge(qb_ready.sem, qb_ready.after(l))
            body(PRE, l * NG - 1, True, False, False)
            body(HEAD, l * NG, True, True, False)
            with act.Fori(1, NG - 1) as g:
                body(STEADY, l * NG + g, True, True, True)
            body(LAST, l * NG + NG - 1, False, True, True)
            body(TAIL, l * NG + NG, False, False, True)

    @block.vector
    def _(dve):
        for s in (w_lo, qb_ready, ln1_steps, z1, xh1, v_in, qk_h, mx_in, rd_in, on_in, ol, xo, xb1, xb2,
                  ln2_steps, z2, xh2, h_h, y_x):
            dve.sem_inc(s.sem, s.credit())
        dve.memset(VS[:, :, :, :], 1.0).then_inc(s_init, 1)
        dve.wait_ge(s_const, 16 * 6)
        for dst, src in ((ident_b, ident[:, :]), (mask_q, z[0][:, 0, 0:P]), (mask_k, z[0][:, 0, P:2 * P])):
            last = dve.tensor_copy(dst[:, :], src)
        last.then_inc(s_init, 1)

        def weights(l):
            dve.wait_ge(Y_ps.sem, Y_ps.after(l * NG - 1))
            for i in range(NCH):
                dve.wait_ge(w_hi.sem, w_hi.after(l, i + 1))
                dve.scalar_tensor_tensor(w_half[1][:, i * CH:(i + 1) * CH], w_raw[i % 2][:, :], WS,
                                         w_half[0][:, i * CH:(i + 1) * CH], ALU.mult, ALU.subtract)\
                   .then_inc(w_lo.sem, 1)
            dve.wait_ge(bias_in.sem, bias_in.after(l))
            dve.wait_ge(QK_ps.sem, QK_ps.after(l * NG - 1))
            dve.tensor_scalar(qbias[:, :], cols[:, 0:4:2], HD ** -0.5, None, ALU.mult).then_inc(qb_ready.sem, 1)
            dve.wait_ge(qb_ready.sem, qb_ready.after(l))

        def norm1(n, g):
            dve.wait_ge(T1_ps.sem, T1_ps.after(n - 1))
            layer_norm(dve, lambda t: x[:, bass.ds(g * TT + t, 1), :], lambda t: z[0][:, t:t + 1, :], norm_buf[0],
                       ln1_steps.sem, lambda k: ln1_steps.after(n, k), z1.sem)

        def add_row(g, row, done):
            for t in range(TT):
                last = dve.tensor_tensor(x[:, bass.ds(g * TT + t, 1), :], x[:, bass.ds(g * TT + t, 1), :],
                                         rows[:, row, :].unsqueeze(1), ALU.add)
            last.then_inc(done.sem, 1)

        def project(n):
            for k in range(KD):
                dve.wait_ge(xf1.sem, xf1.after(n, k + 1))
                if k == 0:
                    dve.wait_ge(xl1.sem, xl1.after(n - 1))
                    dve.wait_ge(V_ps.sem, V_ps.after(n - 1))
                dve.tensor_copy(xT[0][0][:, k, :], xT32[0][:, k, :]).then_inc(xh1.sem, 1)

        def query_key_high(n):
            for m in range(4):
                dve.wait_ge(qk_f.sem, qk_f.after(n, m + 1))
                if m == 0:
                    dve.wait_ge(heads_in[0].sem, heads_in[0].after(n - 1))
                    dve.wait_ge(heads_in[1].sem, heads_in[1].after(n - 1))
                    dve.wait_ge(qk_l.sem, qk_l.after(n - 1))
                dve.tensor_copy(QK[0][:, m, :], qk32[:, m % 2, :]).then_inc(qk_h.sem, 1)

        def values(kind, n):
            for t in range(TT):
                dve.wait_ge(V_ps.sem, V_ps.after(n, t // 2 + 1))
                if t == 0:
                    dve.wait_ge(O_ps.sem, O_ps.after(n - 1))
                bank = W[kind.index(("V", t // 2)) % R]
                dve.scalar_tensor_tensor(VS[:, t, :, 0:HD],
                                         bank[:, (t % 2) * D:(t % 2 + 1) * D].rearrange("p (h d) -> p h d", h=H),
                                         1.0 / WS, rows[:, 0, :].rearrange("p (h d) -> p h d", h=H),
                                         ALU.mult, ALU.add).then_inc(v_in.sem, 1)

        def outputs(kind, n):
            for t in range(TT):
                dve.wait_ge(OS_ps.sem, OS_ps.after(n - 1, t + 1))
                bank = W[kind.index(("OS", t)) % R][:, :].rearrange("p (h d) -> p h d", h=H)
                if t == 0:
                    dve.wait_ge(OT_ps.sem, OT_ps.after(n - 2))
                dve.reciprocal(rden[:, t, :], bank[:, :, HD]).then_inc(rd_in.sem, 1)
                dve.wait_ge(rd_in.sem, rd_in.after(n - 1, t + 1))
                dve.tensor_tensor(On[:, t, :].rearrange("p (h d) -> p h d", h=H), bank[:, :, 0:HD],
                                  rden[:, t, :].unsqueeze(2).to_broadcast([P, H, HD]), ALU.mult)\
                   .then_inc(on_in.sem, 1)

        def residual(kind, n, g, name, ps, done, bias_done):
            dve.wait_ge(bias_done.sem, bias_done.after(n - 1))
            for k in range(2):
                dve.wait_ge(ps.sem, ps.after(n - 1, k + 1))
                xs = x[:, bass.ds(g * TT + 2 * k, 2), :].rearrange("p t d -> p (t d)")
                dve.scalar_tensor_tensor(xs, W[kind.index((name, k)) % R][:, :], 1.0 / WS, xs,
                                         ALU.mult, ALU.add).then_inc(done.sem, 1)

        def outputs_low(kind, n):
            for k in range(KD):
                dve.wait_ge(oh.sem, oh.after(n - 1, k + 1))
                if k == 0:
                    dve.wait_ge(OP_ps.sem, OP_ps.after(n - 2))
                dve.tensor_tensor(oT[1][:, k, :], W[kind.index(("OT", k)) % R][:, :], oT[0][:, k, :],
                                  ALU.subtract).then_inc(ol.sem, 1)

        def norm2(n, g):
            dve.wait_ge(xo.sem, xo.after(n - 1))
            dve.wait_ge(T2_ps.sem, T2_ps.after(n - 2))
            layer_norm(dve, lambda t: x[:, bass.ds(g * TT + t, 1), :], lambda t: z[1][:, t:t + 1, :], norm_buf[1],
                       ln2_steps.sem, lambda k: ln2_steps.after(n - 1, k), z2.sem)

        def norm2_high(n):
            for k in range(KD):
                dve.wait_ge(xf2.sem, xf2.after(n - 1, k + 1))
                if k == 0:
                    dve.wait_ge(xl2.sem, xl2.after(n - 2))
                    dve.wait_ge(H_ps.sem, H_ps.after(n - 2))
                dve.tensor_copy(xT[1][0][:, k, :], xT32[1][:, k, :]).then_inc(xh2.sem, 1)

        def maxima(n, c, chunks=range(6)):
            for q in chunks:
                b, i = divmod(q, 3)
                dve.wait_ge(M_ps.sem, M_ps.after(n, 6 * c + q + 1))
                if q == 0:
                    if c < 2:
                        dve.wait_ge(MT_ps.sem, MT_ps.after(n - 1, c + 3))
                    else:
                        dve.wait_ge(MT_ps.sem, MT_ps.after(n, c - 1))
                bank = M[(6 * c + q) % 2]
                if i < 2:
                    out, src = mx[c % 2][:, 2 * b + 1, 2 * i:2 * i + 2], bank[:, :].rearrange("p (h k) -> p h k", h=2)
                else:
                    out, src = mx[c % 2][:, 2 * b, :], bank[:, :].rearrange("p (h k) -> p h k", h=C)
                dve.tensor_reduce(out, src, AX.X, ALU.max, negate=True).then_inc(mx_in.sem, 1)

        def hidden_high(n, m):
            dve.wait_ge(h_f.sem, h_f.after(n - 1, m + 1))
            if m == 0:
                dve.wait_ge(Y_ps.sem, Y_ps.after(n - 2))
            dve.tensor_copy(hT[0][:, m, :], h32[:, m % 2, :]).then_inc(h_h.sem, 1)

        def body(kind, n, g, ahead, front, back, next_g=None):
            if front:
                values(kind, n)
            if back:
                outputs(kind, n)
            if front:
                maxima(n, 0, range(3))
            if back:
                outputs_low(kind, n)
            if front:
                maxima(n, 0, range(3, 6))
            if back:
                residual(kind, n, g - 1, "OP", OP_ps, xo, xb1)
            if front:
                maxima(n, 1)
            if ahead:
                project(n + 1)
            if back:
                norm2(n, g - 1)
            if ahead:
                query_key_high(n + 1)
            if front:
                maxima(n, 2)
            if back:
                norm2_high(n)
            if front:
                maxima(n, 3)
                add_row(g, 1, xb1)
            if back:
                dve.wait_ge(z2.sem, z2.after(n - 1))
                add_row(g - 1, 2, xb2)
                for m in range(KF):
                    hidden_high(n, m)
            if next_g is not None:
                norm1(n + 2, next_g)
            if back:
                residual(kind, n, g - 1, "Y", Y_ps, y_x, xb2)

        with dve.Fori(0, L) as l:
            weights(l)
            dve.wait_ge(y_x.sem, y_x.after(l * NG - 1))
            norm1(l * NG, 0)
            body(PRE, l * NG - 1, 0, True, False, False)
            norm1(l * NG + 1, 1)
            body(HEAD, l * NG, 0, True, True, False, 2)
            with dve.Fori(1, NG - 2) as g:
                body(STEADY, l * NG + g, g, True, True, True, g + 2)
            body(STEADY, l * NG + NG - 2, NG - 2, True, True, True)
            body(LAST, l * NG + NG - 1, NG - 1, False, True, True)
            body(TAIL, l * NG + NG, NG, False, False, True)
        dve.wait_ge(y_x.sem, y_x.after(L * NG - 1))

    @block.gpsimd
    def _(pool):
        for s in (xl1, qk_l, xl2, h_l):
            pool.sem_inc(s.sem, s.credit())
        pool.memset(QS[:, :, :], 0.0).then_inc(s_init, 1)
        pool.memset(KS[:, :, :], 0.0).then_inc(s_init, 1)

        def low(i, n, hi, out, last_read):
            for k in range(KD):
                pool.wait_ge(hi.sem, hi.after(n, k + 1))
                if k == 0:
                    pool.wait_ge(last_read.sem, last_read.after(n - 1))
                pool.tensor_tensor(xT[i][1][:, k, :], xT32[i][:, k, :], xT[i][0][:, k, :], ALU.subtract)\
                    .then_inc(out.sem, 1)

        def query_key_low(n):
            for m in range(4):
                pool.wait_ge(qk_h.sem, qk_h.after(n, m + 1))
                if m == 0:
                    pool.wait_ge(heads_in[0].sem, heads_in[0].after(n - 1))
                    pool.wait_ge(heads_in[1].sem, heads_in[1].after(n - 1))
                pool.tensor_tensor(QK[1][:, m, :], qk32[:, m % 2, :], QK[0][:, m, :], ALU.subtract)\
                    .then_inc(qk_l.sem, 1)

        def hidden_low(n, m):
            pool.wait_ge(h_h.sem, h_h.after(n - 1, m + 1))
            if m == 0:
                pool.wait_ge(Y_ps.sem, Y_ps.after(n - 2))
            pool.tensor_tensor(hT[1][:, m, :], h32[:, m % 2, :], hT[0][:, m, :], ALU.subtract)\
                .then_inc(h_l.sem, 1)

        def body(n, ahead, back):
            if ahead:
                low(0, n + 1, xh1, xl1, V_ps)
                query_key_low(n + 1)
            if back:
                low(1, n - 1, xh2, xl2, H_ps)
                for m in range(KF):
                    hidden_low(n, m)

        with pool.Fori(0, L) as l:
            body(l * NG - 1, True, False)
            body(l * NG, True, False)
            with pool.Fori(1, NG - 1) as g:
                body(l * NG + g, True, True)
            body(l * NG + NG - 1, False, True)
            body(l * NG + NG, False, True)

    block_ctx.close()


def cross(nc, sb, sem, psum, shared, dram):
    x, ident, QS, KS, VS = shared["x"], shared["ident"], shared["QS"], shared["KS"], shared["VS"]
    W, M, SC, O = psum["W"], psum["M"], psum["S"], psum["O"]
    QK, qk32, mx, mrow, PR, OTs, On, oT, rden = (
        shared[k] for k in ("QK", "qk32", "mx", "mrow", "PR", "OTs", "On", "oT", "rden"))
    weight, weight_ws = shared["expert_weight"], shared["expert_weight_ws"]
    xT_halves = dram["xT_halves"]

    WC = KD * 3 * D + KD * F2 + KF2 * D + KD * E
    w_raw = sb("c_raw", [P, WC], F32)
    w_half = [sb(f"c_half{i}", [P, WC], F16) for i in range(2)]
    at, views = 0, {}
    for name, k, cols_of in (("q", KD, D), ("k", KD, D), ("v", KD, D), ("f1", KD, F2), ("f2", KF2, D), ("r", KD, E)):
        views[name] = [w[:, at:at + k * cols_of].rearrange("p (k n) -> p k n", k=k) for w in w_half]
        at += k * cols_of
    ROWS = 4 * D + E
    rows = sb("c_rows", [P, ROWS], F32)
    row = {name: rows[:, i * D:(i + 1) * D] for i, name in enumerate(("fw", "fb", "bv", "b2"))}
    router_bias = rows[:, 4 * D:ROWS]
    cols = sb("c_cols", [P, 8], F32)
    qbias = sb("c_qbias", [P, 2], F32)
    x0 = sb("c_x0", [P, TT, D], F32)
    ctx32 = sb("c_ctx32", [P, KD, GB * S], F32)
    ctx = [sb(f"c_ctx{h}", [P, KD, GB * S], F16) for h in range(2)]
    z = [sb(f"c_z{i}", [P, TT, D], F32) for i in range(3)]
    norm_buf = [NormBuffers(sb, f"c_norm{i}", shared["dve_gate"]) for i in range(3)]
    xT = [[sb(f"c_xT{i}_{h}", [P, KD, GT], F16) for h in range(2)] for i in range(2)]
    h32 = sb("c_h32", [P, 2, GT], F32)
    hT = [sb(f"c_hT{h}", [P, KF2, GT], F16) for h in range(2)]
    logit = sb("c_logit", [P, TT, E], F32)
    top = sb("c_top", [P, TT, 8], F32)
    less = sb("c_less", [P, TT, E], F32)
    chosen = sb("c_chosen", [P, TT, E], F32)
    power = sb("c_power", [P, TT, E], F32)
    total = sb("c_total", [P, TT], F32)

    def sig(name, per, unit=1):
        return Signal(sem("c_" + name), per, unit)

    s_const, s_w_hi, s_w_lo, s_qb = sem("c_const"), sem("c_w_hi"), sem("c_w_lo"), sem("c_qb")
    x0_in, ctx_in = sig("x0_in", 1, 16), sig("ctx_in", 1, 16)
    steps = [sig(f"steps{i}", NORM_STEPS) for i in range(3)]
    zf, mix, z1, z1b = sig("zf", TT), sig("mix", 3), sig("z1", TT), sig("z1b", 1)
    T1_ps, xh1, xl1 = sig("T1_ps", KD), sig("xh1", KD), sig("xl1", KD)
    ctx_h, ctx_l = sig("ctx_h", 1), sig("ctx_l", 1)
    V_ps, v_in = sig("V_ps", 1), sig("v_in", GB)
    QK_ps, qk_f, qk_h, qk_l = sig("QK_ps", 4), sig("qk_f", 4), sig("qk_h", 4), sig("qk_l", 4)
    heads_in = [sig(f"heads_in{m}", 6, 16) for m in range(2)]
    CH = 4
    M_ps, mx_in = sig("M_ps", CH * C), sig("mx_in", CH * C)
    MT_ps, mrow_in = sig("MT_ps", C), sig("mrow_in", C)
    m_in = [sig(f"m_in{i}", C // 2, 16) for i in range(2)]
    S_ps, p_in, O_ps, o_in = sig("S_ps", CH * C), sig("p_in", CH * C), sig("O_ps", C), sig("o_in", C)
    OS_ps, rd_in, on_in = sig("OS_ps", TT), sig("rd_in", TT), sig("on_in", TT)
    OT_ps, oh, ol = sig("OT_ps", KD), sig("oh", KD), sig("ol", KD)
    H_ps, h_f, h_h, h_l = sig("H_ps", KF2), sig("h_f", KF2), sig("h_h", KF2), sig("h_l", KF2)
    Y_ps, y_in, z2, x_in = sig("Y_ps", 2), sig("y_in", 2), sig("z2", TT), sig("x_in", 1)
    T2_ps, xh2, xl2, halves_out = sig("T2_ps", KD), sig("xh2", KD), sig("xl2", KD), sig("halves_out", 2, 16)
    R_ps, route, powers = sig("R_ps", 1), sig("route", TT + 7), sig("powers", 1)

    R = len(W)
    READERS = {"T1": [(xh1, 1), (xl1, 1)], "V": [(v_in, GB)], "QK": [(qk_f, 1)], "MT": [(mrow_in, 1)],
               "OS": [(on_in, 1)], "OT": [(oh, 1), (ol, 1)], "H": [(h_f, 1)], "Y": [(y_in, 1)],
               "T2": [(xh2, 1), (xl2, 1)], "R": [(route, 1)]}
    ROUND = {"T1": 1, "QK": 1, "V": 0, "MT": 0} | {stage: -1 for stage in ("OS", "OT", "H", "Y", "T2", "R")}

    def tiles_of(ahead, front, back):
        def some(wanted, stage, count):
            return [(stage, k) for k in range(count)] if wanted else []

        out = some(front, "V", 1) + some(back, "OS", TT) + some(back, "OT", KD)
        out += [("MT", 0)] * front + some(back, "H", KF2) + [("MT", 1)] * front
        out += some(ahead, "T1", KD) + some(ahead, "QK", 4) + some(back, "Y", 2) + [("MT", 2)] * front
        out += [("MT", 3)] * front + some(back, "T2", KD) + some(back, "R", 1)
        return out + [None] * (-len(out) % R)

    PRE, HEAD, STEADY = tiles_of(True, False, False), tiles_of(True, True, False), tiles_of(True, True, True)
    LAST, TAIL = tiles_of(False, True, True), tiles_of(False, False, True)
    BEFORE = {id(PRE): [], id(HEAD): [(PRE, -1)], id(STEADY): [(HEAD, -1), (STEADY, -1)],
              id(LAST): [(STEADY, -1)], id(TAIL): [(LAST, -1)]}

    def work(kind, tile):
        return W[kind.index(tile) % R]

    def free_tile(pe, kind, n, tile, inputs=()):
        pos = kind.index(tile)
        need = {signal: (m, signal.per) for signal, m in inputs}
        for other, m in [(kind, 0)] if pos >= R else BEFORE[id(kind)]:
            q = pos - R if pos >= R else len(other) - R + pos
            while other[q] is None:
                q -= R
            stage, k = other[q]
            for signal, each in READERS[stage]:
                at = (m + ROUND[stage], (k + 1) * each)
                need[signal] = max(need.get(signal, at), at)
        for signal, (m, raises) in need.items():
            pe.wait_ge(signal.sem, signal.after(n + m, raises))
        return work(kind, tile)

    def all_bodies(eng, body):
        body(PRE, -1, True, False, False)
        body(HEAD, 0, True, True, False)
        with eng.Fori(1, NG - 1) as n:
            body(STEADY, n, True, True, True)
        body(LAST, NG - 1, False, True, True)
        body(TAIL, NG, False, False, True)

    block_ctx = ExitStack()
    block = block_ctx.enter_context(nc.Block())

    @block.sync
    def _(sp):
        for s in (x0_in, ctx_in, *heads_in, *m_in, halves_out):
            sp.sem_inc(s.sem, s.credit())
        sp.dma_start(w_raw[:, :], dram["cross_weights"]).then_inc(s_const, 16)
        sp.dma_start(rows[:, :], dram["cross_rows"].partition_broadcast(P)).then_inc(s_const, 16)
        sp.dma_start(cols[:, :], dram["cross_cols"]).then_inc(s_const, 16)
        sp.dma_start(KS[R_POS:R_POS + 2, :, :], dram["zeros2"]).then_inc(s_const, 16)

        def load(n):
            sp.wait_ge(mix.sem, mix.after(n - 1))
            sp.dma_start(x0[:, :, :], dram["x"][bass.ds(n * GT, GT)].rearrange("(t p) d -> p t d", p=P))\
              .then_inc(x0_in.sem, 16)
            sp.wait_ge(ctx_h.sem, ctx_h.after(n - 1))
            sp.wait_ge(ctx_l.sem, ctx_l.after(n - 1))
            sp.dma_start(ctx32[:, :, :], dram["ctx"][:, :, bass.ds(n * (GB * S), GB * S)]).then_inc(ctx_in.sem, 16)

        def heads(n, m):
            sp.wait_ge(S_ps.sem, S_ps.after(n - 1, 2 * CH * (m + 1)))
            part_from_wait(sp, shared["sp_gate"])
            sp.wait_ge(qk_h.sem, qk_h.after(n, 2 * m + 2))
            sp.wait_ge(qk_l.sem, qk_l.after(n, 2 * m + 2))
            for tile, dst, width, half_rows in ((2 * m, QS, GT, ((0, 0), (R_HI2, 0), (R_LO, 1))),
                                                (2 * m + 1, KS, GB * S, ((0, 0), (R_LO, 0), (R_HI2, 1)))):
                for r, half in half_rows:
                    sp.dma_start(dst[r:r + HD, 8 * m:8 * m + 8, 0:width], QK[half][:, tile, 0:width])\
                      .then_inc(heads_in[m].sem, 16)

        def maximum(n, c):
            sp.wait_ge(mrow_in.sem, mrow_in.after(n, c + 1))
            sp.dma_start(QS[R_MAX:R_MAX + 1, C * c:C * c + C, :], mrow[c % 2][0:C, :])\
              .then_inc(m_in[c % 2].sem, 16)

        def halves(n):
            for half, s in enumerate((xh2, xl2)):
                sp.wait_ge(s.sem, s.after(n))
                part_from_wait(sp, shared["sp_gate"])
                sp.dma_start(xT_halves[half, :, :, bass.ds(n * GT, GT)], xT[1][half][:, :, :])\
                  .then_inc(halves_out.sem, 16)

        def body(kind, n, ahead, front, back):
            if front:
                for c in range(3):
                    maximum(n, c)
            if ahead:
                heads(n + 1, 0)
            if front:
                maximum(n, 3)
            if ahead:
                heads(n + 1, 1)
            if back:
                halves(n - 1)

        load(0)
        body(PRE, -1, True, False, False)
        load(1)
        body(HEAD, 0, True, True, False)
        load(2)
        with sp.Fori(1, NG - 2) as n:
            body(STEADY, n, True, True, True)
            load(n + 2)
        body(STEADY, NG - 2, True, True, True)
        body(LAST, NG - 1, False, True, True)
        body(TAIL, NG, False, False, True)
        sp.wait_ge(halves_out.sem, halves_out.after(NG - 1))

    @block.tensor
    def _(pe):
        for s in (T1_ps, V_ps, QK_ps, M_ps, MT_ps, S_ps, O_ps, OS_ps, OT_ps, H_ps, Y_ps, T2_ps, R_ps):
            pe.sem_inc(s.sem, s.credit())
        pe.wait_ge(s_const, 16 * 4)
        pe.wait_ge(s_w_hi, 1)
        pe.wait_ge(s_w_lo, 1)

        def turn(kind, n, name, ps, src, ready):
            for k in range(KD):
                bank = free_tile(pe, kind, n, (name, k), ((ready, ROUND[name]),))
                for t in range(TT):
                    last = pe.transpose(bank[:, t * P:(t + 1) * P], src[:, t, k * P:(k + 1) * P], ident[:, :])
                last.then_inc(ps.sem, 1)

        def row_scores(n, c, q):
            if c % 2 == 0 and q == 0:
                pe.wait_ge(heads_in[c // 2].sem, heads_in[c // 2].after(n))
            i = CH * c + q
            pe.wait_ge(mx_in.sem, mx_in.after(n, i - 1) if i >= 2 else mx_in.after(n - 1, CH * C - 1 + i))
            bank, b = M[i % 2], q // 2
            for u in range(C):
                last = pe.matmul(bank[:, u * S:(u + 1) * S], QS[0:R_MAX, C * c + u, q * P:(q + 1) * P],
                                 KS[0:R_MAX, C * c + u, b * S:(b + 1) * S], start=True, stop=True)
            last.then_inc(M_ps.sem, 1)

        def turn_maxima(kind, n, c):
            bank = free_tile(pe, kind, n, ("MT", c))
            pe.wait_ge(mx_in.sem, mx_in.after(n, CH * (c + 1)))
            for t in range(TT):
                last = pe.transpose(bank[0:C, t * P:(t + 1) * P], mx[c % 2][:, t, :], ident[:, :])
            last.then_inc(MT_ps.sem, 1)

        def key_scores(n, c, q):
            if q == 0:
                pe.wait_ge(m_in[c % 2].sem, m_in[c % 2].after(n, c // 2 + 1))
            i = CH * c + q
            pe.wait_ge(p_in.sem, p_in.after(n, i - 1) if i >= 2 else p_in.after(n - 1, CH * C - 1 + i))
            bank, b = SC[i % 2], q // 2
            for u in range(2):
                h = C * c + 2 * (q % 2) + u
                last = pe.matmul(bank[0:S, u * T:(u + 1) * T], KS[:, h, b * S:(b + 1) * S],
                                 QS[:, h, b * T:(b + 1) * T], start=True, stop=True)
            last.then_inc(S_ps.sem, 1)

        def attend(n, c):
            if c == 0:
                pe.wait_ge(v_in.sem, v_in.after(n))
            pe.wait_ge(p_in.sem, p_in.after(n, CH * (c + 1)))
            pe.wait_ge(o_in.sem, o_in.after(n, c) if c else o_in.after(n - 1))
            for b in range(GB):
                for u in range(C):
                    last = pe.matmul(O[32 * u:32 * u + 32, b * T:(b + 1) * T], VS[0:S, b, C * c + u, :],
                                     PR[c % 2][0:S, 2 * b + u // 2, (u % 2) * T:(u % 2 + 1) * T],
                                     start=True, stop=True)
            last.then_inc(O_ps.sem, 1)

        def values(kind, n):
            bank = free_tile(pe, kind, n, ("V", 0), ((ctx_h, 0), (ctx_l, 0)))
            for b in range(GB):
                last = split_matmuls(pe, bank[0:S, b * D:(b + 1) * D], lambda h, k: ctx[h][:, k, b * S:(b + 1) * S],
                                     lambda h, k: views["v"][h][:, k, :], KD)
            last.then_inc(V_ps.sem, 1)

        def queries_keys(kind, n):
            for m in range(4):
                ready = (((xh1, 1), (xl1, 1)), ((ctx_h, 1), (ctx_l, 1)), (), ())[m]
                bank = free_tile(pe, kind, n, ("QK", m), ready)
                side, src, width = (("q", xT[0], GT), ("k", ctx, GB * S))[m % 2]
                split_matmuls(pe, bank[:, 0:width],
                              lambda h, k: views[side][h][:, k, (m // 2) * P:(m // 2 + 1) * P],
                              lambda h, k: src[h][:, k, :], KD).then_inc(QK_ps.sem, 1)

        def turn_outputs(kind, n):
            for t in range(TT):
                bank = free_tile(pe, kind, n, ("OS", t), ((o_in, -1),))
                for c in range(C):
                    last = pe.transpose(bank[:, c * P:(c + 1) * P], OTs[:, c, t * P:(t + 1) * P], ident[:, :])
                last.then_inc(OS_ps.sem, 1)

        def hidden(kind, n):
            for m in range(KF2):
                bank = free_tile(pe, kind, n, ("H", m), ((oh, -1), (ol, -1)))
                split_matmuls(pe, bank[:, :], lambda h, k: views["f1"][h][:, k, m * P:(m + 1) * P],
                              lambda h, k: oT[h][:, k, :], KD).then_inc(H_ps.sem, 1)

        def outputs(kind, n):
            for k in range(2):
                bank = free_tile(pe, kind, n, ("Y", k), ((h_h, -1), (h_l, -1)))
                for u in range(2):
                    t = 2 * k + u
                    last = split_matmuls(pe, bank[:, u * D:(u + 1) * D], lambda h, kk: hT[h][:, kk, t * P:(t + 1) * P],
                                         lambda h, kk: views["f2"][h][:, kk, :], KF2)
                last.then_inc(Y_ps.sem, 1)

        def router(kind, n):
            bank = free_tile(pe, kind, n, ("R", 0), ((xh2, -1), (xl2, -1)))
            for t in range(TT):
                last = split_matmuls(pe, bank[:, t * E:(t + 1) * E], lambda h, k: xT[1][h][:, k, t * P:(t + 1) * P],
                                     lambda h, k: views["r"][h][:, k, :], KD)
            last.then_inc(R_ps.sem, 1)

        def body(kind, n, ahead, front, back):
            def interleaved(c):
                for q in range(CH):
                    if c + 1 < C:
                        row_scores(n, c + 1, q)
                    key_scores(n, c, q)

            if front:
                values(kind, n)
                row_scores(n, 0, 0)
                row_scores(n, 0, 1)
            if back:
                turn_outputs(kind, n)
            if front:
                row_scores(n, 0, 2)
                row_scores(n, 0, 3)
            if back:
                turn(kind, n, "OT", OT_ps, On, on_in)
            if front:
                turn_maxima(kind, n, 0)
            if back:
                hidden(kind, n)
            if front:
                interleaved(0)
                turn_maxima(kind, n, 1)
                attend(n, 0)
            if ahead:
                turn(kind, n, "T1", T1_ps, z[1], z1)
                queries_keys(kind, n)
            if back:
                outputs(kind, n)
            if front:
                interleaved(1)
                turn_maxima(kind, n, 2)
                attend(n, 1)
                interleaved(2)
                turn_maxima(kind, n, 3)
                attend(n, 2)
            if back:
                turn(kind, n, "T2", T2_ps, z[2], z2)
            if front:
                interleaved(3)
                attend(n, 3)
            if back:
                router(kind, n)

        all_bodies(pe, body)

    @block.scalar
    def _(act):
        for s in (ctx_h, xh1, qk_f, mrow_in, p_in, o_in, oh, h_f, xh2, powers):
            act.sem_inc(s.sem, s.credit())
        act.wait_ge(s_const, 16 * 4)
        act.activation(w_half[0][:, :], w_raw[:, :], ACT.Copy, scale=WS).then_inc(s_w_hi, 1)
        act.wait_ge(s_qb, 1)

        def project(kind, n):
            act.wait_ge(ctx_in.sem, ctx_in.after(n + 1))
            act.wait_ge(V_ps.sem, V_ps.after(n))
            act.wait_ge(QK_ps.sem, QK_ps.after(n))
            act.wait_ge(ctx_l.sem, ctx_l.after(n))
            act.activation(ctx[0][:, :, :], ctx32[:, :, :], ACT.Copy).then_inc(ctx_h.sem, 1)
            for k in range(KD):
                act.wait_ge(T1_ps.sem, T1_ps.after(n + 1, k + 1))
                act.activation(xT[0][0][:, k, :], work(kind, ("T1", k))[:, :], ACT.Copy).then_inc(xh1.sem, 1)

        def queries_keys(kind, n):
            for m in range(4):
                act.wait_ge(QK_ps.sem, QK_ps.after(n + 1, m + 1))
                for s in (qk_h, qk_l):
                    act.wait_ge(s.sem, s.after(n + 1, m - 1) if m >= 2 else s.after(n, m + 3))
                query = m % 2 == 0
                width = GT if query else GB * S
                act.activation(qk32[:, m % 2, 0:width], work(kind, ("QK", m))[:, 0:width], ACT.Identity,
                               bias=qbias[:, m // 2:m // 2 + 1] if query else cols[:, m:m + 1],
                               scale=(HD ** -0.5 if query else 1.0) / WS).then_inc(qk_f.sem, 1)

        def max_row(kind, n, c):
            act.wait_ge(MT_ps.sem, MT_ps.after(n, c + 1))
            act.wait_ge(m_in[c % 2].sem, m_in[c % 2].after(n, c // 2))
            act.activation(mrow[c % 2][0:C, :], work(kind, ("MT", c))[0:C, :], ACT.Copy).then_inc(mrow_in.sem, 1)

        def exps(n, c):
            if c < 2:
                act.wait_ge(O_ps.sem, O_ps.after(n - 1, c + 3))
            else:
                act.wait_ge(O_ps.sem, O_ps.after(n, c - 1))
            for q in range(CH):
                act.wait_ge(S_ps.sem, S_ps.after(n, CH * c + q + 1))
                act.activation(PR[c % 2][0:S, q, :], SC[(CH * c + q) % 2][0:S, :], ACT.Exp).then_inc(p_in.sem, 1)

        def out_rows(n, c):
            act.wait_ge(O_ps.sem, O_ps.after(n, c + 1))
            if c == 0:
                act.wait_ge(OS_ps.sem, OS_ps.after(n - 1))
            act.activation(OTs[:, c, :], O[:, :], ACT.Copy).then_inc(o_in.sem, 1)

        def hidden(kind, n):
            for m in range(KF2):
                act.wait_ge(H_ps.sem, H_ps.after(n - 1, m + 1))
                for s in (h_h, h_l):
                    act.wait_ge(s.sem, s.after(n - 1, m - 1) if m >= 2 else s.after(n - 2, KF2 - 1 + m))
                act.activation(h32[:, m % 2, :], work(kind, ("H", m))[:, :], ACT.Relu,
                               bias=cols[:, 4 + m:5 + m], scale=1.0 / WS).then_inc(h_f.sem, 1)

        def body(kind, n, ahead, front, back):
            if back:
                for k in range(KD):
                    act.wait_ge(OT_ps.sem, OT_ps.after(n - 1, k + 1))
                    act.wait_ge(H_ps.sem, H_ps.after(n - 2))
                    act.activation(oT[0][:, k, :], work(kind, ("OT", k))[:, :], ACT.Copy).then_inc(oh.sem, 1)
            if front:
                max_row(kind, n, 0)
            if back:
                hidden(kind, n)
            if front:
                exps(n, 0)
                max_row(kind, n, 1)
                out_rows(n, 0)
            if ahead:
                project(kind, n)
                queries_keys(kind, n)
            if front:
                exps(n, 1)
                max_row(kind, n, 2)
                out_rows(n, 1)
                exps(n, 2)
                max_row(kind, n, 3)
                out_rows(n, 2)
            if back:
                for k in range(KD):
                    act.wait_ge(T2_ps.sem, T2_ps.after(n - 1, k + 1))
                    if k == 0:
                        act.wait_ge(halves_out.sem, halves_out.after(n - 2))
                        act.wait_ge(R_ps.sem, R_ps.after(n - 2))
                    act.activation(xT[1][0][:, k, :], work(kind, ("T2", k))[:, :], ACT.Copy).then_inc(xh2.sem, 1)
            if front:
                exps(n, 3)
                out_rows(n, 3)
            if back:
                act.wait_ge(route.sem, route.after(n - 1, TT + 2))
                act.activation(power[:, :, :], less[:, :, :], ACT.Exp).then_inc(powers.sem, 1)

        all_bodies(act, body)

    @block.vector
    def _(dve):
        for s in (*steps, zf, mix, z1, z1b, xl1, ctx_l, v_in, qk_h, mx_in, rd_in, on_in, ol, h_h, y_in, z2, x_in,
                  xl2, route):
            dve.sem_inc(s.sem, s.credit())
        dve.wait_ge(s_const, 16 * 4)
        dve.wait_ge(s_w_hi, 1)
        dve.scalar_tensor_tensor(w_half[1][:, :], w_raw[:, :], WS, w_half[0][:, :], ALU.mult, ALU.subtract)\
           .then_inc(s_w_lo, 1)
        dve.tensor_scalar(qbias[:, :], cols[:, 0:4:2], HD ** -0.5, None, ALU.mult).then_inc(s_qb, 1)

        def norm_sum(n):
            dve.wait_ge(z1.sem, z1.after(n - 1))
            layer_norm(dve, lambda t: x[:, bass.ds(n * TT + t, 1), :], lambda t: z[0][:, t:t + 1, :], norm_buf[0],
                       steps[0].sem, lambda k: steps[0].after(n, k), zf.sem)
            dve.wait_ge(zf.sem, zf.after(n))
            for i, (other, op) in enumerate(((row["fw"], ALU.mult), (row["fb"], ALU.add), (None, ALU.add))):
                if other is None:
                    dve.wait_ge(x0_in.sem, x0_in.after(n))
                dve.wait_ge(mix.sem, mix.after(n, i))
                second = x0[:, :, :] if other is None else other.unsqueeze(1).to_broadcast([P, TT, D])
                dve.tensor_tensor(z[0][:, :, :], z[0][:, :, :], second, op).then_inc(mix.sem, 1)
            dve.wait_ge(mix.sem, mix.after(n))
            dve.wait_ge(T1_ps.sem, T1_ps.after(n - 1))
            layer_norm(dve, lambda t: z[0][:, t, :], lambda t: z[1][:, t, :], norm_buf[1],
                       steps[1].sem, lambda k: steps[1].after(n, k), z1.sem)
            dve.wait_ge(z1.sem, z1.after(n))
            dve.tensor_tensor(x[:, bass.ds(n * TT, TT), :], z[1][:, :, :], row["b2"].unsqueeze(1)
                              .to_broadcast([P, TT, D]), ALU.add).then_inc(z1b.sem, 1)

        def project_low(kind, n):
            dve.wait_ge(ctx_h.sem, ctx_h.after(n + 1))
            dve.tensor_tensor(ctx[1][:, :, :], ctx32[:, :, :], ctx[0][:, :, :], ALU.subtract).then_inc(ctx_l.sem, 1)
            for k in range(KD):
                dve.wait_ge(xh1.sem, xh1.after(n + 1, k + 1))
                dve.tensor_tensor(xT[0][1][:, k, :], work(kind, ("T1", k))[:, :], xT[0][0][:, k, :], ALU.subtract)\
                   .then_inc(xl1.sem, 1)

        def query_key_high(n):
            for m in range(4):
                dve.wait_ge(qk_f.sem, qk_f.after(n + 1, m + 1))
                if m == 0:
                    for s in (*heads_in, qk_l):
                        dve.wait_ge(s.sem, s.after(n))
                width = GT if m % 2 == 0 else GB * S
                dve.tensor_copy(QK[0][:, m, 0:width], qk32[:, m % 2, 0:width]).then_inc(qk_h.sem, 1)

        def values(kind, n):
            dve.wait_ge(O_ps.sem, O_ps.after(n - 1))
            for b in range(GB):
                dve.wait_ge(V_ps.sem, V_ps.after(n))
                dve.scalar_tensor_tensor(VS[0:S, b, :, 0:HD],
                                         work(kind, ("V", 0))[0:S, b * D:(b + 1) * D].rearrange("p (h d) -> p h d", h=H),
                                         1.0 / WS, row["bv"][0:S].rearrange("p (h d) -> p h d", h=H),
                                         ALU.mult, ALU.add).then_inc(v_in.sem, 1)

        def maxima(n, c, chunks=range(CH)):
            for q in chunks:
                dve.wait_ge(M_ps.sem, M_ps.after(n, CH * c + q + 1))
                if q == 0:
                    dve.wait_ge(MT_ps.sem, MT_ps.after(n - 1, c + 3) if c < 2 else MT_ps.after(n, c - 1))
                dve.tensor_reduce(mx[c % 2][:, q, :],
                                  M[(CH * c + q) % 2][:, 0:C * S].rearrange("p (h k) -> p h k", h=C),
                                  AX.X, ALU.max, negate=True).then_inc(mx_in.sem, 1)

        def outputs(kind, n):
            for t in range(TT):
                dve.wait_ge(OS_ps.sem, OS_ps.after(n - 1, t + 1))
                bank = work(kind, ("OS", t))[:, :].rearrange("p (h d) -> p h d", h=H)
                dve.reciprocal(rden[:, t, :], bank[:, :, HD]).then_inc(rd_in.sem, 1)
                dve.wait_ge(rd_in.sem, rd_in.after(n - 1, t + 1))
                dve.tensor_tensor(On[:, t, :].rearrange("p (h d) -> p h d", h=H), bank[:, :, 0:HD],
                                  rden[:, t, :].unsqueeze(2).to_broadcast([P, H, HD]), ALU.mult)\
                   .then_inc(on_in.sem, 1)

        def outputs_low(kind, n):
            for k in range(KD):
                dve.wait_ge(oh.sem, oh.after(n - 1, k + 1))
                dve.tensor_tensor(oT[1][:, k, :], work(kind, ("OT", k))[:, :], oT[0][:, k, :], ALU.subtract)\
                   .then_inc(ol.sem, 1)

        def hidden_high(n):
            for m in range(KF2):
                dve.wait_ge(h_f.sem, h_f.after(n - 1, m + 1))
                if m == 0:
                    dve.wait_ge(Y_ps.sem, Y_ps.after(n - 2))
                dve.tensor_copy(hT[0][:, m, :], h32[:, m % 2, :]).then_inc(h_h.sem, 1)

        def residual(kind, n):
            for k in range(2):
                dve.wait_ge(Y_ps.sem, Y_ps.after(n - 1, k + 1))
                part = x[:, bass.ds((n - 1) * TT + 2 * k, 2), :].rearrange("p t d -> p (t d)")
                dve.scalar_tensor_tensor(part, work(kind, ("Y", k))[:, :], 1.0 / WS, part, ALU.mult, ALU.add)\
                   .then_inc(y_in.sem, 1)
            dve.wait_ge(y_in.sem, y_in.after(n - 1))
            dve.wait_ge(T2_ps.sem, T2_ps.after(n - 2))
            layer_norm(dve, lambda t: x[:, bass.ds((n - 1) * TT + t, 1), :], lambda t: z[2][:, t:t + 1, :],
                       norm_buf[2], steps[2].sem, lambda k: steps[2].after(n - 1, k), z2.sem)
            dve.wait_ge(z2.sem, z2.after(n - 1))
            part_from_wait(dve, shared["dve_gate"])
            dve.tensor_copy(x[:, bass.ds((n - 1) * TT, TT), :], z[2][:, :, :]).then_inc(x_in.sem, 1)

        def normed_low(kind, n):
            for k in range(KD):
                dve.wait_ge(xh2.sem, xh2.after(n - 1, k + 1))
                dve.tensor_tensor(xT[1][1][:, k, :], work(kind, ("T2", k))[:, :], xT[1][0][:, k, :], ALU.subtract)\
                   .then_inc(xl2.sem, 1)

        def router(kind, n):
            dve.wait_ge(R_ps.sem, R_ps.after(n))
            dve.scalar_tensor_tensor(logit[:, :, :], work(kind, ("R", 0))[:, 0:TT * E].rearrange("p (t e) -> p t e", t=TT),
                                     1.0 / WS, router_bias.unsqueeze(1).to_broadcast([P, TT, E]),
                                     ALU.mult, ALU.add).then_inc(route.sem, 1)
            dve.wait_ge(route.sem, route.after(n, 1))
            part_from_wait(dve, shared["dve_gate"])
            for t in range(TT):
                dve.max(top[:, t, :], logit[:, t, :]).then_inc(route.sem, 1)
            dve.wait_ge(route.sem, route.after(n, TT + 1))
            dve.tensor_tensor(less[:, :, :], logit[:, :, :], top[:, :, 0:1].to_broadcast([P, TT, E]), ALU.subtract)\
               .then_inc(route.sem, 1)
            dve.tensor_tensor(chosen[:, :, :], logit[:, :, :], top[:, :, 1:2].to_broadcast([P, TT, E]), ALU.is_ge)\
               .then_inc(route.sem, 1)
            dve.wait_ge(route.sem, route.after(n, TT + 3))
            dve.wait_ge(powers.sem, powers.after(n))
            dve.tensor_tensor(power[:, :, :], power[:, :, :], chosen[:, :, :], ALU.mult).then_inc(route.sem, 1)
            dve.wait_ge(route.sem, route.after(n, TT + 4))
            dve.tensor_reduce(total[:, :], power[:, :, :], AX.X, ALU.add).then_inc(route.sem, 1)
            dve.wait_ge(route.sem, route.after(n, TT + 5))
            dve.reciprocal(total[:, :], total[:, :]).then_inc(route.sem, 1)
            dve.wait_ge(route.sem, route.after(n, TT + 6))
            dve.tensor_tensor(power[:, :, :], power[:, :, :], total[:, :].unsqueeze(2).to_broadcast([P, TT, E]),
                              ALU.mult).then_inc(route.sem, 1)
            dve.wait_ge(route.sem, route.after(n, TT + 7))
            for scale, dst in ((1.0, weight), (1.0 / WS, weight_ws)):
                for t in range(TT):
                    dve.tensor_scalar(dst[:, :].rearrange("p (e n) -> p n e", e=E)[:, bass.ds(n * TT + t, 1), :],
                                      power[:, t:t + 1, :], scale, None, ALU.mult)

        def body(kind, n, ahead, front, back, next_norm):
            if front:
                values(kind, n)
                maxima(n, 0, range(0, 2))
            if back:
                outputs(kind, n)
            if front:
                maxima(n, 0, range(2, 4))
            if back:
                outputs_low(kind, n)
                hidden_high(n)
            if front:
                maxima(n, 1)
            if ahead:
                project_low(kind, n)
                query_key_high(n)
            if back:
                residual(kind, n)
            if front:
                maxima(n, 2)
                maxima(n, 3)
            if back:
                normed_low(kind, n)
            if next_norm:
                norm_sum(n + 2)
            if back:
                router(kind, n - 1)

        norm_sum(0)
        body(PRE, -1, True, False, False, True)
        body(HEAD, 0, True, True, False, True)
        with dve.Fori(1, NG - 2) as n:
            body(STEADY, n, True, True, True, True)
        body(STEADY, NG - 2, True, True, True, False)
        body(LAST, NG - 1, False, True, True, False)
        body(TAIL, NG, False, False, True, False)

    @block.gpsimd
    def _(pool):
        for s in (qk_l, h_l):
            pool.sem_inc(s.sem, s.credit())

        def body(kind, n, ahead, front, back):
            if back:
                for m in range(KF2):
                    pool.wait_ge(h_h.sem, h_h.after(n - 1, m + 1))
                    if m == 0:
                        pool.wait_ge(Y_ps.sem, Y_ps.after(n - 2))
                    pool.tensor_tensor(hT[1][:, m, :], h32[:, m % 2, :], hT[0][:, m, :], ALU.subtract)\
                        .then_inc(h_l.sem, 1)
            if ahead:
                for m in range(4):
                    pool.wait_ge(qk_h.sem, qk_h.after(n + 1, m + 1))
                    if m == 0:
                        for s in heads_in:
                            pool.wait_ge(s.sem, s.after(n))
                    width = GT if m % 2 == 0 else GB * S
                    pool.tensor_tensor(QK[1][:, m, 0:width], qk32[:, m % 2, 0:width], QK[0][:, m, 0:width],
                                       ALU.subtract).then_inc(qk_l.sem, 1)

        all_bodies(pool, body)

    block_ctx.close()


def experts(nc, sb, sem, banks, shared, dram, out):
    x, weight, weight_ws = shared["x"], shared["expert_weight"], shared["expert_weight_ws"]
    HB, YB = banks[0:4], banks[4:8]

    WC = KD * F + KF * D
    w_raw = [sb(f"e_raw{i}", [P, KD * F], F32) for i in range(2)]
    w_half = [[sb(f"e_half{i}_{h}", [P, WC], F16) for h in range(2)] for i in range(2)]
    part = (slice(0, KD * F), slice(KD * F, WC))
    assert KD * F == KF * D
    w1 = [[w[:, part[0]].rearrange("p (k n) -> p k n", k=KD) for w in pair] for pair in w_half]
    w2 = [[w[:, part[1]].rearrange("p (k n) -> p k n", k=KF) for w in pair] for pair in w_half]
    b1_all = sb("e_b1_all", [P, E, KF], F32)
    b1 = [sb(f"e_b1_{i}", [P, KF], F32) for i in range(2)]
    b2 = sb("e_b2", [P, E, D], F32)
    xT = [sb(f"e_xT{h}", [P, KD, N_TOK], F16) for h in range(2)]
    h32 = sb("e_h32", [P, 2, GT], F32)
    hT = [[sb(f"e_hT{i}_{h}", [P, KF, GT], F16) for h in range(2)] for i in range(2)]
    z = sb("e_z", [P, TT, D], F32)
    norm_buf = NormBuffers(sb, "e_norm", shared["dve_gate"])

    def sig(name, per, unit=1):
        return Signal(sem("e_" + name), per, unit)

    s_const, s_xT = sem("e_const"), sem("e_xT_in")
    raw_in = [sig(f"raw_in{i}", 1, 16) for i in range(2)]
    w_hi, w_lo, b1_in = [sig(f"w_hi{i}", 1) for i in range(2)], [sig(f"w_lo{i}", 1) for i in range(2)], sig("b1_in", 1)
    H_ps, h_f, h_h, h_l = sig("H_ps", KF), sig("h_f", KF), sig("h_h", KF), sig("h_l", KF)
    Y_ps, bias_x, y_x = sig("Y_ps", TT), sig("bias_x", TT), sig("y_x", TT)
    steps, z_in, z_out = sig("steps", NORM_STEPS), sig("z_in", TT), sig("z_out", 1, 16)

    def all_rounds(eng, step):
        def expert(e, parity, last):
            with eng.Fori(0, NG // 2 - 1) as i:
                step(e, 2 * i + 1, 1, parity, False, last)
                step(e, 2 * i + 2, 0, parity, False, last)
            step(e, NG - 1, 1, parity, False, last)

        step(0, 0, 0, 0, True, False)
        with eng.Fori(0, E // 2 - 1) as i:
            e = 2 * i
            expert(e, 0, False)
            step(e + 1, 0, 0, 1, False, False)
            expert(e + 1, 1, False)
            step(e + 2, 0, 0, 0, False, False)
        expert(E - 2, 0, False)
        step(E - 1, 0, 0, 1, False, True)
        expert(E - 1, 1, True)
        step(E - 1, NG, 0, 1, False, True)

    def is_number(v, *values):
        return isinstance(v, int) and v in values

    block_ctx = ExitStack()
    block = block_ctx.enter_context(nc.Block())

    @block.sync
    def _(sp):
        for s in (*raw_in, z_out):
            sp.sem_inc(s.sem, s.credit())

        def load_expert(e):
            for i in range(2):
                sp.wait_ge(w_hi[i].sem, w_hi[i].after(e - 1))
                sp.wait_ge(w_lo[i].sem, w_lo[i].after(e - 1))
                sp.dma_start(w_raw[i][:, :], dram["expert_weights"][bass.ds(e, 1), :, part[i]]
                             .rearrange("a p n -> (a p) n")).then_inc(raw_in[i].sem, 16)

        load_expert(0)
        for half in range(2):
            sp.dma_start(xT[half][:, :, :], dram["xT_halves"][half]).then_inc(s_xT, 16)
        sp.dma_start(b1_all[:, :, :], dram["expert_b1"]).then_inc(s_const, 16)
        sp.dma_start(b2[:, :, :], dram["expert_b2"].partition_broadcast(P).rearrange("p (e d) -> p e d", e=E))\
          .then_inc(s_const, 16)
        with sp.Fori(1, E) as e:
            load_expert(e)
        rows = out.rearrange("b t d -> (b t) d")
        with sp.Fori(0, NG) as g:
            sp.wait_ge(z_in.sem, z_in.after(g))
            sp.dma_start(rows[bass.ds(g * GT, GT)].rearrange("(t p) d -> p t d", p=P), z[:, :, :])\
              .then_inc(z_out.sem, 16)
        sp.wait_ge(z_out.sem, z_out.after(NG - 1))

    @block.tensor
    def _(pe):
        for s in (H_ps, Y_ps):
            pe.sem_inc(s.sem, s.credit())
        pe.wait_ge(s_xT, 16 * 2)

        def step(e, g, odd, parity, first, last):
            r = e * NG + g
            before = parity if not is_number(g, 0) else 1 - parity
            for m in range(KF):
                if not is_number(g, NG):
                    if is_number(g, 0) and m == 0:
                        pe.wait_ge(w_hi[0].sem, w_hi[0].after(e))
                        pe.wait_ge(w_lo[0].sem, w_lo[0].after(e))
                    pe.wait_ge(h_f.sem, h_f.after(r, m - 3) if m >= 4 else h_f.after(r - 1, KF - 3 + m))
                    split_matmuls(pe, HB[m % 4][:, :], lambda h, k: w1[parity][h][:, k, m * P:(m + 1) * P],
                                  lambda h, k: xT[h][:, k, bass.ds(g * GT, GT)], KD).then_inc(H_ps.sem, 1)
                if not first and m % 2 == 1:
                    t = m // 2
                    if t == 0:
                        if is_number(g, 1) or not isinstance(g, int):
                            pe.wait_ge(w_hi[1].sem, w_hi[1].after(e))
                            pe.wait_ge(w_lo[1].sem, w_lo[1].after(e))
                        pe.wait_ge(h_h.sem, h_h.after(r - 1))
                        pe.wait_ge(h_l.sem, h_l.after(r - 1))
                    pe.wait_ge(y_x.sem, y_x.after(r - 2, t + 1))
                    hidden = hT[1 - odd]
                    split_matmuls(pe, YB[t][:, 0:D], lambda h, k: hidden[h][:, k, t * P:(t + 1) * P],
                                  lambda h, k: w2[before][h][:, k, :], KF).then_inc(Y_ps.sem, 1)

        all_rounds(pe, step)

    @block.scalar
    def _(act):
        for s in (*w_hi, h_f):
            act.sem_inc(s.sem, s.credit())

        def split(e, parity, i):
            act.wait_ge(raw_in[i].sem, raw_in[i].after(e))
            if not is_number(e, 0):
                ps = (H_ps, Y_ps)[i]
                act.wait_ge(ps.sem, ps.after((e - 1) * NG - 1))
            act.wait_ge(w_lo[i].sem, w_lo[i].after(e - 1))
            act.activation(w_half[parity][0][:, part[i]], w_raw[i][:, :], ACT.Copy, scale=WS).then_inc(w_hi[i].sem, 1)

        split(0, 0, 0)
        split(0, 0, 1)

        def step(e, g, odd, parity, first, last):
            if is_number(g, NG):
                return
            r = e * NG + g
            if is_number(g, 0):
                act.wait_ge(b1_in.sem, b1_in.after(e))
            for m in range(KF):
                act.wait_ge(H_ps.sem, H_ps.after(r, m + 1))
                for s in (h_h, h_l):
                    act.wait_ge(s.sem, s.after(r, m - 1) if m >= 2 else s.after(r - 1, KF - 1 + m))
                act.activation(h32[:, m % 2, :], HB[m % 4][:, :], ACT.Gelu, bias=b1[parity][:, m:m + 1],
                               scale=1.0 / WS).then_inc(h_f.sem, 1)
            if is_number(g, 0, NG - 1) and not last:
                split(e + 1, 1 - parity, 0 if is_number(g, 0) else 1)

        all_rounds(act, step)

    @block.vector
    def _(dve):
        for s in (*w_lo, b1_in, h_h, bias_x, y_x, steps, z_in):
            dve.sem_inc(s.sem, s.credit())
        dve.wait_ge(s_const, 16 * 2)

        def split(e, parity, i):
            if i == 0:
                if not is_number(e, 0):
                    dve.wait_ge(h_f.sem, h_f.after((e - 1) * NG - 1))
                dve.tensor_copy(b1[parity][:, :].unsqueeze(1), b1_all[:, bass.ds(e, 1), :]).then_inc(b1_in.sem, 1)
            dve.wait_ge(w_hi[i].sem, w_hi[i].after(e))
            dve.scalar_tensor_tensor(w_half[parity][1][:, part[i]], w_raw[i][:, :], WS,
                                     w_half[parity][0][:, part[i]], ALU.mult, ALU.subtract).then_inc(w_lo[i].sem, 1)

        split(0, 0, 0)
        split(0, 0, 1)

        def step(e, g, odd, parity, first, last):
            r = e * NG + g
            expert = e - 1 if is_number(g, 0) else e
            group = NG - 1 if is_number(g, 0) else g - 1
            if not first:
                dve.wait_ge(y_x.sem, y_x.after(r - 2))
                for t in range(TT):
                    n = group * TT + t
                    dve.scalar_tensor_tensor(x[:, bass.ds(n, 1), :], b2[:, bass.ds(expert, 1), :],
                                             weight[:, bass.ds(expert * (N_TOK // P) + n, 1)],
                                             x[:, bass.ds(n, 1), :], ALU.mult, ALU.add).then_inc(bias_x.sem, 1)
            for m in range(KF):
                if not is_number(g, NG):
                    dve.wait_ge(h_f.sem, h_f.after(r, m + 1))
                    if m == 0:
                        dve.wait_ge(Y_ps.sem, Y_ps.after(r - 2))
                    dve.tensor_copy(hT[odd][0][:, m, :], h32[:, m % 2, :]).then_inc(h_h.sem, 1)
                if not first and m % 2 == 1:
                    t = m // 2
                    n = group * TT + t
                    if t == 0:
                        dve.wait_ge(bias_x.sem, bias_x.after(r - 1))
                    dve.wait_ge(Y_ps.sem, Y_ps.after(r - 1, t + 1))
                    dve.scalar_tensor_tensor(x[:, bass.ds(n, 1), :], YB[t][:, 0:D].unsqueeze(1),
                                             weight_ws[:, bass.ds(expert * (N_TOK // P) + n, 1)],
                                             x[:, bass.ds(n, 1), :], ALU.mult, ALU.add).then_inc(y_x.sem, 1)
            if is_number(g, 0, NG - 1) and not last:
                split(e + 1, 1 - parity, 0 if is_number(g, 0) else 1)
            if last and not is_number(g, 0):
                dve.wait_ge(y_x.sem, y_x.after(r - 1))
                dve.wait_ge(z_out.sem, z_out.after(group - 1))
                layer_norm(dve, lambda t: x[:, bass.ds(group * TT + t, 1), :], lambda t: z[:, t:t + 1, :], norm_buf,
                           steps.sem, lambda k: steps.after(group, k), z_in.sem)

        all_rounds(dve, step)

    @block.gpsimd
    def _(pool):
        pool.sem_inc(h_l.sem, h_l.credit())

        def step(e, g, odd, parity, first, last):
            if is_number(g, NG):
                return
            r = e * NG + g
            for m in range(KF):
                pool.wait_ge(h_h.sem, h_h.after(r, m + 1))
                if m == 0:
                    pool.wait_ge(Y_ps.sem, Y_ps.after(r - 2))
                low = hT[odd][1][:, m, :]
                pool.tensor_tensor(low, h32[:, m % 2, :], hT[odd][0][:, m, :], ALU.subtract)\
                    .then_inc(h_l.sem, 1)

        all_rounds(pool, step)

    block_ctx.close()


def build(nc, dram, out):
    with ExitStack() as ctx:
        def sem(name):
            return ctx.enter_context(nc.semaphore(name))

        def sb(name, shape, dt):
            return ctx.enter_context(nc.sbuf_tensor(name, shape, dt))

        banks = [ctx.enter_context(nc.psum_tensor(f"bank{i}", [P, 512], F32)) for i in range(8)]
        psum = {"W": banks[0:3], "M": banks[3:5], "S": banks[5:7], "O": banks[7]}
        x = sb("x", [P, N_TOK // P, D], F32)
        ident = sb("ident", [P, P], F32)
        weight, weight_ws = (sb(name, [P, E * N_TOK // P], F32) for name in ("expert_weight", "expert_weight_ws"))
        shared = {"x": x, "ident": ident, "expert_weight": weight, "expert_weight_ws": weight_ws,
                  "dve_gate": sem("dve_gate"), "sp_gate": sem("sp_gate")}
        dram = {**dram, "xT_halves": nc.dram_tensor("xT_halves", (2, P, KD, N_TOK), F16, kind="Internal").ap()}
        with ExitStack() as att:
            def sa(name, shape, dt):
                return att.enter_context(nc.sbuf_tensor(name, shape, dt))

            shared["QS"] = sa("QS", [P, H, GT], F16)
            shared["KS"] = sa("KS", [P, H, GT], F16)
            shared["VS"] = sa("VS", [P, TT, H, 2 * HD], F32)
            shared["QK"] = [sa(f"QK{h}", [P, 4, GT], F16) for h in range(2)]
            shared["qk32"] = sa("qk32", [P, 2, GT], F32)
            shared["mx"] = [sa(f"mx{i}", [P, TT, C], F32) for i in range(2)]
            shared["mrow"] = [sa(f"mrow{i}", [C, GT], F16) for i in range(2)]
            shared["PR"] = [sa(f"PR{i}", [P, 6, GT], F32) for i in range(2)]
            shared["OTs"] = sa("OTs", [P, C, GT], F32)
            shared["On"] = sa("On", [P, TT, D], F32)
            shared["oT"] = [sa(f"oT{h}", [P, KD, GT], F16) for h in range(2)]
            shared["rden"] = sa("rden", [P, TT, H], F32)
            with ExitStack() as own:
                decoder(nc, lambda *a: own.enter_context(nc.sbuf_tensor(*a)), sem, psum, shared, dram)
            with ExitStack() as own:
                cross(nc, lambda *a: own.enter_context(nc.sbuf_tensor(*a)), sem, psum, shared, dram)
        with ExitStack() as own:
            experts(nc, lambda *a: own.enter_context(nc.sbuf_tensor(*a)), sem, banks, shared, dram, out)


def constants():
    import numpy as np

    slopes = (2.0 ** (-0.5)) ** np.arange(1, H + 1)
    alibi = (slopes.astype(np.float32)[:, None] * (np.arange(GT) % T)[None]).astype(np.float32)
    high = alibi.astype(np.float16)
    low = (alibi - high.astype(np.float32)).astype(np.float16)
    after = np.triu(np.ones((P, P), np.float32), 1) * -1e38
    return {
        "ident": np.eye(P, dtype=np.float32), "masks": np.concatenate([after, after.T], 1),
        "ones2": np.ones((2, H, GT), np.float16), "alibi": np.stack([high, low]),
        "zeros2": np.zeros((2, H, GT), np.float16),
    }


def laid_out(inputs):
    import numpy as np

    f = {k.replace("L0_", ""): np.asarray(v) for k, v in inputs.items()}

    def stationary(w):
        return w.reshape(-1, P, w.shape[1]).transpose(1, 0, 2).reshape(P, -1)

    def columns(b):
        return b.reshape(-1, P).T

    order = np.concatenate([(i * H + 8 * m + np.arange(8)[None]) * HD + np.arange(HD)[:, None]
                            for m in range(2) for i in range(2)]).ravel()

    weights = np.stack([np.concatenate([
        stationary(f["attn_in_proj_w"][l][np.append(order, np.arange(2 * D, 3 * D))].T), stationary(f["attn_out_proj_w"][l].T),
        stationary(f["attn_ffn1_w"][l].T), stationary(f["attn_ffn2_w"][l].T)], 1) for l in range(L)])
    cols = np.stack([np.concatenate([
        columns(f["attn_in_proj_b"][l][order]), columns(f["attn_ffn1_b"][l]), columns(f["attn_ln1_w"][l]),
        columns(f["attn_ln1_b"][l]), columns(f["attn_ln2_w"][l]), columns(f["attn_ln2_b"][l])], 1) for l in range(L)])
    rows = np.stack([f["attn_in_proj_b"][:, 2 * D:], f["attn_out_proj_b"], f["attn_ffn2_b"]], 1)
    wide = [(0, D - E_CTX), (0, 0)]
    heads = order.reshape(4, P)
    cross_weights = np.concatenate([
        stationary(f["xattn_Wq"][:, heads[0::2].ravel() % D]), stationary(np.pad(f["xattn_Wk"], wide)[:, heads[1::2].ravel() % D]),
        stationary(np.pad(f["xattn_Wv"], wide)), stationary(f["xattn_W1"]), stationary(f["xattn_W2"]),
        stationary(f["ffn_Wr"])], 1)
    both = np.concatenate([f["xattn_bq"], f["xattn_bk"]])
    cross_cols = np.concatenate([columns(both[order]), columns(f["xattn_b1"])], 1)
    cross_rows = np.concatenate([f[k] for k in ("attn_final_w", "attn_final_b", "xattn_bv", "xattn_b2", "ffn_br")])
    ctx = np.pad(f["ctx_768"].reshape(B * S, E_CTX).T, wide).reshape(KD, P, B * S).transpose(1, 0, 2)
    expert_weights = np.stack([np.concatenate([stationary(f["ffn_W1"][e]), stationary(f["ffn_W2"][e])], 1)
                               for e in range(E)])
    expert_b1 = f["ffn_b1"].reshape(E, KF, P).transpose(2, 0, 1)
    return {"x": f["x"].reshape(N_TOK, D), "weights": weights, "cols": cols, "rows": rows,
            "cross_weights": cross_weights, "cross_cols": cross_cols, "cross_rows": cross_rows, "ctx": ctx,
            "expert_weights": expert_weights, "expert_b1": expert_b1, "expert_b2": f["ffn_b2"].ravel()}


def kernel(**inputs):
    import numpy as np
    import concourse.bacc as bacc
    from concourse.bass_utils import run_bass_kernel_spmd

    nc = bacc.Bacc("TRN2", target_bir_lowering=False, num_devices=1)
    arrays, dram = {}, {}
    for name, a in {**laid_out(inputs), **constants()}.items():
        a = np.ascontiguousarray(a)
        arrays[f"in_{name}"] = a
        dram[name] = nc.dram_tensor(f"in_{name}", a.shape, mybir.dt.from_np(a.dtype), kind="ExternalInput").ap()
    out = nc.dram_tensor("out", (B, T, D), F32, kind="ExternalOutput").ap()
    build(nc, dram, out)
    r = run_bass_kernel_spmd(nc, [arrays], core_ids=[0])
    return r.results[0]["out"]
```

```python
from contextlib import ExitStack

import concourse.bass as bass
from concourse import mybir

ALU = mybir.AluOpType
ACT = mybir.ActivationFunctionType
AX = mybir.AxisListType
F32 = mybir.dt.float32
F16 = mybir.dt.float16
BF16 = mybir.dt.bfloat16

P = 128
D = 256
KD = D // P
B, T = 16, 256
N_TOK = B * T
GT = 512
NG = N_TOK // GT
TT = GT // P
GB = GT // T
L = 4
H, HD = 16, 16
F = 1024
KF = F // P
C = 4
S, E_CTX = 120, 192
F2 = 512
KF2 = F2 // P
E = 8
EPS = 1e-5
WS = 64.0

R_LO, R_HI2, R_POS, R_MAX = 16, 32, 48, 96


class Signal:

    def __init__(self, sem, per, unit=1):
        self.sem, self.per, self.unit = sem, per, unit

    def credit(self):
        return self.per * self.unit

    def after(self, n, k=None):
        k = self.per if k is None else k
        return n * (self.per * self.unit) + (self.per + k) * self.unit


def part_from_wait(engine, gate):
    engine.sem_inc(gate, 1)


def split_matmuls(pe, out, stat, mov, tiles, hold_open=False):
    last = None
    for k in range(tiles):
        for n, (a, b) in enumerate(((0, 0), (0, 1), (1, 0))):
            last = pe.matmul(out, stat(a, k), mov(b, k), start=(k == 0 and n == 0),
                             stop=(k == tiles - 1 and n == 2))
    return last


NEWTON = 3
NORM_STEPS = 2 * TT + 3 + 3 * NEWTON


class NormBuffers:

    def __init__(self, sb, name, gate):
        self.gate = gate
        self.stats = sb(f"{name}_stats", [P, TT, 6], F32)
        self.mean_var = sb(f"{name}_mean_var", [P, TT, 2], F32)
        self.var = sb(f"{name}_var", [P, TT], F32)
        self.half = sb(f"{name}_half", [P, TT], mybir.dt.int32)
        self.root = [sb(f"{name}_root{i}", [P, TT], F32) for i in range(2)]
        self.square = sb(f"{name}_square", [P, TT], F32)
        self.slope = sb(f"{name}_slope", [P, TT], F32)


def norm_stats(dve, x_tiles, buf, steps, tiles=range(TT)):
    part_from_wait(dve, buf.gate)
    for t in tiles:
        dve.bn_stats(buf.stats[:, t, :], x_tiles(t)).then_inc(steps, 1)


def layer_norm(dve, x_tiles, z_tiles, buf, steps, value, done, with_stats=True):
    if with_stats:
        norm_stats(dve, x_tiles, buf, steps)
    dve.wait_ge(steps, value(TT))
    part_from_wait(dve, buf.gate)
    for t in range(TT):
        dve.bn_aggr(buf.mean_var[:, t, :], buf.stats[:, t, :]).then_inc(steps, 1)
    k = 2 * TT
    dve.wait_ge(steps, value(k))
    dve.tensor_scalar(buf.var[:, :], buf.mean_var[:, :, 1], EPS, None, ALU.add).then_inc(steps, 1)
    dve.wait_ge(steps, value(k + 1))
    dve.tensor_scalar(buf.half[:, :], buf.var[:, :].bitcast(mybir.dt.int32), 1, None,
                      ALU.logical_shift_right).then_inc(steps, 1)
    dve.wait_ge(steps, value(k + 2))
    dve.tensor_scalar(buf.root[0][:, :].bitcast(mybir.dt.int32), buf.half[:, :], -1.0, float(0x5F3759DF),
                      ALU.mult, ALU.add).then_inc(steps, 1)
    k += 3
    for i in range(NEWTON):
        y, new = buf.root[i % 2], buf.root[(i + 1) % 2]
        dve.wait_ge(steps, value(k))
        dve.tensor_tensor(buf.square[:, :], y[:, :], y[:, :], ALU.mult).then_inc(steps, 1)
        dve.wait_ge(steps, value(k + 1))
        dve.scalar_tensor_tensor(buf.slope[:, :], buf.square[:, :], -0.5, buf.var[:, :], ALU.mult, ALU.mult)\
           .then_inc(steps, 1)
        dve.wait_ge(steps, value(k + 2))
        dve.scalar_tensor_tensor(new[:, :], buf.slope[:, :], 1.5, y[:, :], ALU.add, ALU.mult).then_inc(steps, 1)
        k += 3
    rstd = buf.root[NEWTON % 2]
    dve.wait_ge(steps, value(k))
    for t in range(TT):
        dve.tensor_scalar(z_tiles(t), x_tiles(t), buf.mean_var[:, t, 0:1], rstd[:, t:t + 1],
                          ALU.subtract, ALU.mult).then_inc(done, 1)


def decoder(nc, sb, sem, psum, shared, dram):
    x, ident, QS, KS, VS = shared["x"], shared["ident"], shared["QS"], shared["KS"], shared["VS"]
    W, M, SC, O = psum["W"], psum["M"], psum["S"], psum["O"]

    CH = 512
    PARTS = {"qkv": range(0, 3), "o": range(3, 4), "f1": range(4, 8), "f2": range(8, 12)}
    NCH = 12
    assert KD * (3 * D + D + F) + KF * D == CH * NCH and KD * 3 * D == 3 * CH and KD * F == 4 * CH
    NRAW = 3
    w_raw = [sb(f"w_raw{i}", [P, CH], F32) for i in range(NRAW)]
    w_half = [sb(f"w_half{i}", [P, CH * NCH], F16) for i in range(2)]
    at = 0
    views = {}
    for name, k, cols in (("qkv", KD, 3 * D), ("o", KD, D), ("f1", KD, F), ("f2", KF, D)):
        views[name] = [w[:, at:at + k * cols].rearrange("p (k n) -> p k n", k=k) for w in w_half]
        at += k * cols
    rows = sb("rows", [P, 3, D], F32)
    cols = sb("cols", [P, 20], F32)
    AHEAD_COLS = 8
    qbias = sb("qbias", [P, 2], F32)
    COL = {"qkb": 0, "ln1w": 4, "ln1b": 6, "ln2w": 8, "ln2b": 10, "f1b": 12}

    ident_b = sb("ident_b", [P, P], BF16)
    mask_q = sb("mask_q", [P, P], BF16)
    mask_k = sb("mask_k", [P, P], BF16)

    z = [sb(f"z{i}", [P, TT, D], F32) for i in range(2)]
    xT32 = [sb(f"xT32_{i}", [P, KD, GT], F32) for i in range(2)]
    xT = [[sb(f"xT{i}_{h}", [P, KD, GT], F16) for h in range(2)] for i in range(2)]
    norm_buf = [NormBuffers(sb, f"norm{i + 1}", shared["dve_gate"]) for i in range(2)]
    QK = shared["QK"]
    qk32 = shared["qk32"]
    mx, mrow, PR, OTs, On, oT = (shared[k] for k in ("mx", "mrow", "PR", "OTs", "On", "oT"))
    rden = shared["rden"]
    h32 = sb("h32", [P, 2, GT], F32)
    hT = [sb(f"hT_{h}", [P, KF, GT], F16) for h in range(2)]

    def sig(name, per, unit=1):
        return Signal(sem("d_" + name), per, unit)

    s_const, s_rows, s_x_first, s_x = sem("d_const"), sem("d_rows_in"), sem("d_x_first"), sem("d_x_in")
    s_init, s_masks = sem("d_init"), sem("d_masks")
    raw_in, w_hi, w_lo = [sig(f"raw_in{i}", NCH // NRAW, 16) for i in range(NRAW)], sig("w_hi", NCH), sig("w_lo", NCH)
    ahead_in, qb_ready, row_in, back_in = sig("ahead_in", 1, 16), sig("qb_ready", 1), \
        [sig(f"row_in{i}", 1, 16) for i in range(3)], sig("back_in", 1, 16)
    ln1_steps, z1 = sig("ln1_steps", NORM_STEPS), sig("z1", TT)
    T1_ps, xh1, xf1, xl1 = sig("T1_ps", KD), sig("xh1", KD), sig("xf1", KD), sig("xl1", KD)
    V_ps, v_f, v_in = sig("V_ps", 2), sig("v_f", TT), sig("v_in", TT)
    QK_ps, qk_h, qk_f, qk_l = sig("QK_ps", 4), sig("qk_h", 4), sig("qk_f", 4), sig("qk_l", 4)
    heads_in = [sig(f"heads_in{m}", 6, 16) for m in range(2)]
    M_ps, mx_in = sig("M_ps", 6 * C), sig("mx_in", 6 * C)
    MT_ps, mrow_in, m_in = sig("MT_ps", C), sig("mrow_in", C), [sig(f"m_in{i}", C // 2, 16) for i in range(2)]
    S_ps, p_in, O_ps, o_in = sig("S_ps", 6 * C), sig("p_in", 6 * C), sig("O_ps", C), sig("o_in", C)
    OS_ps, rd_in, on_in = sig("OS_ps", TT), sig("rd_in", TT), sig("on_in", TT)
    OT_ps, oh, ol = sig("OT_ps", KD), sig("oh", KD), sig("ol", KD)
    OP_ps, xo = sig("OP_ps", 2), sig("xo", 2)
    xb1, xb2 = sig("xb1", 1), sig("xb2", 1)
    ln2_steps, z2 = sig("ln2_steps", NORM_STEPS), sig("z2", TT)
    T2_ps, xh2, xf2, xl2 = sig("T2_ps", KD), sig("xh2", KD), sig("xf2", KD), sig("xl2", KD)
    H_ps, h_f, h_h, h_l = sig("H_ps", KF), sig("h_f", KF), sig("h_h", KF), sig("h_l", KF)
    Y_ps, y_x = sig("Y_ps", 2), sig("y_x", 2)

    R = len(W)
    READERS = {
        "T1": [(xf1, 1)], "V": [(v_f, 2)], "QK": [(qk_f, 1)], "MT": [(mrow_in, 1)],
        "OS": [(on_in, 1)], "OT": [(oh, 1), (ol, 1)], "OP": [(xo, 1)], "T2": [(xf2, 1)],
        "H": [(h_f, 1)], "Y": [(y_x, 1)],
    }
    ROUND = {"T1": 1, "QK": 1, "V": 0, "MT": 0} | {stage: -1 for stage in ("OS", "OT", "OP", "T2", "H", "Y")}

    def tiles_of(ahead, front, back):
        a, f, b = (lambda *x: list(x) if ahead else []), (lambda *x: list(x) if front else []), \
                  (lambda *x: list(x) if back else [])
        two, four = range(2), range(4)
        out = f(*(("V", k) for k in two)) + b(*(("OS", k) for k in four)) + b(*(("OT", k) for k in two))
        out += f(("MT", 0)) + a(*(("T1", k) for k in two)) + b(*(("OP", k) for k in two)) + f(("MT", 1))
        out += a(*(("QK", k) for k in four)) + f(("MT", 2)) + b(*(("T2", k) for k in two)) + f(("MT", 3))
        out += b(*(("H", m) for m in range(KF)), *(("Y", k) for k in two))
        return out + [None] * (-len(out) % R)

    PRE, HEAD, STEADY = tiles_of(True, False, False), tiles_of(True, True, False), tiles_of(True, True, True)
    LAST, TAIL = tiles_of(False, True, True), tiles_of(False, False, True)
    BEFORE = {id(PRE): [], id(HEAD): [(PRE, -1)], id(STEADY): [(HEAD, -1), (STEADY, -1)],
              id(LAST): [(STEADY, -1)], id(TAIL): [(LAST, -1)]}

    def free_tile(pe, kind, n, tile, inputs=()):
        pos = kind.index(tile)
        need = {signal: (-1, signal.per) for signal in inputs}
        for other, m in [(kind, 0)] if pos >= R else BEFORE[id(kind)]:
            q = pos - R if pos >= R else len(other) - R + pos
            while other[q] is None:
                q -= R
            stage, k = other[q]
            for signal, each in READERS[stage]:
                at = (m + ROUND[stage], (k + 1) * each)
                need[signal] = max(need.get(signal, at), at)
        for signal, (m, raises) in need.items():
            pe.wait_ge(signal.sem, signal.after(n + m, raises))
        return W[pos % R]

    def all_bodies(eng, body):
        body(PRE, -1, 0, -1, True, False, False, 0)
        body(HEAD, 0, 0, 0, True, True, False, 0)
        with eng.Fori(0, L - 1) as l:
            with eng.Fori(1, NG - 2) as g:
                body(STEADY, l * NG + g, l, g, True, True, True, 0)
            body(STEADY, l * NG + NG - 2, l, NG - 2, True, True, True, 0)
            body(STEADY, l * NG + NG - 1, l, NG - 1, True, True, True, 1)
            body(STEADY, l * NG + NG, l + 1, 0, True, True, True, 2)
        l = L - 1
        with eng.Fori(1, NG - 2) as g:
            body(STEADY, l * NG + g, l, g, True, True, True, 0)
        body(STEADY, l * NG + NG - 2, l, NG - 2, True, True, True, 0)
        body(LAST, l * NG + NG - 1, l, NG - 1, False, True, True, 0)
        body(TAIL, l * NG + NG, l, NG, False, False, True, 0)

    block_ctx = ExitStack()
    block = block_ctx.enter_context(nc.Block())

    @block.sync
    def _(sp):
        for s in (*raw_in, ahead_in, *row_in, back_in, *heads_in, *m_in):
            sp.sem_inc(s.sem, s.credit())
        xd = dram["x"].rearrange("(n p) d -> p n d", p=P)
        sp.dma_start(x[:, 0:TT, :], xd[:, 0:TT]).then_inc(s_x_first, 16)
        sp.dma_start(ident[:, :], dram["ident"]).then_inc(s_const, 16)
        sp.dma_start(z[1][:, 0, :], dram["masks"]).then_inc(s_const, 16)

        def heads(n, m):
            sp.wait_ge(S_ps.sem, S_ps.after(n - 1, 12 * (m + 1)))
            part_from_wait(sp, shared["sp_gate"])
            sp.wait_ge(qk_h.sem, qk_h.after(n, 2 * m + 2))
            sp.wait_ge(qk_l.sem, qk_l.after(n, 2 * m + 2))
            for tile, dst, half_rows in ((2 * m, QS, ((0, 0), (R_HI2, 0), (R_LO, 1))),
                                         (2 * m + 1, KS, ((0, 0), (R_LO, 0), (R_HI2, 1)))):
                for row, half in half_rows:
                    sp.dma_start(dst[row:row + HD, 8 * m:8 * m + 8, :], QK[half][:, tile, :])\
                      .then_inc(heads_in[m].sem, 16)

        def maximum(n, c):
            sp.wait_ge(mrow_in.sem, mrow_in.after(n, c + 1))
            sp.dma_start(QS[R_MAX:R_MAX + 1, C * c:C * c + C, :], mrow[c % 2][0:C, :])\
              .then_inc(m_in[c % 2].sem, 16)

        def raw(l, chunks):
            for i in chunks:
                before = (l, i - NRAW + 1) if i >= NRAW else (l - 1, NCH - NRAW + i + 1)
                sp.wait_ge(w_hi.sem, w_hi.after(*before))
                part_from_wait(sp, shared["sp_gate"])
                sp.wait_ge(w_lo.sem, w_lo.after(*before))
                part_from_wait(sp, shared["sp_gate"])
                sp.dma_start(w_raw[i % NRAW][:, :], dram["weights"][bass.ds(l, 1), :, i * CH:(i + 1) * CH]
                             .rearrange("a p n -> (a p) n")).then_inc(raw_in[i % NRAW].sem, 16)

        def columns(l, part, done):
            sp.dma_start(cols[:, part], dram["cols"][bass.ds(l, 1), :, part].rearrange("a p c -> (a p) c"))\
              .then_inc(done.sem, 16)

        def ahead_columns(l):
            sp.wait_ge(qk_f.sem, qk_f.after(l * NG - 1))
            part_from_wait(sp, shared["sp_gate"])
            sp.wait_ge(qb_ready.sem, qb_ready.after(l - 1))
            part_from_wait(sp, shared["sp_gate"])
            columns(l, slice(0, AHEAD_COLS), ahead_in)

        def row(l, i):
            last = (v_in, xb1, xb2)[i]
            sp.wait_ge(last.sem, last.after(l * NG - 1))
            part_from_wait(sp, shared["sp_gate"])
            sp.dma_start(rows[:, i, :], dram["rows"][bass.ds(l, 1), i, :].rearrange("a n -> (a n)")
                         .partition_broadcast(P)).then_inc(row_in[i].sem, 16)

        def back_columns(l):
            sp.wait_ge(h_f.sem, h_f.after(l * NG - 1))
            part_from_wait(sp, shared["sp_gate"])
            columns(l, slice(AHEAD_COLS, 20), back_in)

        def body(kind, n, l, g, ahead, front, back, swap):
            if kind is PRE:
                ahead_columns(0)
                raw(0, range(NRAW))
                for i in range(3):
                    row(0, i)
                back_columns(0)
                sp.dma_start(x[:, TT:, :], xd[:, TT:]).then_inc(s_x, 16)
                sp.wait_ge(s_init, 3)
                sp.dma_start(QS[R_POS:R_POS + 2, :, :], dram["ones2"]).then_inc(s_rows, 16)
                sp.dma_start(KS[R_POS:R_POS + 2, :, :], dram["alibi"]).then_inc(s_rows, 16)
                sp.dma_start(KS[R_MAX:R_MAX + 1, :, :], dram["ones2"][0:1]).then_inc(s_rows, 16)
            if swap == 1:
                ahead_columns(l + 1)
                raw(l + 1, range(NRAW))
            if front:
                maximum(n, 0)
                maximum(n, 1)
                if swap == 1:
                    raw(l + 1, range(NRAW, 2 * NRAW))
                maximum(n, 2)
            if ahead:
                heads(n + 1, 0)
            if front:
                maximum(n, 3)
            if ahead:
                heads(n + 1, 1)
            if kind is PRE:
                raw(0, range(NRAW, NCH))
            if swap == 1:
                row(l + 1, 0)
                row(l + 1, 1)
            if swap == 2:
                raw(l, range(2 * NRAW, NCH))
                row(l, 2)
                back_columns(l)

        all_bodies(sp, body)

    @block.tensor
    def _(pe):
        for s in (T1_ps, V_ps, QK_ps, M_ps, MT_ps, S_ps, O_ps, OS_ps, OT_ps, OP_ps, T2_ps, H_ps, Y_ps):
            pe.sem_inc(s.sem, s.credit())
        pe.wait_ge(s_const, 16 * 2)

        def part_ready(part, l):
            for s in (w_hi, w_lo):
                pe.wait_ge(s.sem, s.after(l, PARTS[part].stop))

        def transpose_group(kind, n, name, ps, src, ready, ready_n):
            for k in range(KD):
                bank = free_tile(pe, kind, n, (name, k))
                pe.wait_ge(ready.sem, ready.after(ready_n))
                for t in range(TT):
                    last = pe.transpose(bank[:, t * P:(t + 1) * P], src[:, t, k * P:(k + 1) * P], ident[:, :])
                last.then_inc(ps.sem, 1)

        def values(kind, n):
            for k in range(2):
                bank = free_tile(pe, kind, n, ("V", k))
                for u in range(2):
                    t = 2 * k + u
                    last = split_matmuls(pe, bank[:, u * D:(u + 1) * D],
                                         lambda h, kk: xT[0][h][:, kk, t * P:(t + 1) * P],
                                         lambda h, kk: views["qkv"][h][:, kk, 2 * D:3 * D], KD)
                last.then_inc(V_ps.sem, 1)

        def queries_keys(kind, n):
            for m in range(4):
                bank = free_tile(pe, kind, n, ("QK", m))
                if m == 0:
                    pe.wait_ge(xh1.sem, xh1.after(n + 1))
                    pe.wait_ge(xl1.sem, xl1.after(n + 1))
                split_matmuls(pe, bank[:, :], lambda h, kk: views["qkv"][h][:, kk, m * P:(m + 1) * P],
                              lambda h, kk: xT[0][h][:, kk, :], KD).then_inc(QK_ps.sem, 1)

        def chunk_bank(banks, made, read, n, c, i):
            q = 6 * c + i
            if q >= 2:
                pe.wait_ge(read.sem, read.after(n, q - 1))
            else:
                pe.wait_ge(read.sem, read.after(n - 1, 6 * C - 1 + q))
            return banks[q % 2]

        def row_scores(n, c, chunks):
            if c % 2 == 0 and 0 in chunks:
                pe.wait_ge(heads_in[c // 2].sem, heads_in[c // 2].after(n))
            for q in chunks:
                b, i = divmod(q, 3)
                bank = chunk_bank(M, M_ps, mx_in, n, c, q)
                if i < 2:
                    for u in range(2):
                        h = C * c + 2 * i + u
                        pe.matmul(bank[:, u * T:(u + 1) * T], QS[0:R_MAX, h, b * T + P:(b + 1) * T],
                                  KS[0:R_MAX, h, b * T:(b + 1) * T], start=True, stop=False)
                        last = pe.matmul(bank[:, u * T + P:(u + 1) * T], ident_b[:, :], mask_q[:, :],
                                         start=False, stop=True)
                else:
                    for u in range(C):
                        h = C * c + u
                        pe.matmul(bank[:, u * P:(u + 1) * P], QS[0:R_MAX, h, b * T:b * T + P],
                                  KS[0:R_MAX, h, b * T:b * T + P], start=True, stop=False)
                        last = pe.matmul(bank[:, u * P:(u + 1) * P], ident_b[:, :], mask_q[:, :],
                                         start=False, stop=True)
                last.then_inc(M_ps.sem, 1)

        def turn_maxima(kind, n, c):
            bank = free_tile(pe, kind, n, ("MT", c))
            pe.wait_ge(mx_in.sem, mx_in.after(n, 6 * c + 6))
            for t in range(TT):
                last = pe.transpose(bank[0:C, t * P:(t + 1) * P], mx[c % 2][:, t, :], ident[:, :])
            last.then_inc(MT_ps.sem, 1)

        def key_scores(n, c, chunks):
            if 0 in chunks:
                pe.wait_ge(m_in[c % 2].sem, m_in[c % 2].after(n, c // 2 + 1))
            for q in chunks:
                b, i = divmod(q, 3)
                bank = chunk_bank(SC, S_ps, p_in, n, c, q)
                if i < 2:
                    for u in range(2):
                        h = C * c + 2 * i + u
                        pe.matmul(bank[:, u * T:(u + 1) * T], KS[:, h, b * T:b * T + P],
                                  QS[:, h, b * T:(b + 1) * T], start=True, stop=False)
                        last = pe.matmul(bank[:, u * T:u * T + P], ident_b[:, :], mask_k[:, :],
                                         start=False, stop=True)
                else:
                    for u in range(C):
                        h = C * c + u
                        pe.matmul(bank[:, u * P:(u + 1) * P], KS[:, h, b * T + P:(b + 1) * T],
                                  QS[:, h, b * T + P:(b + 1) * T], start=True, stop=False)
                        last = pe.matmul(bank[:, u * P:(u + 1) * P], ident_b[:, :], mask_k[:, :],
                                         start=False, stop=True)
                last.then_inc(S_ps.sem, 1)

        def attend(n, c):
            if c == 0:
                pe.wait_ge(v_in.sem, v_in.after(n))
            pe.wait_ge(p_in.sem, p_in.after(n, 6 * c + 6))
            if c == 0:
                pe.wait_ge(o_in.sem, o_in.after(n - 1))
            else:
                pe.wait_ge(o_in.sem, o_in.after(n, c))
            probs = PR[c % 2]
            for b in range(GB):
                for u in range(C):
                    pe.matmul(O[32 * u:32 * u + 32, b * T:(b + 1) * T], VS[:, 2 * b, C * c + u, :],
                              probs[:, 3 * b + u // 2, (u % 2) * T:(u % 2 + 1) * T], start=True, stop=False)
                for u in range(C):
                    last = pe.matmul(O[32 * u:32 * u + 32, b * T + P:(b + 1) * T],
                                     VS[:, 2 * b + 1, C * c + u, :],
                                     probs[:, 3 * b + 2, u * P:(u + 1) * P], start=False, stop=True)
            last.then_inc(O_ps.sem, 1)

        def turn_outputs(kind, n):
            for t in range(TT):
                bank = free_tile(pe, kind, n, ("OS", t))
                pe.wait_ge(o_in.sem, o_in.after(n - 1))
                for c in range(C):
                    last = pe.transpose(bank[:, c * P:(c + 1) * P], OTs[:, c, t * P:(t + 1) * P], ident[:, :])
                last.then_inc(OS_ps.sem, 1)

        def token_major(kind, n, name, ps, src, weight, tiles, ready):
            for k in range(2):
                bank = free_tile(pe, kind, n, (name, k))
                for u in range(2):
                    t = 2 * k + u
                    def source(h, kk):
                        if t == 0 and h == 0:
                            for s in ready:
                                pe.wait_ge(s.sem, s.after(n - 1, kk + 1))
                        return src[h][:, kk, t * P:(t + 1) * P]

                    last = split_matmuls(pe, bank[:, u * D:(u + 1) * D], source,
                                         lambda h, kk: weight[h][:, kk, :], tiles)
                last.then_inc(ps.sem, 1)

        def hidden(kind, n, m):
            bank = free_tile(pe, kind, n, ("H", m))
            if m == 0:
                pe.wait_ge(xh2.sem, xh2.after(n - 1))
                pe.wait_ge(xl2.sem, xl2.after(n - 1))
            split_matmuls(pe, bank[:, :], lambda h, kk: views["f1"][h][:, kk, m * P:(m + 1) * P],
                          lambda h, kk: xT[1][h][:, kk, :], KD).then_inc(H_ps.sem, 1)

        def body(kind, n, l, g, ahead, front, back, swap):
            def interleaved(c):
                row_scores(n, c + 1, [0])
                for q in range(6):
                    if q < 5:
                        row_scores(n, c + 1, [q + 1])
                    key_scores(n, c, [q])

            if kind is HEAD:
                pe.wait_ge(s_rows, 16 * 3)
                pe.wait_ge(s_masks, 1)
                pe.wait_ge(s_init, 3)
            if front:
                values(kind, n)
                row_scores(n, 0, range(2))
            if back:
                turn_outputs(kind, n)
            if front:
                row_scores(n, 0, [2, 3])
            if back:
                transpose_group(kind, n, "OT", OT_ps, On, on_in, n - 1)
            if front:
                row_scores(n, 0, [4, 5])
                turn_maxima(kind, n, 0)
            if ahead:
                transpose_group(kind, n, "T1", T1_ps, z[0], z1, n + 1)
            if back:
                part_ready("o", l - 1 if swap == 2 else l)
                token_major(kind, n, "OP", OP_ps, oT, views["o"], KD, (oh, ol))
            if front:
                interleaved(0)
                turn_maxima(kind, n, 1)
            if ahead:
                part_ready("qkv", l + 1 if swap == 1 else l)
                queries_keys(kind, n)
            if front:
                attend(n, 0)
                interleaved(1)
                turn_maxima(kind, n, 2)
            if back:
                transpose_group(kind, n, "T2", T2_ps, z[1], z2, n - 1)
            if front:
                attend(n, 1)
                interleaved(2)
                turn_maxima(kind, n, 3)
                attend(n, 2)
            if back:
                part_ready("f1", l - 1 if swap == 2 else l)
            for m, chunks in enumerate(([0, 1], [2, 3, 4, 5], [])):
                if back:
                    hidden(kind, n, m)
                if front:
                    key_scores(n, 3, chunks)
            if front:
                attend(n, 3)
            if back:
                for m in range(3, KF):
                    hidden(kind, n, m)
                part_ready("f2", l - 1 if swap == 2 else l)
                token_major(kind, n, "Y", Y_ps, hT, views["f2"], KF, (h_h, h_l))

        all_bodies(pe, body)

    @block.scalar
    def _(act):
        for s in (w_hi, xf1, v_f, qk_f, mrow_in, p_in, o_in, oh, xf2, h_f):
            act.sem_inc(s.sem, s.credit())

        def weights(l, part):
            last = {"qkv": V_ps, "o": OP_ps, "f1": H_ps, "f2": Y_ps}[part]
            act.wait_ge(last.sem, last.after(l * NG - 1))
            for i in PARTS[part]:
                act.wait_ge(raw_in[i % NRAW].sem, raw_in[i % NRAW].after(l, i // NRAW + 1))
                act.activation(w_half[0][:, i * CH:(i + 1) * CH], w_raw[i % NRAW][:, :], ACT.Copy, scale=WS)\
                   .then_inc(w_hi.sem, 1)

        def project(kind, n):
            for k in range(KD):
                act.wait_ge(T1_ps.sem, T1_ps.after(n, k + 1))
                if k == 0:
                    act.wait_ge(xh1.sem, xh1.after(n - 1))
                    act.wait_ge(xl1.sem, xl1.after(n - 1))
                act.activation(xT32[0][:, k, :], W[kind.index(("T1", k)) % R][:, :], ACT.Identity,
                               bias=cols[:, COL["ln1b"] + k:COL["ln1b"] + k + 1],
                               scale=cols[:, COL["ln1w"] + k:COL["ln1w"] + k + 1]).then_inc(xf1.sem, 1)

        def queries_keys(kind, n):
            for m in range(4):
                act.wait_ge(QK_ps.sem, QK_ps.after(n, m + 1))
                for s in (qk_h, qk_l):
                    act.wait_ge(s.sem, s.after(n, m - 1) if m >= 2 else s.after(n - 1, m + 3))
                query = m % 2 == 0
                bias = qbias[:, m // 2:m // 2 + 1] if query else cols[:, COL["qkb"] + m:COL["qkb"] + m + 1]
                act.activation(qk32[:, m % 2, :], W[kind.index(("QK", m)) % R][:, :], ACT.Identity, bias=bias,
                               scale=(HD ** -0.5 if query else 1.0) / WS).then_inc(qk_f.sem, 1)

        def values(kind, n):
            for t in range(TT):
                act.wait_ge(V_ps.sem, V_ps.after(n, t // 2 + 1))
                if t == 0:
                    act.wait_ge(O_ps.sem, O_ps.after(n - 1))
                bank = W[kind.index(("V", t // 2)) % R]
                act.activation(VS[:, t, :, 0:HD],
                               bank[:, (t % 2) * D:(t % 2 + 1) * D].rearrange("p (h d) -> p h d", h=H),
                               ACT.Copy, scale=1.0 / WS).then_inc(v_f.sem, 1)

        def outputs_high(kind, n):
            for k in range(KD):
                act.wait_ge(OT_ps.sem, OT_ps.after(n - 1, k + 1))
                if k == 0:
                    act.wait_ge(OP_ps.sem, OP_ps.after(n - 2))
                act.activation(oT[0][:, k, :], W[kind.index(("OT", k)) % R][:, :], ACT.Copy).then_inc(oh.sem, 1)

        def norm2(kind, n):
            for k in range(KD):
                act.wait_ge(T2_ps.sem, T2_ps.after(n - 1, k + 1))
                if k == 0:
                    act.wait_ge(xh2.sem, xh2.after(n - 2))
                    act.wait_ge(xl2.sem, xl2.after(n - 2))
                act.activation(xT32[1][:, k, :], W[kind.index(("T2", k)) % R][:, :], ACT.Identity,
                               bias=cols[:, COL["ln2b"] + k:COL["ln2b"] + k + 1],
                               scale=cols[:, COL["ln2w"] + k:COL["ln2w"] + k + 1]).then_inc(xf2.sem, 1)

        def max_row(kind, n, c):
            act.wait_ge(MT_ps.sem, MT_ps.after(n, c + 1))
            act.wait_ge(m_in[c % 2].sem, m_in[c % 2].after(n, c // 2))
            act.activation(mrow[c % 2][0:C, :], W[kind.index(("MT", c)) % R][0:C, :], ACT.Copy)\
               .then_inc(mrow_in.sem, 1)

        def gelu(kind, n, m):
            act.wait_ge(H_ps.sem, H_ps.after(n - 1, m + 1))
            for s in (h_h, h_l):
                if m >= 2:
                    act.wait_ge(s.sem, s.after(n - 1, m - 1))
                else:
                    act.wait_ge(s.sem, s.after(n - 2, KF - 1 + m))
            act.activation(h32[:, m % 2, :], W[kind.index(("H", m)) % R][:, :], ACT.Gelu,
                           bias=cols[:, COL["f1b"] + m:COL["f1b"] + m + 1], scale=1.0 / WS).then_inc(h_f.sem, 1)

        def exps(n, c):
            if c < 2:
                act.wait_ge(O_ps.sem, O_ps.after(n - 1, c + 3))
            else:
                act.wait_ge(O_ps.sem, O_ps.after(n, c - 1))
            for q in range(6):
                act.wait_ge(S_ps.sem, S_ps.after(n, 6 * c + q + 1))
                act.activation(PR[c % 2][:, q, :], SC[(6 * c + q) % 2][:, :], ACT.Exp).then_inc(p_in.sem, 1)

        def out_rows(n, c):
            act.wait_ge(O_ps.sem, O_ps.after(n, c + 1))
            if c == 0:
                act.wait_ge(OS_ps.sem, OS_ps.after(n - 1))
            act.activation(OTs[:, c, :], O[:, :], ACT.Copy).then_inc(o_in.sem, 1)

        def body(kind, n, l, g, ahead, front, back, swap):
            if kind is PRE:
                weights(0, "qkv")
            if kind is HEAD:
                for part in ("o", "f1", "f2"):
                    weights(0, part)
                act.wait_ge(back_in.sem, back_in.after(0))
                act.wait_ge(s_init, 3)
            if front:
                values(kind, n)
            if back:
                outputs_high(kind, n)
            if front:
                max_row(kind, n, 0)
            if ahead:
                if kind is PRE or swap == 1:
                    act.wait_ge(ahead_in.sem, ahead_in.after(l + swap))
                project(kind, n + 1)
            if front:
                exps(n, 0)
                max_row(kind, n, 1)
            if swap == 1:
                weights(l + 1, "qkv")
            if ahead:
                if kind is PRE or swap == 1:
                    act.wait_ge(qb_ready.sem, qb_ready.after(l + swap))
                queries_keys(kind, n + 1)
            if swap == 2:
                weights(l, "o")
            if front:
                out_rows(n, 0)
                exps(n, 1)
                max_row(kind, n, 2)
            if back:
                norm2(kind, n)
            if front:
                out_rows(n, 1)
                exps(n, 2)
                max_row(kind, n, 3)
                out_rows(n, 2)
                exps(n, 3)
            if back:
                gelu(kind, n, 0)
            if front:
                out_rows(n, 3)
            if back:
                for m in range(1, KF):
                    gelu(kind, n, m)
            if swap == 2:
                weights(l, "f1")
                weights(l, "f2")
                act.wait_ge(back_in.sem, back_in.after(l))

        all_bodies(act, body)

    @block.vector
    def _(dve):
        for s in (w_lo, qb_ready, ln1_steps, z1, xh1, qk_h, mx_in, rd_in, on_in, ol, xo, xb1, xb2,
                  ln2_steps, z2, xh2, h_h, y_x):
            dve.sem_inc(s.sem, s.credit())

        def weights(l, part):
            for i in PARTS[part]:
                dve.wait_ge(w_hi.sem, w_hi.after(l, i + 1))
                dve.scalar_tensor_tensor(w_half[1][:, i * CH:(i + 1) * CH], w_raw[i % NRAW][:, :], WS,
                                         w_half[0][:, i * CH:(i + 1) * CH], ALU.mult, ALU.subtract)\
                   .then_inc(w_lo.sem, 1)

        def query_bias(l):
            dve.wait_ge(ahead_in.sem, ahead_in.after(l))
            dve.tensor_scalar(qbias[:, :], cols[:, 0:4:2], HD ** -0.5, None, ALU.mult).then_inc(qb_ready.sem, 1)

        def norm1(n, g):
            dve.wait_ge(T1_ps.sem, T1_ps.after(n - 1))
            layer_norm(dve, lambda t: x[:, bass.ds(g * TT + t, 1), :], lambda t: z[0][:, t:t + 1, :], norm_buf[0],
                       ln1_steps.sem, lambda k: ln1_steps.after(n, k), z1.sem)

        def add_row(g, row, done):
            for t in range(TT):
                last = dve.tensor_tensor(x[:, bass.ds(g * TT + t, 1), :], x[:, bass.ds(g * TT + t, 1), :],
                                         rows[:, row, :].unsqueeze(1), ALU.add)
            last.then_inc(done.sem, 1)

        def project(n):
            for k in range(KD):
                dve.wait_ge(xf1.sem, xf1.after(n, k + 1))
                if k == 0:
                    dve.wait_ge(xl1.sem, xl1.after(n - 1))
                    dve.wait_ge(V_ps.sem, V_ps.after(n - 1))
                dve.tensor_copy(xT[0][0][:, k, :], xT32[0][:, k, :]).then_inc(xh1.sem, 1)

        def query_key_high(n, tiles):
            for m in tiles:
                dve.wait_ge(qk_f.sem, qk_f.after(n, m + 1))
                if m == 0:
                    dve.wait_ge(heads_in[0].sem, heads_in[0].after(n - 1))
                    dve.wait_ge(heads_in[1].sem, heads_in[1].after(n - 1))
                    dve.wait_ge(qk_l.sem, qk_l.after(n - 1))
                dve.tensor_copy(QK[0][:, m, :], qk32[:, m % 2, :]).then_inc(qk_h.sem, 1)

        def outputs(kind, n):
            for t in range(TT):
                dve.wait_ge(OS_ps.sem, OS_ps.after(n - 1, t + 1))
                bank = W[kind.index(("OS", t)) % R][:, :].rearrange("p (h d) -> p h d", h=H)
                if t == 0:
                    dve.wait_ge(OT_ps.sem, OT_ps.after(n - 2))
                dve.reciprocal(rden[:, t, :], bank[:, :, HD]).then_inc(rd_in.sem, 1)
                dve.wait_ge(rd_in.sem, rd_in.after(n - 1, t + 1))
                dve.tensor_tensor(On[:, t, :].rearrange("p (h d) -> p h d", h=H), bank[:, :, 0:HD],
                                  rden[:, t, :].unsqueeze(2).to_broadcast([P, H, HD]), ALU.mult)\
                   .then_inc(on_in.sem, 1)

        def residual(kind, n, g, name, ps, done, bias_done):
            dve.wait_ge(bias_done.sem, bias_done.after(n - 1))
            for k in range(2):
                dve.wait_ge(ps.sem, ps.after(n - 1, k + 1))
                xs = x[:, bass.ds(g * TT + 2 * k, 2), :].rearrange("p t d -> p (t d)")
                dve.scalar_tensor_tensor(xs, W[kind.index((name, k)) % R][:, :], 1.0 / WS, xs,
                                         ALU.mult, ALU.add).then_inc(done.sem, 1)

        def outputs_low(kind, n):
            for k in range(KD):
                dve.wait_ge(oh.sem, oh.after(n - 1, k + 1))
                if k == 0:
                    dve.wait_ge(OP_ps.sem, OP_ps.after(n - 2))
                dve.tensor_tensor(oT[1][:, k, :], W[kind.index(("OT", k)) % R][:, :], oT[0][:, k, :],
                                  ALU.subtract).then_inc(ol.sem, 1)

        def norm2_stats(n, g, t):
            dve.wait_ge(xo.sem, xo.after(n - 1))
            norm_stats(dve, lambda t: x[:, bass.ds(g * TT + t, 1), :], norm_buf[1], ln2_steps.sem, [t])

        def norm2(n, g):
            dve.wait_ge(T2_ps.sem, T2_ps.after(n - 2))
            layer_norm(dve, lambda t: x[:, bass.ds(g * TT + t, 1), :], lambda t: z[1][:, t:t + 1, :], norm_buf[1],
                       ln2_steps.sem, lambda k: ln2_steps.after(n - 1, k), z2.sem, with_stats=False)

        def norm2_high(n):
            for k in range(KD):
                dve.wait_ge(xf2.sem, xf2.after(n - 1, k + 1))
                if k == 0:
                    dve.wait_ge(xl2.sem, xl2.after(n - 2))
                    dve.wait_ge(H_ps.sem, H_ps.after(n - 2))
                dve.tensor_copy(xT[1][0][:, k, :], xT32[1][:, k, :]).then_inc(xh2.sem, 1)

        def maxima(n, c, chunks=range(6)):
            for q in chunks:
                b, i = divmod(q, 3)
                dve.wait_ge(M_ps.sem, M_ps.after(n, 6 * c + q + 1))
                if q == 0:
                    if c < 2:
                        dve.wait_ge(MT_ps.sem, MT_ps.after(n - 1, c + 3))
                    else:
                        dve.wait_ge(MT_ps.sem, MT_ps.after(n, c - 1))
                bank = M[(6 * c + q) % 2]
                if i < 2:
                    out, src = mx[c % 2][:, 2 * b + 1, 2 * i:2 * i + 2], bank[:, :].rearrange("p (h k) -> p h k", h=2)
                else:
                    out, src = mx[c % 2][:, 2 * b, :], bank[:, :].rearrange("p (h k) -> p h k", h=C)
                dve.tensor_reduce(out, src, AX.X, ALU.max, negate=True).then_inc(mx_in.sem, 1)

        def hidden_high(n, m):
            dve.wait_ge(h_f.sem, h_f.after(n - 1, m + 1))
            if m == 0:
                dve.wait_ge(Y_ps.sem, Y_ps.after(n - 2))
            dve.tensor_copy(hT[0][:, m, :], h32[:, m % 2, :]).then_inc(h_h.sem, 1)

        def body(kind, n, l, g, ahead, front, back, swap):
            last_g = NG - 1 if swap == 2 else g - 1
            next_g = {NG - 2: 0, NG - 1: 1}.get(g, g + 2) if isinstance(g, int) else g + 2
            if kind is PRE:
                dve.wait_ge(s_x_first, 16)
                norm1(0, 0)
                query_bias(0)
                dve.memset(KS[:, :, :], 0.0).then_inc(s_init, 1)
                dve.memset(VS[:, :, :, :], 1.0).then_inc(s_init, 1)
                weights(0, "qkv")
                dve.wait_ge(s_const, 16 * 2)
                for dst, src in ((ident_b, ident[:, :]), (mask_q, z[1][:, 0, 0:P]), (mask_k, z[1][:, 0, P:2 * P])):
                    last = dve.tensor_copy(dst[:, :], src)
                last.then_inc(s_masks, 1)
            if kind is HEAD:
                for part in ("o", "f1", "f2"):
                    weights(0, part)
                for s in row_in[1:]:
                    dve.wait_ge(s.sem, s.after(0))
            if swap == 1:
                query_bias(l + 1)
            if swap == 2:
                dve.wait_ge(row_in[1].sem, row_in[1].after(l))
            if front:
                maxima(n, 0, range(2))
            if back:
                outputs(kind, n)
            if front:
                maxima(n, 0, range(2, 6))
            if back:
                outputs_low(kind, n)
            if ahead:
                project(n + 1)
            if back:
                residual(kind, n, last_g, "OP", OP_ps, xo, xb1)
            for q in range(6):
                if front:
                    maxima(n, 1, [q])
                if back and q < TT:
                    norm2_stats(n, last_g, q)
            if back:
                norm2(n, last_g)
            if swap == 1:
                weights(l + 1, "qkv")
            if ahead:
                query_key_high(n + 1, range(3))
            if front:
                maxima(n, 2, [0])
            if ahead:
                query_key_high(n + 1, [3])
            if swap == 2:
                weights(l, "o")
            if front:
                maxima(n, 2, range(1, 6))
            if back:
                norm2_high(n)
            if front:
                maxima(n, 3)
                add_row(g, 1, xb1)
            if back:
                dve.wait_ge(z2.sem, z2.after(n - 1))
                add_row(last_g, 2, xb2)
                for m in range(KF):
                    hidden_high(n, m)
            if swap == 2:
                weights(l, "f1")
            if kind in (PRE, HEAD, STEADY) and not (isinstance(l, int) and l == L - 1 and isinstance(g, int)
                                                    and g == NG - 2):
                if kind is PRE:
                    dve.wait_ge(s_x, 16)
                norm1(n + 2, next_g)
            if back:
                residual(kind, n, last_g, "Y", Y_ps, y_x, xb2)
            if swap == 2:
                weights(l, "f2")
                dve.wait_ge(row_in[2].sem, row_in[2].after(l))

        all_bodies(dve, body)
        dve.wait_ge(y_x.sem, y_x.after(L * NG - 1))

    @block.gpsimd
    def _(pool):
        for s in (xl1, v_in, qk_l, xl2, h_l):
            pool.sem_inc(s.sem, s.credit())
        pool.memset(QS[:, :, :], 0.0).then_inc(s_init, 1)

        def low(i, n, hi, out, last_read):
            for k in range(KD):
                pool.wait_ge(hi.sem, hi.after(n, k + 1))
                if k == 0:
                    pool.wait_ge(last_read.sem, last_read.after(n - 1))
                pool.tensor_tensor(xT[i][1][:, k, :], xT32[i][:, k, :], xT[i][0][:, k, :], ALU.subtract)\
                    .then_inc(out.sem, 1)

        def values(n):
            for t in range(TT):
                pool.wait_ge(v_f.sem, v_f.after(n, t + 1))
                pool.tensor_tensor(VS[:, t, :, 0:HD], VS[:, t, :, 0:HD],
                                   rows[:, 0, :].rearrange("p (h d) -> p h d", h=H), ALU.add).then_inc(v_in.sem, 1)

        def query_key_low(n):
            for m in range(4):
                pool.wait_ge(qk_h.sem, qk_h.after(n, m + 1))
                if m == 0:
                    pool.wait_ge(heads_in[0].sem, heads_in[0].after(n - 1))
                    pool.wait_ge(heads_in[1].sem, heads_in[1].after(n - 1))
                pool.tensor_tensor(QK[1][:, m, :], qk32[:, m % 2, :], QK[0][:, m, :], ALU.subtract)\
                    .then_inc(qk_l.sem, 1)

        def hidden_low(n, m):
            pool.wait_ge(h_h.sem, h_h.after(n - 1, m + 1))
            if m == 0:
                pool.wait_ge(Y_ps.sem, Y_ps.after(n - 2))
            pool.tensor_tensor(hT[1][:, m, :], h32[:, m % 2, :], hT[0][:, m, :], ALU.subtract)\
                .then_inc(h_l.sem, 1)

        def body(kind, n, l, g, ahead, front, back, swap):
            if kind is HEAD or swap == 2:
                pool.wait_ge(row_in[0].sem, row_in[0].after(l))
            if front:
                values(n)
            if ahead:
                low(0, n + 1, xh1, xl1, V_ps)
                query_key_low(n + 1)
            if back:
                low(1, n - 1, xh2, xl2, H_ps)
                for m in range(KF):
                    hidden_low(n, m)

        all_bodies(pool, body)

    block_ctx.close()


def cross(nc, sb, sem, psum, shared, dram):
    x, ident, QS, KS, VS = shared["x"], shared["ident"], shared["QS"], shared["KS"], shared["VS"]
    W, M, SC, O = psum["W"], psum["M"], psum["S"], psum["O"]
    QK, qk32, mx, mrow, PR, OTs, On, oT, rden = (
        shared[k] for k in ("QK", "qk32", "mx", "mrow", "PR", "OTs", "On", "oT", "rden"))
    weight, weight_ws = shared["expert_weight"], shared["expert_weight_ws"]
    xT_halves = dram["xT_halves"]

    WC = KD * 3 * D + KD * F2 + KF2 * D + KD * E
    w_raw = sb("c_raw", [P, WC], F32)
    w_half = [sb(f"c_half{i}", [P, WC], F16) for i in range(2)]
    at, views = 0, {}
    for name, k, cols_of in (("q", KD, D), ("k", KD, D), ("v", KD, D), ("f1", KD, F2), ("f2", KF2, D), ("r", KD, E)):
        views[name] = [w[:, at:at + k * cols_of].rearrange("p (k n) -> p k n", k=k) for w in w_half]
        at += k * cols_of
    ROWS = 4 * D + E
    rows = sb("c_rows", [P, ROWS], F32)
    row = {name: rows[:, i * D:(i + 1) * D] for i, name in enumerate(("fw", "fb", "bv", "b2"))}
    router_bias = rows[:, 4 * D:ROWS]
    cols = sb("c_cols", [P, 8], F32)
    qbias = sb("c_qbias", [P, 2], F32)
    x0 = sb("c_x0", [P, TT, D], F32)
    ctx32 = sb("c_ctx32", [P, KD, GB * S], F32)
    ctx = [sb(f"c_ctx{h}", [P, KD, GB * S], F16) for h in range(2)]
    z = [sb(f"c_z{i}", [P, TT, D], F32) for i in range(3)]
    norm_buf = [NormBuffers(sb, f"c_norm{i}", shared["dve_gate"]) for i in range(3)]
    xT = [[sb(f"c_xT{i}_{h}", [P, KD, GT], F16) for h in range(2)] for i in range(2)]
    h32 = sb("c_h32", [P, 2, GT], F32)
    hT = [sb(f"c_hT{h}", [P, KF2, GT], F16) for h in range(2)]
    logit = sb("c_logit", [P, TT, E], F32)
    top = sb("c_top", [P, TT, 8], F32)
    less = sb("c_less", [P, TT, E], F32)
    chosen = sb("c_chosen", [P, TT, E], F32)
    power = sb("c_power", [P, TT, E], F32)
    total = sb("c_total", [P, TT], F32)

    def sig(name, per, unit=1):
        return Signal(sem("c_" + name), per, unit)

    s_const, s_w_in, s_w_hi, s_w_lo, s_qb = (
        sem("c_" + name) for name in ("const", "w_in", "w_hi", "w_lo", "qb"))
    x0_in, ctx_in = sig("x0_in", 1, 16), sig("ctx_in", 1, 16)
    steps = [sig(f"steps{i}", NORM_STEPS) for i in range(3)]
    zf, mix, z1, z1b = sig("zf", TT), sig("mix", 3), sig("z1", TT), sig("z1b", 1)
    T1_ps, xh1, xl1 = sig("T1_ps", KD), sig("xh1", KD), sig("xl1", KD)
    ctx_h, ctx_l = sig("ctx_h", 1), sig("ctx_l", 1)
    V_ps, v_f, v_in = sig("V_ps", 1), sig("v_f", GB), sig("v_in", GB)
    QK_ps, qk_f, qk_h, qk_l = sig("QK_ps", 4), sig("qk_f", 4), sig("qk_h", 4), sig("qk_l", 4)
    heads_in = [sig(f"heads_in{m}", 6, 16) for m in range(2)]
    CH = 4
    M_ps, mx_in = sig("M_ps", CH * C), sig("mx_in", CH * C)
    MT_ps, mrow_in = sig("MT_ps", C), sig("mrow_in", C)
    m_in = [sig(f"m_in{i}", C // 2, 16) for i in range(2)]
    S_ps, p_in, O_ps, o_in = sig("S_ps", CH * C), sig("p_in", CH * C), sig("O_ps", C), sig("o_in", C)
    OS_ps, rd_in, on_in = sig("OS_ps", TT), sig("rd_in", TT), sig("on_in", TT)
    OT_ps, oh, ol = sig("OT_ps", KD), sig("oh", KD), sig("ol", KD)
    H_ps, h_f, h_h, h_l = sig("H_ps", KF2), sig("h_f", KF2), sig("h_h", KF2), sig("h_l", KF2)
    Y_ps, y_in, z2, x_in = sig("Y_ps", 2), sig("y_in", 2), sig("z2", TT), sig("x_in", 1)
    T2_ps, xh2, xl2, halves_out = sig("T2_ps", KD), sig("xh2", KD), sig("xl2", KD), sig("halves_out", 2, 16)
    R_ps, route, powers = sig("R_ps", 1), sig("route", TT + 7), sig("powers", 1)

    R = len(W)
    READERS = {"T1": [(xh1, 1), (xl1, 1)], "V": [(v_f, GB)], "QK": [(qk_f, 1)], "MT": [(mrow_in, 1)],
               "OS": [(on_in, 1)], "OT": [(oh, 1), (ol, 1)], "H": [(h_f, 1)], "Y": [(y_in, 1)],
               "T2": [(xh2, 1), (xl2, 1)], "R": [(route, 1)]}
    ROUND = {"T1": 1, "QK": 1, "V": 0, "MT": 0} | {stage: -1 for stage in ("OS", "OT", "H", "Y", "T2", "R")}

    def tiles_of(ahead, front, back):
        def some(wanted, stage, count):
            return [(stage, k) for k in range(count)] if wanted else []

        out = some(front, "V", 1) + some(back, "OS", TT) + some(back, "OT", KD)
        out += [("MT", 0)] * front + some(back, "H", KF2) + [("MT", 1)] * front
        out += some(ahead, "T1", KD) + some(ahead, "QK", 4) + some(back, "Y", 2) + [("MT", 2)] * front
        out += [("MT", 3)] * front + some(back, "T2", KD) + some(back, "R", 1)
        return out + [None] * (-len(out) % R)

    PRE, HEAD, STEADY = tiles_of(True, False, False), tiles_of(True, True, False), tiles_of(True, True, True)
    LAST, TAIL = tiles_of(False, True, True), tiles_of(False, False, True)
    BEFORE = {id(PRE): [], id(HEAD): [(PRE, -1)], id(STEADY): [(HEAD, -1), (STEADY, -1)],
              id(LAST): [(STEADY, -1)], id(TAIL): [(LAST, -1)]}

    def work(kind, tile):
        return W[kind.index(tile) % R]

    def free_tile(pe, kind, n, tile, inputs=()):
        pos = kind.index(tile)
        need = {signal: (m, signal.per) for signal, m in inputs}
        for other, m in [(kind, 0)] if pos >= R else BEFORE[id(kind)]:
            q = pos - R if pos >= R else len(other) - R + pos
            while other[q] is None:
                q -= R
            stage, k = other[q]
            for signal, each in READERS[stage]:
                at = (m + ROUND[stage], (k + 1) * each)
                need[signal] = max(need.get(signal, at), at)
        for signal, (m, raises) in need.items():
            pe.wait_ge(signal.sem, signal.after(n + m, raises))
        return work(kind, tile)

    def all_bodies(eng, body):
        body(PRE, -1, True, False, False)
        body(HEAD, 0, True, True, False)
        with eng.Fori(1, NG - 1) as n:
            body(STEADY, n, True, True, True)
        body(LAST, NG - 1, False, True, True)
        body(TAIL, NG, False, False, True)

    block_ctx = ExitStack()
    block = block_ctx.enter_context(nc.Block())

    @block.sync
    def _(sp):
        for s in (x0_in, ctx_in, *heads_in, *m_in, halves_out):
            sp.sem_inc(s.sem, s.credit())
        def load_x0(n):
            sp.wait_ge(mix.sem, mix.after(n - 1))
            sp.dma_start(x0[:, :, :], dram["x"][bass.ds(n * GT, GT)].rearrange("(t p) d -> p t d", p=P))\
              .then_inc(x0_in.sem, 16)

        def load(n):
            sp.wait_ge(ctx_h.sem, ctx_h.after(n - 1))
            sp.wait_ge(ctx_l.sem, ctx_l.after(n - 1))
            sp.dma_start(ctx32[:, :, :], dram["ctx"][:, :, bass.ds(n * (GB * S), GB * S)]).then_inc(ctx_in.sem, 16)

        def heads(n, m):
            sp.wait_ge(S_ps.sem, S_ps.after(n - 1, 2 * CH * (m + 1)))
            part_from_wait(sp, shared["sp_gate"])
            sp.wait_ge(qk_h.sem, qk_h.after(n, 2 * m + 2))
            sp.wait_ge(qk_l.sem, qk_l.after(n, 2 * m + 2))
            for tile, dst, width, half_rows in ((2 * m, QS, GT, ((0, 0), (R_HI2, 0), (R_LO, 1))),
                                                (2 * m + 1, KS, GB * S, ((0, 0), (R_LO, 0), (R_HI2, 1)))):
                for r, half in half_rows:
                    sp.dma_start(dst[r:r + HD, 8 * m:8 * m + 8, 0:width], QK[half][:, tile, 0:width])\
                      .then_inc(heads_in[m].sem, 16)

        def maximum(n, c):
            sp.wait_ge(mrow_in.sem, mrow_in.after(n, c + 1))
            sp.dma_start(QS[R_MAX:R_MAX + 1, C * c:C * c + C, :], mrow[c % 2][0:C, :])\
              .then_inc(m_in[c % 2].sem, 16)

        def halves(n):
            for half, s in enumerate((xh2, xl2)):
                sp.wait_ge(s.sem, s.after(n))
                part_from_wait(sp, shared["sp_gate"])
                sp.dma_start(xT_halves[half, :, :, bass.ds(n * GT, GT)], xT[1][half][:, :, :])\
                  .then_inc(halves_out.sem, 16)

        def body(kind, n, ahead, front, back):
            if front:
                for c in range(3):
                    maximum(n, c)
            if ahead:
                heads(n + 1, 0)
            if front:
                maximum(n, 3)
            if ahead:
                heads(n + 1, 1)
            if back:
                halves(n - 1)

        sp.dma_start(rows[:, :], dram["cross_rows"].partition_broadcast(P)).then_inc(s_const, 16)
        sp.dma_start(cols[:, :], dram["cross_cols"]).then_inc(s_const, 16)
        sp.dma_start(KS[R_POS:R_POS + 2, :, :], dram["zeros2"]).then_inc(s_const, 16)
        load_x0(0)
        load(0)
        sp.dma_start(w_raw[:, :], dram["cross_weights"]).then_inc(s_w_in, 16)
        load_x0(1)
        body(PRE, -1, True, False, False)
        load(1)
        load_x0(2)
        body(HEAD, 0, True, True, False)
        load(2)
        with sp.Fori(1, NG - 2) as n:
            load_x0(n + 2)
            body(STEADY, n, True, True, True)
            load(n + 2)
        body(STEADY, NG - 2, True, True, True)
        body(LAST, NG - 1, False, True, True)
        body(TAIL, NG, False, False, True)
        sp.wait_ge(halves_out.sem, halves_out.after(NG - 1))

    @block.tensor
    def _(pe):
        for s in (T1_ps, V_ps, QK_ps, M_ps, MT_ps, S_ps, O_ps, OS_ps, OT_ps, H_ps, Y_ps, T2_ps, R_ps):
            pe.sem_inc(s.sem, s.credit())
        pe.wait_ge(s_const, 16 * 3)

        def turn(kind, n, name, ps, src, ready):
            for k in range(KD):
                bank = free_tile(pe, kind, n, (name, k), ((ready, ROUND[name]),))
                for t in range(TT):
                    last = pe.transpose(bank[:, t * P:(t + 1) * P], src[:, t, k * P:(k + 1) * P], ident[:, :])
                last.then_inc(ps.sem, 1)

        def row_scores(n, c, q):
            if c % 2 == 0 and q == 0:
                pe.wait_ge(heads_in[c // 2].sem, heads_in[c // 2].after(n))
            i = CH * c + q
            pe.wait_ge(mx_in.sem, mx_in.after(n, i - 1) if i >= 2 else mx_in.after(n - 1, CH * C - 1 + i))
            bank, b = M[i % 2], q // 2
            for u in range(C):
                last = pe.matmul(bank[:, u * S:(u + 1) * S], QS[0:R_MAX, C * c + u, q * P:(q + 1) * P],
                                 KS[0:R_MAX, C * c + u, b * S:(b + 1) * S], start=True, stop=True)
            last.then_inc(M_ps.sem, 1)

        def turn_maxima(kind, n, c):
            bank = free_tile(pe, kind, n, ("MT", c))
            pe.wait_ge(mx_in.sem, mx_in.after(n, CH * (c + 1)))
            for t in range(TT):
                last = pe.transpose(bank[0:C, t * P:(t + 1) * P], mx[c % 2][:, t, :], ident[:, :])
            last.then_inc(MT_ps.sem, 1)

        def key_scores(n, c, q):
            if q == 0:
                pe.wait_ge(m_in[c % 2].sem, m_in[c % 2].after(n, c // 2 + 1))
            i = CH * c + q
            pe.wait_ge(p_in.sem, p_in.after(n, i - 1) if i >= 2 else p_in.after(n - 1, CH * C - 1 + i))
            bank, b = SC[i % 2], q // 2
            for u in range(2):
                h = C * c + 2 * (q % 2) + u
                last = pe.matmul(bank[0:S, u * T:(u + 1) * T], KS[:, h, b * S:(b + 1) * S],
                                 QS[:, h, b * T:(b + 1) * T], start=True, stop=True)
            last.then_inc(S_ps.sem, 1)

        def attend(n, c):
            if c == 0:
                pe.wait_ge(v_in.sem, v_in.after(n))
            pe.wait_ge(p_in.sem, p_in.after(n, CH * (c + 1)))
            pe.wait_ge(o_in.sem, o_in.after(n, c) if c else o_in.after(n - 1))
            for b in range(GB):
                for u in range(C):
                    last = pe.matmul(O[32 * u:32 * u + 32, b * T:(b + 1) * T], VS[0:S, b, C * c + u, :],
                                     PR[c % 2][0:S, 2 * b + u // 2, (u % 2) * T:(u % 2 + 1) * T],
                                     start=True, stop=True)
            last.then_inc(O_ps.sem, 1)

        def values(kind, n):
            bank = free_tile(pe, kind, n, ("V", 0), ((ctx_h, 0), (ctx_l, 0)))
            for b in range(GB):
                last = split_matmuls(pe, bank[0:S, b * D:(b + 1) * D], lambda h, k: ctx[h][:, k, b * S:(b + 1) * S],
                                     lambda h, k: views["v"][h][:, k, :], KD)
            last.then_inc(V_ps.sem, 1)

        def queries_keys(kind, n):
            for m in range(4):
                if kind is PRE and m == 0:
                    pe.wait_ge(s_w_hi, 1)
                    pe.wait_ge(s_w_lo, 1)
                ready = (((xh1, 1), (xl1, 1)), ((ctx_h, 1), (ctx_l, 1)), (), ())[m]
                bank = free_tile(pe, kind, n, ("QK", m), ready)
                side, src, width = (("q", xT[0], GT), ("k", ctx, GB * S))[m % 2]
                split_matmuls(pe, bank[:, 0:width],
                              lambda h, k: views[side][h][:, k, (m // 2) * P:(m // 2 + 1) * P],
                              lambda h, k: src[h][:, k, :], KD).then_inc(QK_ps.sem, 1)

        def turn_outputs(kind, n):
            for t in range(TT):
                bank = free_tile(pe, kind, n, ("OS", t), ((o_in, -1),))
                for c in range(C):
                    last = pe.transpose(bank[:, c * P:(c + 1) * P], OTs[:, c, t * P:(t + 1) * P], ident[:, :])
                last.then_inc(OS_ps.sem, 1)

        def hidden(kind, n):
            for m in range(KF2):
                bank = free_tile(pe, kind, n, ("H", m), ((oh, -1), (ol, -1)))
                split_matmuls(pe, bank[:, :], lambda h, k: views["f1"][h][:, k, m * P:(m + 1) * P],
                              lambda h, k: oT[h][:, k, :], KD).then_inc(H_ps.sem, 1)

        def outputs(kind, n):
            for k in range(2):
                bank = free_tile(pe, kind, n, ("Y", k), ((h_h, -1), (h_l, -1)))
                for u in range(2):
                    t = 2 * k + u
                    last = split_matmuls(pe, bank[:, u * D:(u + 1) * D], lambda h, kk: hT[h][:, kk, t * P:(t + 1) * P],
                                         lambda h, kk: views["f2"][h][:, kk, :], KF2)
                last.then_inc(Y_ps.sem, 1)

        def router(kind, n):
            bank = free_tile(pe, kind, n, ("R", 0), ((xh2, -1), (xl2, -1)))
            for t in range(TT):
                last = split_matmuls(pe, bank[:, t * E:(t + 1) * E], lambda h, k: xT[1][h][:, k, t * P:(t + 1) * P],
                                     lambda h, k: views["r"][h][:, k, :], KD)
            last.then_inc(R_ps.sem, 1)

        def body(kind, n, ahead, front, back):
            def interleaved(c):
                for q in range(CH):
                    if c + 1 < C:
                        row_scores(n, c + 1, q)
                    key_scores(n, c, q)

            if front:
                values(kind, n)
                row_scores(n, 0, 0)
                row_scores(n, 0, 1)
            if back:
                turn_outputs(kind, n)
            if front:
                row_scores(n, 0, 2)
                row_scores(n, 0, 3)
            if back:
                turn(kind, n, "OT", OT_ps, On, on_in)
            if front:
                turn_maxima(kind, n, 0)
            if back:
                hidden(kind, n)
            if front:
                interleaved(0)
                turn_maxima(kind, n, 1)
            if ahead:
                turn(kind, n, "T1", T1_ps, z[1], z1)
            if front:
                attend(n, 0)
            if ahead:
                queries_keys(kind, n)
            if back:
                outputs(kind, n)
            if front:
                interleaved(1)
                turn_maxima(kind, n, 2)
                attend(n, 1)
                interleaved(2)
                turn_maxima(kind, n, 3)
                attend(n, 2)
            if back:
                turn(kind, n, "T2", T2_ps, z[2], z2)
            if front:
                interleaved(3)
                attend(n, 3)
            if back:
                router(kind, n)

        all_bodies(pe, body)

    @block.scalar
    def _(act):
        for s in (ctx_h, xh1, v_f, qk_f, mrow_in, p_in, o_in, oh, h_f, xh2, x_in, powers):
            act.sem_inc(s.sem, s.credit())
        act.wait_ge(s_const, 16 * 3)
        act.wait_ge(s_w_in, 16)
        act.activation(w_half[0][:, :], w_raw[:, :], ACT.Copy, scale=WS).then_inc(s_w_hi, 1)
        act.wait_ge(s_qb, 1)

        def project(kind, n):
            act.wait_ge(ctx_in.sem, ctx_in.after(n + 1))
            act.wait_ge(V_ps.sem, V_ps.after(n))
            act.wait_ge(QK_ps.sem, QK_ps.after(n))
            act.wait_ge(ctx_l.sem, ctx_l.after(n))
            act.activation(ctx[0][:, :, :], ctx32[:, :, :], ACT.Copy).then_inc(ctx_h.sem, 1)
            for k in range(KD):
                act.wait_ge(T1_ps.sem, T1_ps.after(n + 1, k + 1))
                act.activation(xT[0][0][:, k, :], work(kind, ("T1", k))[:, :], ACT.Copy).then_inc(xh1.sem, 1)

        def queries_keys(kind, n):
            for m in range(4):
                act.wait_ge(QK_ps.sem, QK_ps.after(n + 1, m + 1))
                for s in (qk_h, qk_l):
                    act.wait_ge(s.sem, s.after(n + 1, m - 1) if m >= 2 else s.after(n, m + 3))
                query = m % 2 == 0
                width = GT if query else GB * S
                act.activation(qk32[:, m % 2, 0:width], work(kind, ("QK", m))[:, 0:width], ACT.Identity,
                               bias=qbias[:, m // 2:m // 2 + 1] if query else cols[:, m:m + 1],
                               scale=(HD ** -0.5 if query else 1.0) / WS).then_inc(qk_f.sem, 1)

        def values(kind, n):
            act.wait_ge(O_ps.sem, O_ps.after(n - 1))
            for b in range(GB):
                act.wait_ge(V_ps.sem, V_ps.after(n))
                act.activation(VS[0:S, b, :, 0:HD],
                               work(kind, ("V", 0))[0:S, b * D:(b + 1) * D].rearrange("p (h d) -> p h d", h=H),
                               ACT.Copy, scale=1.0 / WS).then_inc(v_f.sem, 1)

        def max_row(kind, n, c):
            act.wait_ge(MT_ps.sem, MT_ps.after(n, c + 1))
            act.wait_ge(m_in[c % 2].sem, m_in[c % 2].after(n, c // 2))
            act.activation(mrow[c % 2][0:C, :], work(kind, ("MT", c))[0:C, :], ACT.Copy).then_inc(mrow_in.sem, 1)

        def exps(n, c):
            if c < 2:
                act.wait_ge(O_ps.sem, O_ps.after(n - 1, c + 3))
            else:
                act.wait_ge(O_ps.sem, O_ps.after(n, c - 1))
            for q in range(CH):
                act.wait_ge(S_ps.sem, S_ps.after(n, CH * c + q + 1))
                act.activation(PR[c % 2][0:S, q, :], SC[(CH * c + q) % 2][0:S, :], ACT.Exp).then_inc(p_in.sem, 1)

        def out_rows(n, c):
            act.wait_ge(O_ps.sem, O_ps.after(n, c + 1))
            if c == 0:
                act.wait_ge(OS_ps.sem, OS_ps.after(n - 1))
            act.activation(OTs[:, c, :], O[:, :], ACT.Copy).then_inc(o_in.sem, 1)

        def hidden(kind, n):
            for m in range(KF2):
                act.wait_ge(H_ps.sem, H_ps.after(n - 1, m + 1))
                for s in (h_h, h_l):
                    act.wait_ge(s.sem, s.after(n - 1, m - 1) if m >= 2 else s.after(n - 2, KF2 - 1 + m))
                act.activation(h32[:, m % 2, :], work(kind, ("H", m))[:, :], ACT.Relu,
                               bias=cols[:, 4 + m:5 + m], scale=1.0 / WS).then_inc(h_f.sem, 1)

        def body(kind, n, ahead, front, back):
            if front:
                values(kind, n)
            if back:
                for k in range(KD):
                    act.wait_ge(OT_ps.sem, OT_ps.after(n - 1, k + 1))
                    act.wait_ge(H_ps.sem, H_ps.after(n - 2))
                    act.activation(oT[0][:, k, :], work(kind, ("OT", k))[:, :], ACT.Copy).then_inc(oh.sem, 1)
            if front:
                max_row(kind, n, 0)
            if back:
                hidden(kind, n)
            if front:
                exps(n, 0)
                max_row(kind, n, 1)
            if ahead:
                project(kind, n)
            if front:
                out_rows(n, 0)
            if ahead:
                queries_keys(kind, n)
            if front:
                exps(n, 1)
                max_row(kind, n, 2)
                out_rows(n, 1)
                exps(n, 2)
                max_row(kind, n, 3)
                out_rows(n, 2)
            if back:
                for k in range(KD):
                    act.wait_ge(T2_ps.sem, T2_ps.after(n - 1, k + 1))
                    if k == 0:
                        act.wait_ge(halves_out.sem, halves_out.after(n - 2))
                        act.wait_ge(R_ps.sem, R_ps.after(n - 2))
                    act.activation(xT[1][0][:, k, :], work(kind, ("T2", k))[:, :], ACT.Copy).then_inc(xh2.sem, 1)
                part_from_wait(act, shared["act_gate"])
                act.activation(x[:, bass.ds((n - 1) * TT, TT), :], z[2][:, :, :], ACT.Copy).then_inc(x_in.sem, 1)
            if front:
                exps(n, 3)
                out_rows(n, 3)
            if back:
                act.wait_ge(route.sem, route.after(n - 1, TT + 2))
                act.activation(power[:, :, :], less[:, :, :], ACT.Exp).then_inc(powers.sem, 1)

        all_bodies(act, body)

    @block.vector
    def _(dve):
        for s in (*steps, zf, z1, z1b, xl1, ctx_l, qk_h, mx_in, rd_in, on_in, ol, h_h, y_in, z2,
                  xl2, route):
            dve.sem_inc(s.sem, s.credit())
        dve.wait_ge(s_const, 16 * 3)
        def first_norm(n, stage):
            x_tiles = lambda t: x[:, bass.ds(n * TT + t, 1), :]
            if stage in range(TT):
                norm_stats(dve, x_tiles, norm_buf[0], steps[0].sem, [stage])
            else:
                dve.wait_ge(z1.sem, z1.after(n - 1))
                layer_norm(dve, x_tiles, lambda t: z[0][:, t:t + 1, :], norm_buf[0],
                           steps[0].sem, lambda k: steps[0].after(n, k), zf.sem, with_stats=False)

        def norm_sum(n):
            dve.wait_ge(mix.sem, mix.after(n))
            dve.wait_ge(T1_ps.sem, T1_ps.after(n - 1))
            layer_norm(dve, lambda t: z[0][:, t, :], lambda t: z[1][:, t, :], norm_buf[1],
                       steps[1].sem, lambda k: steps[1].after(n, k), z1.sem)
            dve.wait_ge(z1.sem, z1.after(n))
            dve.tensor_tensor(x[:, bass.ds(n * TT, TT), :], z[1][:, :, :], row["b2"].unsqueeze(1)
                              .to_broadcast([P, TT, D]), ALU.add).then_inc(z1b.sem, 1)

        def project_low(kind, n):
            dve.wait_ge(ctx_h.sem, ctx_h.after(n + 1))
            dve.tensor_tensor(ctx[1][:, :, :], ctx32[:, :, :], ctx[0][:, :, :], ALU.subtract).then_inc(ctx_l.sem, 1)
            for k in range(KD):
                dve.wait_ge(xh1.sem, xh1.after(n + 1, k + 1))
                dve.tensor_tensor(xT[0][1][:, k, :], work(kind, ("T1", k))[:, :], xT[0][0][:, k, :], ALU.subtract)\
                   .then_inc(xl1.sem, 1)

        def query_key_high(n):
            for m in range(4):
                dve.wait_ge(qk_f.sem, qk_f.after(n + 1, m + 1))
                if m == 0:
                    for s in (*heads_in, qk_l):
                        dve.wait_ge(s.sem, s.after(n))
                width = GT if m % 2 == 0 else GB * S
                dve.tensor_copy(QK[0][:, m, 0:width], qk32[:, m % 2, 0:width]).then_inc(qk_h.sem, 1)

        def maxima(n, c, chunks=range(CH)):
            for q in chunks:
                dve.wait_ge(M_ps.sem, M_ps.after(n, CH * c + q + 1))
                if q == 0:
                    dve.wait_ge(MT_ps.sem, MT_ps.after(n - 1, c + 3) if c < 2 else MT_ps.after(n, c - 1))
                dve.tensor_reduce(mx[c % 2][:, q, :],
                                  M[(CH * c + q) % 2][:, 0:C * S].rearrange("p (h k) -> p h k", h=C),
                                  AX.X, ALU.max, negate=True).then_inc(mx_in.sem, 1)

        def outputs(kind, n):
            for t in range(TT):
                dve.wait_ge(OS_ps.sem, OS_ps.after(n - 1, t + 1))
                bank = work(kind, ("OS", t))[:, :].rearrange("p (h d) -> p h d", h=H)
                dve.reciprocal(rden[:, t, :], bank[:, :, HD]).then_inc(rd_in.sem, 1)
                dve.wait_ge(rd_in.sem, rd_in.after(n - 1, t + 1))
                dve.tensor_tensor(On[:, t, :].rearrange("p (h d) -> p h d", h=H), bank[:, :, 0:HD],
                                  rden[:, t, :].unsqueeze(2).to_broadcast([P, H, HD]), ALU.mult)\
                   .then_inc(on_in.sem, 1)

        def outputs_low(kind, n):
            for k in range(KD):
                dve.wait_ge(oh.sem, oh.after(n - 1, k + 1))
                dve.tensor_tensor(oT[1][:, k, :], work(kind, ("OT", k))[:, :], oT[0][:, k, :], ALU.subtract)\
                   .then_inc(ol.sem, 1)

        def hidden_high(n):
            for m in range(KF2):
                dve.wait_ge(h_f.sem, h_f.after(n - 1, m + 1))
                if m == 0:
                    dve.wait_ge(Y_ps.sem, Y_ps.after(n - 2))
                dve.tensor_copy(hT[0][:, m, :], h32[:, m % 2, :]).then_inc(h_h.sem, 1)

        def residual(kind, n):
            for k in range(2):
                dve.wait_ge(Y_ps.sem, Y_ps.after(n - 1, k + 1))
                part = x[:, bass.ds((n - 1) * TT + 2 * k, 2), :].rearrange("p t d -> p (t d)")
                dve.scalar_tensor_tensor(part, work(kind, ("Y", k))[:, :], 1.0 / WS, part, ALU.mult, ALU.add)\
                   .then_inc(y_in.sem, 1)

        def last_norm(n, stage):
            x_tiles = lambda t: x[:, bass.ds((n - 1) * TT + t, 1), :]
            if stage in range(TT):
                dve.wait_ge(y_in.sem, y_in.after(n - 1))
                norm_stats(dve, x_tiles, norm_buf[2], steps[2].sem, [stage])
            else:
                dve.wait_ge(T2_ps.sem, T2_ps.after(n - 2))
                dve.wait_ge(x_in.sem, x_in.after(n - 2))
                layer_norm(dve, x_tiles, lambda t: z[2][:, t:t + 1, :], norm_buf[2], steps[2].sem,
                           lambda k: steps[2].after(n - 1, k), z2.sem, with_stats=False)

        def normed_low(kind, n):
            for k in range(KD):
                dve.wait_ge(xh2.sem, xh2.after(n - 1, k + 1))
                dve.tensor_tensor(xT[1][1][:, k, :], work(kind, ("T2", k))[:, :], xT[1][0][:, k, :], ALU.subtract)\
                   .then_inc(xl2.sem, 1)

        def router(kind, n):
            dve.wait_ge(R_ps.sem, R_ps.after(n))
            dve.scalar_tensor_tensor(logit[:, :, :], work(kind, ("R", 0))[:, 0:TT * E].rearrange("p (t e) -> p t e", t=TT),
                                     1.0 / WS, router_bias.unsqueeze(1).to_broadcast([P, TT, E]),
                                     ALU.mult, ALU.add).then_inc(route.sem, 1)
            dve.wait_ge(route.sem, route.after(n, 1))
            part_from_wait(dve, shared["dve_gate"])
            for t in range(TT):
                dve.max(top[:, t, :], logit[:, t, :]).then_inc(route.sem, 1)
            dve.wait_ge(route.sem, route.after(n, TT + 1))
            dve.tensor_tensor(less[:, :, :], logit[:, :, :], top[:, :, 0:1].to_broadcast([P, TT, E]), ALU.subtract)\
               .then_inc(route.sem, 1)
            dve.tensor_tensor(chosen[:, :, :], logit[:, :, :], top[:, :, 1:2].to_broadcast([P, TT, E]), ALU.is_ge)\
               .then_inc(route.sem, 1)
            dve.wait_ge(route.sem, route.after(n, TT + 3))
            dve.wait_ge(powers.sem, powers.after(n))
            dve.tensor_tensor(power[:, :, :], power[:, :, :], chosen[:, :, :], ALU.mult).then_inc(route.sem, 1)
            dve.wait_ge(route.sem, route.after(n, TT + 4))
            dve.tensor_reduce(total[:, :], power[:, :, :], AX.X, ALU.add).then_inc(route.sem, 1)
            dve.wait_ge(route.sem, route.after(n, TT + 5))
            dve.reciprocal(total[:, :], total[:, :]).then_inc(route.sem, 1)
            dve.wait_ge(route.sem, route.after(n, TT + 6))
            dve.tensor_tensor(power[:, :, :], power[:, :, :], total[:, :].unsqueeze(2).to_broadcast([P, TT, E]),
                              ALU.mult).then_inc(route.sem, 1)
            dve.wait_ge(route.sem, route.after(n, TT + 7))
            for scale, dst in ((1.0, weight), (1.0 / WS, weight_ws)):
                for t in range(TT):
                    dve.tensor_scalar(dst[:, :].rearrange("p (e n) -> p n e", e=E)[:, bass.ds(n * TT + t, 1), :],
                                      power[:, t:t + 1, :], scale, None, ALU.mult)

        def body(kind, n, ahead, front, back, next_norm):
            if front:
                maxima(n, 0, range(0, 2))
            if back:
                outputs(kind, n)
            if front:
                maxima(n, 0, range(2, 4))
            if back:
                outputs_low(kind, n)
                hidden_high(n)
            if front:
                maxima(n, 1)
            if ahead:
                project_low(kind, n)
            if next_norm:
                for stage in range(TT + 1):
                    first_norm(n + 2, stage)
            if ahead:
                query_key_high(n)
            if back:
                residual(kind, n)
            for q in range(CH):
                if front:
                    maxima(n, 2, [q])
                if back:
                    last_norm(n, q)
            if back:
                last_norm(n, TT)
            if front:
                maxima(n, 3)
            if back:
                normed_low(kind, n)
            if next_norm:
                norm_sum(n + 2)
            if back:
                router(kind, n - 1)

        for stage in range(TT + 1):
            first_norm(0, stage)
        norm_sum(0)
        dve.tensor_scalar(qbias[:, :], cols[:, 0:4:2], HD ** -0.5, None, ALU.mult).then_inc(s_qb, 1)
        dve.wait_ge(s_w_hi, 1)
        dve.scalar_tensor_tensor(w_half[1][:, :], w_raw[:, :], WS, w_half[0][:, :], ALU.mult, ALU.subtract)\
           .then_inc(s_w_lo, 1)
        body(PRE, -1, True, False, False, True)
        body(HEAD, 0, True, True, False, True)
        with dve.Fori(1, NG - 2) as n:
            body(STEADY, n, True, True, True, True)
        body(STEADY, NG - 2, True, True, True, False)
        body(LAST, NG - 1, False, True, True, False)
        body(TAIL, NG, False, False, True, False)

    @block.gpsimd
    def _(pool):
        for s in (v_in, qk_l, h_l, mix):
            pool.sem_inc(s.sem, s.credit())
        pool.wait_ge(s_const, 16 * 3)

        def add_first(n):
            pool.wait_ge(zf.sem, zf.after(n))
            for i, (other, op) in enumerate(((row["fw"], ALU.mult), (row["fb"], ALU.add), (None, ALU.add))):
                if other is None:
                    pool.wait_ge(x0_in.sem, x0_in.after(n))
                pool.wait_ge(mix.sem, mix.after(n, i))
                second = x0[:, :, :] if other is None else other.unsqueeze(1).to_broadcast([P, TT, D])
                pool.tensor_tensor(z[0][:, :, :], z[0][:, :, :], second, op).then_inc(mix.sem, 1)

        def body(kind, n, ahead, front, back):
            if front:
                for b in range(GB):
                    pool.wait_ge(v_f.sem, v_f.after(n, b + 1))
                    pool.tensor_tensor(VS[0:S, b, :, 0:HD], VS[0:S, b, :, 0:HD],
                                       row["bv"][0:S].rearrange("p (h d) -> p h d", h=H), ALU.add)\
                        .then_inc(v_in.sem, 1)
            if back:
                for m in range(KF2):
                    pool.wait_ge(h_h.sem, h_h.after(n - 1, m + 1))
                    if m == 0:
                        pool.wait_ge(Y_ps.sem, Y_ps.after(n - 2))
                    pool.tensor_tensor(hT[1][:, m, :], h32[:, m % 2, :], hT[0][:, m, :], ALU.subtract)\
                        .then_inc(h_l.sem, 1)
            if ahead:
                for m in range(4):
                    pool.wait_ge(qk_h.sem, qk_h.after(n + 1, m + 1))
                    if m == 0:
                        for s in heads_in:
                            pool.wait_ge(s.sem, s.after(n))
                    width = GT if m % 2 == 0 else GB * S
                    pool.tensor_tensor(QK[1][:, m, 0:width], qk32[:, m % 2, 0:width], QK[0][:, m, 0:width],
                                       ALU.subtract).then_inc(qk_l.sem, 1)
            if ahead and not (isinstance(n, int) and n == NG - 2):
                add_first(n + 2)

        add_first(0)
        body(PRE, -1, True, False, False)
        body(HEAD, 0, True, True, False)
        with pool.Fori(1, NG - 2) as n:
            body(STEADY, n, True, True, True)
        body(STEADY, NG - 2, True, True, True)
        body(LAST, NG - 1, False, True, True)
        body(TAIL, NG, False, False, True)

    block_ctx.close()


def experts(nc, sb, sem, banks, shared, dram, out):
    x, weight, weight_ws = shared["x"], shared["expert_weight"], shared["expert_weight_ws"]
    HB, YB = banks[0:4], banks[4:8]

    WC = KD * F + KF * D
    w_raw = [sb(f"e_raw{i}", [P, KD * F], F32) for i in range(2)]
    w_half = [[sb(f"e_half{i}_{h}", [P, WC], F16) for h in range(2)] for i in range(2)]
    part = (slice(0, KD * F), slice(KD * F, WC))
    assert KD * F == KF * D
    w1 = [[w[:, part[0]].rearrange("p (k n) -> p k n", k=KD) for w in pair] for pair in w_half]
    w2 = [[w[:, part[1]].rearrange("p (k n) -> p k n", k=KF) for w in pair] for pair in w_half]
    b1_all = sb("e_b1_all", [P, E, KF], F32)
    b1 = [sb(f"e_b1_{i}", [P, KF], F32) for i in range(2)]
    b2 = sb("e_b2", [P, E, D], F32)
    xT = [sb(f"e_xT{h}", [P, KD, N_TOK], F16) for h in range(2)]
    h32 = sb("e_h32", [P, 2, GT], F32)
    hT = [[sb(f"e_hT{i}_{h}", [P, KF, GT], F16) for h in range(2)] for i in range(2)]
    z = sb("e_z", [P, TT, D], F32)
    norm_buf = NormBuffers(sb, "e_norm", shared["dve_gate"])

    def sig(name, per, unit=1):
        return Signal(sem("e_" + name), per, unit)

    s_const, s_xT_first, s_xT = sem("e_const"), sem("e_xT_first"), sem("e_xT_in")
    raw_in = [sig(f"raw_in{i}", 1, 16) for i in range(2)]
    w_hi, w_lo, b1_in = [sig(f"w_hi{i}", 1) for i in range(2)], [sig(f"w_lo{i}", 1) for i in range(2)], sig("b1_in", 1)
    H_ps, h_f, h_h, h_l = sig("H_ps", KF), sig("h_f", KF), sig("h_h", KF), sig("h_l", KF)
    Y_ps, bias_x, y_x = sig("Y_ps", TT), sig("bias_x", TT), sig("y_x", TT)
    steps, z_in, z_out = sig("steps", NORM_STEPS), sig("z_in", TT), sig("z_out", 1, 16)

    def all_rounds(eng, step):
        def expert(e, parity, last):
            with eng.Fori(0, NG // 2 - 1) as i:
                step(e, 2 * i + 1, 1, parity, False, last)
                step(e, 2 * i + 2, 0, parity, False, last)
            step(e, NG - 1, 1, parity, False, last)

        step(0, 0, 0, 0, True, False)
        with eng.Fori(0, E // 2 - 1) as i:
            e = 2 * i
            expert(e, 0, False)
            step(e + 1, 0, 0, 1, False, False)
            expert(e + 1, 1, False)
            step(e + 2, 0, 0, 0, False, False)
        expert(E - 2, 0, False)
        step(E - 1, 0, 0, 1, False, True)
        expert(E - 1, 1, True)
        step(E - 1, NG, 0, 1, False, True)

    def is_number(v, *values):
        return isinstance(v, int) and v in values

    block_ctx = ExitStack()
    block = block_ctx.enter_context(nc.Block())

    @block.sync
    def _(sp):
        for s in (*raw_in, z_out):
            sp.sem_inc(s.sem, s.credit())

        def load_expert(e):
            for i in range(2):
                sp.wait_ge(w_hi[i].sem, w_hi[i].after(e - 1))
                sp.wait_ge(w_lo[i].sem, w_lo[i].after(e - 1))
                sp.dma_start(w_raw[i][:, :], dram["expert_weights"][bass.ds(e, 1), :, part[i]]
                             .rearrange("a p n -> (a p) n")).then_inc(raw_in[i].sem, 16)

        sp.dma_start(w_raw[0][:, :], dram["expert_weights"][0, :, part[0]]).then_inc(raw_in[0].sem, 16)
        for half in range(2):
            sp.dma_start(xT[half][:, :, 0:GT], dram["xT_halves"][half, :, :, 0:GT]).then_inc(s_xT_first, 16)
        sp.dma_start(b1_all[:, :, :], dram["expert_b1"]).then_inc(s_const, 16)
        sp.dma_start(b2[:, :, :], dram["expert_b2"].partition_broadcast(P).rearrange("p (e d) -> p e d", e=E))\
          .then_inc(s_const, 16)
        sp.dma_start(w_raw[1][:, :], dram["expert_weights"][0, :, part[1]]).then_inc(raw_in[1].sem, 16)
        for half in range(2):
            sp.dma_start(xT[half][:, :, GT:], dram["xT_halves"][half, :, :, GT:]).then_inc(s_xT, 16)
        with sp.Fori(1, E) as e:
            load_expert(e)
        rows = out.rearrange("b t d -> (b t) d")
        with sp.Fori(0, NG) as g:
            sp.wait_ge(z_in.sem, z_in.after(g))
            sp.dma_start(rows[bass.ds(g * GT, GT)].rearrange("(t p) d -> p t d", p=P), z[:, :, :])\
              .then_inc(z_out.sem, 16)
        sp.wait_ge(z_out.sem, z_out.after(NG - 1))

    @block.tensor
    def _(pe):
        for s in (H_ps, Y_ps):
            pe.sem_inc(s.sem, s.credit())
        pe.wait_ge(s_xT_first, 16 * 2)

        def step(e, g, odd, parity, first, last):
            r = e * NG + g
            before = parity if not is_number(g, 0) else 1 - parity
            for m in range(KF):
                if not is_number(g, NG):
                    if is_number(g, 0) and m == 0:
                        pe.wait_ge(w_hi[0].sem, w_hi[0].after(e))
                        pe.wait_ge(w_lo[0].sem, w_lo[0].after(e))
                    pe.wait_ge(h_f.sem, h_f.after(r, m - 3) if m >= 4 else h_f.after(r - 1, KF - 3 + m))
                    split_matmuls(pe, HB[m % 4][:, :], lambda h, k: w1[parity][h][:, k, m * P:(m + 1) * P],
                                  lambda h, k: xT[h][:, k, bass.ds(g * GT, GT)], KD).then_inc(H_ps.sem, 1)
                if not first and m % 2 == 1:
                    t = m // 2
                    if t == 0:
                        if is_number(g, 1) or not isinstance(g, int):
                            pe.wait_ge(w_hi[1].sem, w_hi[1].after(e))
                            pe.wait_ge(w_lo[1].sem, w_lo[1].after(e))
                        pe.wait_ge(h_h.sem, h_h.after(r - 1))
                        pe.wait_ge(h_l.sem, h_l.after(r - 1))
                    pe.wait_ge(y_x.sem, y_x.after(r - 2, t + 1))
                    hidden = hT[1 - odd]
                    split_matmuls(pe, YB[t][:, 0:D], lambda h, k: hidden[h][:, k, t * P:(t + 1) * P],
                                  lambda h, k: w2[before][h][:, k, :], KF).then_inc(Y_ps.sem, 1)

        def step_loaded(e, g, odd, parity, first, last):
            step(e, g, odd, parity, first, last)
            if first:
                pe.wait_ge(s_xT, 16 * 2)

        all_rounds(pe, step_loaded)

    @block.scalar
    def _(act):
        for s in (*w_hi, h_f):
            act.sem_inc(s.sem, s.credit())

        def split(e, parity, i):
            act.wait_ge(raw_in[i].sem, raw_in[i].after(e))
            if not is_number(e, 0):
                ps = (H_ps, Y_ps)[i]
                act.wait_ge(ps.sem, ps.after((e - 1) * NG - 1))
            act.wait_ge(w_lo[i].sem, w_lo[i].after(e - 1))
            act.activation(w_half[parity][0][:, part[i]], w_raw[i][:, :], ACT.Copy, scale=WS).then_inc(w_hi[i].sem, 1)

        split(0, 0, 0)
        split(0, 0, 1)

        def step(e, g, odd, parity, first, last):
            if is_number(g, NG):
                return
            r = e * NG + g
            if is_number(g, 0):
                act.wait_ge(b1_in.sem, b1_in.after(e))
            for m in range(KF):
                act.wait_ge(H_ps.sem, H_ps.after(r, m + 1))
                for s in (h_h, h_l):
                    act.wait_ge(s.sem, s.after(r, m - 1) if m >= 2 else s.after(r - 1, KF - 1 + m))
                act.activation(h32[:, m % 2, :], HB[m % 4][:, :], ACT.Gelu, bias=b1[parity][:, m:m + 1],
                               scale=1.0 / WS).then_inc(h_f.sem, 1)
            if is_number(g, 0, NG - 1) and not last:
                split(e + 1, 1 - parity, 0 if is_number(g, 0) else 1)

        all_rounds(act, step)

    @block.vector
    def _(dve):
        for s in (*w_lo, b1_in, h_h, bias_x, y_x, steps, z_in):
            dve.sem_inc(s.sem, s.credit())
        dve.wait_ge(s_const, 16 * 2)

        def split(e, parity, i):
            if i == 0:
                if not is_number(e, 0):
                    dve.wait_ge(h_f.sem, h_f.after((e - 1) * NG - 1))
                dve.tensor_copy(b1[parity][:, :].unsqueeze(1), b1_all[:, bass.ds(e, 1), :]).then_inc(b1_in.sem, 1)
            dve.wait_ge(w_hi[i].sem, w_hi[i].after(e))
            dve.scalar_tensor_tensor(w_half[parity][1][:, part[i]], w_raw[i][:, :], WS,
                                     w_half[parity][0][:, part[i]], ALU.mult, ALU.subtract).then_inc(w_lo[i].sem, 1)

        split(0, 0, 0)
        split(0, 0, 1)

        def step(e, g, odd, parity, first, last):
            r = e * NG + g
            expert = e - 1 if is_number(g, 0) else e
            group = NG - 1 if is_number(g, 0) else g - 1
            if not first:
                dve.wait_ge(y_x.sem, y_x.after(r - 2))
                for t in range(TT):
                    n = group * TT + t
                    dve.scalar_tensor_tensor(x[:, bass.ds(n, 1), :], b2[:, bass.ds(expert, 1), :],
                                             weight[:, bass.ds(expert * (N_TOK // P) + n, 1)],
                                             x[:, bass.ds(n, 1), :], ALU.mult, ALU.add).then_inc(bias_x.sem, 1)
            for m in range(KF):
                if not is_number(g, NG):
                    dve.wait_ge(h_f.sem, h_f.after(r, m + 1))
                    if m == 0:
                        dve.wait_ge(Y_ps.sem, Y_ps.after(r - 2))
                    dve.tensor_copy(hT[odd][0][:, m, :], h32[:, m % 2, :]).then_inc(h_h.sem, 1)
                if not first and m % 2 == 1:
                    t = m // 2
                    n = group * TT + t
                    if t == 0:
                        dve.wait_ge(bias_x.sem, bias_x.after(r - 1))
                    dve.wait_ge(Y_ps.sem, Y_ps.after(r - 1, t + 1))
                    dve.scalar_tensor_tensor(x[:, bass.ds(n, 1), :], YB[t][:, 0:D].unsqueeze(1),
                                             weight_ws[:, bass.ds(expert * (N_TOK // P) + n, 1)],
                                             x[:, bass.ds(n, 1), :], ALU.mult, ALU.add).then_inc(y_x.sem, 1)
            if is_number(g, 0, NG - 1) and not last:
                split(e + 1, 1 - parity, 0 if is_number(g, 0) else 1)
            if last and not is_number(g, 0):
                dve.wait_ge(y_x.sem, y_x.after(r - 1))
                dve.wait_ge(z_out.sem, z_out.after(group - 1))
                layer_norm(dve, lambda t: x[:, bass.ds(group * TT + t, 1), :], lambda t: z[:, t:t + 1, :], norm_buf,
                           steps.sem, lambda k: steps.after(group, k), z_in.sem)

        all_rounds(dve, step)

    @block.gpsimd
    def _(pool):
        pool.sem_inc(h_l.sem, h_l.credit())

        def step(e, g, odd, parity, first, last):
            if is_number(g, NG):
                return
            r = e * NG + g
            for m in range(KF):
                pool.wait_ge(h_h.sem, h_h.after(r, m + 1))
                if m == 0:
                    pool.wait_ge(Y_ps.sem, Y_ps.after(r - 2))
                low = hT[odd][1][:, m, :]
                pool.tensor_tensor(low, h32[:, m % 2, :], hT[odd][0][:, m, :], ALU.subtract)\
                    .then_inc(h_l.sem, 1)

        all_rounds(pool, step)

    block_ctx.close()


def build(nc, dram, out):
    with ExitStack() as ctx:
        def sem(name):
            return ctx.enter_context(nc.semaphore(name))

        def sb(name, shape, dt):
            return ctx.enter_context(nc.sbuf_tensor(name, shape, dt))

        banks = [ctx.enter_context(nc.psum_tensor(f"bank{i}", [P, 512], F32)) for i in range(8)]
        psum = {"W": banks[0:3], "M": banks[3:5], "S": banks[5:7], "O": banks[7]}
        x = sb("x", [P, N_TOK // P, D], F32)
        ident = sb("ident", [P, P], F32)
        weight, weight_ws = (sb(name, [P, E * N_TOK // P], F32) for name in ("expert_weight", "expert_weight_ws"))
        shared = {"x": x, "ident": ident, "expert_weight": weight, "expert_weight_ws": weight_ws,
                  "dve_gate": sem("dve_gate"), "act_gate": sem("act_gate"), "sp_gate": sem("sp_gate")}
        dram = {**dram, "xT_halves": nc.dram_tensor("xT_halves", (2, P, KD, N_TOK), F16, kind="Internal").ap()}
        with ExitStack() as att:
            def sa(name, shape, dt):
                return att.enter_context(nc.sbuf_tensor(name, shape, dt))

            shared["QS"] = sa("QS", [P, H, GT], F16)
            shared["KS"] = sa("KS", [P, H, GT], F16)
            shared["VS"] = sa("VS", [P, TT, H, 2 * HD], F32)
            shared["QK"] = [sa(f"QK{h}", [P, 4, GT], F16) for h in range(2)]
            shared["qk32"] = sa("qk32", [P, 2, GT], F32)
            shared["mx"] = [sa(f"mx{i}", [P, TT, C], F32) for i in range(2)]
            shared["mrow"] = [sa(f"mrow{i}", [C, GT], F16) for i in range(2)]
            shared["PR"] = [sa(f"PR{i}", [P, 6, GT], F32) for i in range(2)]
            shared["OTs"] = sa("OTs", [P, C, GT], F32)
            shared["On"] = sa("On", [P, TT, D], F32)
            shared["oT"] = [sa(f"oT{h}", [P, KD, GT], F16) for h in range(2)]
            shared["rden"] = sa("rden", [P, TT, H], F32)
            with ExitStack() as own:
                decoder(nc, lambda *a: own.enter_context(nc.sbuf_tensor(*a)), sem, psum, shared, dram)
            with ExitStack() as own:
                cross(nc, lambda *a: own.enter_context(nc.sbuf_tensor(*a)), sem, psum, shared, dram)
        with ExitStack() as own:
            experts(nc, lambda *a: own.enter_context(nc.sbuf_tensor(*a)), sem, banks, shared, dram, out)


def constants():
    import numpy as np

    slopes = (2.0 ** (-0.5)) ** np.arange(1, H + 1)
    alibi = (slopes.astype(np.float32)[:, None] * (np.arange(GT) % T)[None]).astype(np.float32)
    high = alibi.astype(np.float16)
    low = (alibi - high.astype(np.float32)).astype(np.float16)
    after = np.triu(np.ones((P, P), np.float32), 1) * -1e38
    return {
        "ident": np.eye(P, dtype=np.float32), "masks": np.concatenate([after, after.T], 1),
        "ones2": np.ones((2, H, GT), np.float16), "alibi": np.stack([high, low]),
        "zeros2": np.zeros((2, H, GT), np.float16),
    }


def laid_out(inputs):
    import numpy as np

    f = {k.replace("L0_", ""): np.asarray(v) for k, v in inputs.items()}

    def stationary(w):
        return w.reshape(-1, P, w.shape[1]).transpose(1, 0, 2).reshape(P, -1)

    def columns(b):
        return b.reshape(-1, P).T

    order = np.concatenate([(i * H + 8 * m + np.arange(8)[None]) * HD + np.arange(HD)[:, None]
                            for m in range(2) for i in range(2)]).ravel()

    weights = np.stack([np.concatenate([
        stationary(f["attn_in_proj_w"][l][np.append(order, np.arange(2 * D, 3 * D))].T),
        stationary(f["attn_out_proj_w"][l].T),
        stationary(f["attn_ffn1_w"][l].T), stationary(f["attn_ffn2_w"][l].T)], 1) for l in range(L)])
    cols = np.stack([np.concatenate([
        columns(f["attn_in_proj_b"][l][order]), columns(f["attn_ln1_w"][l]), columns(f["attn_ln1_b"][l]),
        columns(f["attn_ln2_w"][l]), columns(f["attn_ln2_b"][l]), columns(f["attn_ffn1_b"][l])], 1) for l in range(L)])
    rows = np.stack([f["attn_in_proj_b"][:, 2 * D:], f["attn_out_proj_b"], f["attn_ffn2_b"]], 1)
    wide = [(0, D - E_CTX), (0, 0)]
    heads = order.reshape(4, P)
    cross_weights = np.concatenate([
        stationary(f["xattn_Wq"][:, heads[0::2].ravel() % D]),
        stationary(np.pad(f["xattn_Wk"], wide)[:, heads[1::2].ravel() % D]),
        stationary(np.pad(f["xattn_Wv"], wide)), stationary(f["xattn_W1"]), stationary(f["xattn_W2"]),
        stationary(f["ffn_Wr"])], 1)
    both = np.concatenate([f["xattn_bq"], f["xattn_bk"]])
    cross_cols = np.concatenate([columns(both[order]), columns(f["xattn_b1"])], 1)
    cross_rows = np.concatenate([f[k] for k in ("attn_final_w", "attn_final_b", "xattn_bv", "xattn_b2", "ffn_br")])
    ctx = np.pad(f["ctx_768"].reshape(B * S, E_CTX).T, wide).reshape(KD, P, B * S).transpose(1, 0, 2)
    expert_weights = np.stack([np.concatenate([stationary(f["ffn_W1"][e]), stationary(f["ffn_W2"][e])], 1)
                               for e in range(E)])
    expert_b1 = f["ffn_b1"].reshape(E, KF, P).transpose(2, 0, 1)
    return {"x": f["x"].reshape(N_TOK, D), "weights": weights, "cols": cols, "rows": rows,
            "cross_weights": cross_weights, "cross_cols": cross_cols, "cross_rows": cross_rows, "ctx": ctx,
            "expert_weights": expert_weights, "expert_b1": expert_b1, "expert_b2": f["ffn_b2"].ravel()}


def kernel(**inputs):
    import numpy as np
    import concourse.bacc as bacc
    from concourse.bass_utils import run_bass_kernel_spmd

    nc = bacc.Bacc("TRN2", target_bir_lowering=False, num_devices=1)
    arrays, dram = {}, {}
    for name, a in {**laid_out(inputs), **constants()}.items():
        a = np.ascontiguousarray(a)
        arrays[f"in_{name}"] = a
        dram[name] = nc.dram_tensor(f"in_{name}", a.shape, mybir.dt.from_np(a.dtype), kind="ExternalInput").ap()
    out = nc.dram_tensor("out", (B, T, D), F32, kind="ExternalOutput").ap()
    build(nc, dram, out)
    r = run_bass_kernel_spmd(nc, [arrays], core_ids=[0])
    return r.results[0]["out"]
```
